# Optimizing a Trainium2 kernel written in Bass

```python
import numpy as np
import jax
import jax.numpy as jnp

def _softmax(x, axis=-1):
    return jax.nn.softmax(x, axis=axis)

def _gelu(x):
    return jax.nn.gelu(x, approximate=True)

def _silu(x):
    return jax.nn.silu(x)

def _sigmoid(x):
    return jax.nn.sigmoid(x)

def _layernorm(x, axis=-1, eps=1e-05):
    m = jnp.mean(x, axis=axis, keepdims=True)
    v = jnp.var(x, axis=axis, keepdims=True)
    return (x - m) / jnp.sqrt(v + eps)

def _scatter_add(tgt, idx, src, axis=0):
    return tgt.at[idx].add(src)

def _segment_sum(src, seg, n):
    return jax.ops.segment_sum(src, seg, n)
kernel_name = 'mk_vit_tower_d2_tok_img256_r4_41d4fe'

def setup_inputs(seed: int=0):
    np.random.seed(seed)
    _w = jnp.asarray

    def _rec_inputs():
        import jax
        import jax.numpy as jnp
        _rk = jax.random.key(seed)
        x = -0.000125008 + 0.999885 * jax.random.normal(jax.random.fold_in(_rk, 1), (8, 64, 128, 128), jnp.float32)
        return x
    x = _rec_inputs()

    def _L0_tok_setup():
        import jax, jax.numpy as jnp
        import numpy as np
        D_MODEL = 64
        NHEAD = 8
        DS = 4
        OFFSET_SCALE = 4.0

        def bilinear_sample(fm, pts):
            B, C, H, W = fm.shape
            x = (pts[..., 0] + 1.0) * 0.5 * (W - 1)
            y = (pts[..., 1] + 1.0) * 0.5 * (H - 1)
            x0 = jnp.clip(jnp.floor(x), 0.0, W - 2)
            y0 = jnp.clip(jnp.floor(y), 0.0, H - 2)
            wx = jnp.clip(x - x0, 0.0, 1.0)
            wy = jnp.clip(y - y0, 0.0, 1.0)
            x0i = x0.astype(jnp.int32)
            y0i = y0.astype(jnp.int32)
            fm2 = fm.reshape(B, C, H * W)
            N, P = (pts.shape[1], pts.shape[2])

            def gather(yi, xi):
                idx = (yi * W + xi).reshape(B, N * P)
                g = jnp.take_along_axis(fm2, idx[:, None, :], axis=2)
                return g.reshape(B, C, N, P)
            v00 = gather(y0i, x0i)
            v01 = gather(y0i, x0i + 1)
            v10 = gather(y0i + 1, x0i)
            v11 = gather(y0i + 1, x0i + 1)
            wx_ = wx[:, None]
            wy_ = wy[:, None]
            out = v00 * (1 - wx_) * (1 - wy_) + v01 * wx_ * (1 - wy_) + v10 * (1 - wx_) * wy_ + v11 * wx_ * wy_
            return jnp.moveaxis(out, 1, -1)

        def layer_norm(x, g, b, eps=1e-05):
            mu = jnp.mean(x, axis=-1, keepdims=True)
            var = jnp.var(x, axis=-1, keepdims=True)
            return (x - mu) * jax.lax.rsqrt(var + eps) * g + b

        def reference_points(B, H, W):
            yc = jnp.linspace(-1.0, 1.0, H // DS)
            xc = jnp.linspace(-1.0, 1.0, W // DS)
            yg, xg = jnp.meshgrid(yc, xc, indexing='ij')
            ref = jnp.stack([xg.reshape(-1), yg.reshape(-1)], axis=-1)
            return jnp.broadcast_to(ref[None], (B,) + ref.shape)
        key = jax.random.key(seed)
        ks = jax.random.split(key, 6)
        B, C, H, W = (8, D_MODEL, 128, 128)
        s = 0.05
        return {'feature_map': jax.random.normal(ks[0], (B, C, H, W), jnp.float32), 'W_q': jax.random.normal(ks[1], (C, C), jnp.float32) * s, 'W_k': jax.random.normal(ks[2], (C, C), jnp.float32) * s, 'W_v': jax.random.normal(ks[3], (C, C), jnp.float32) * s, 'W_o1': jax.random.normal(ks[4], (C, C // DS), jnp.float32) * s, 'b_o1': jnp.zeros((C // DS,), jnp.float32), 'ln_g': jnp.ones((C // DS,), jnp.float32), 'ln_b': jnp.zeros((C // DS,), jnp.float32), 'W_o2': jax.random.normal(ks[5], (C // DS, NHEAD * 2), jnp.float32) * s, 'b_o2': jnp.zeros((NHEAD * 2,), jnp.float32)}
    _L0_tok_all = _L0_tok_setup()
    _L0_tok_in = {k: v for k, v in _L0_tok_all.items() if k in ('W_q', 'W_k', 'W_v', 'W_o1', 'b_o1', 'ln_g', 'ln_b', 'W_o2', 'b_o2')}
    del _L0_tok_all

    def _L0_attn_setup():
        import jax, jax.numpy as jnp
        import numpy as np
        IN_C = 64
        HID_C = 64
        HEADS = 8
        SCALE = 1.0 / np.sqrt(HID_C / HEADS).astype(np.float32)
        key = jax.random.key(seed)
        k_v, k_q, k_k, k_w, k_o, k_b = jax.random.split(key, 6)
        B, S = (4, 512)
        lim_in = 1.0 / np.sqrt(IN_C)
        lim_out = 1.0 / np.sqrt(IN_C * HEADS)
        v = jax.random.normal(k_v, (B, S, IN_C), dtype=jnp.float32)
        WQ = jax.random.uniform(k_q, (IN_C, IN_C * HEADS), jnp.float32, -lim_in, lim_in)
        WK = jax.random.uniform(k_k, (IN_C, IN_C * HEADS), jnp.float32, -lim_in, lim_in)
        WV = jax.random.uniform(k_w, (IN_C, IN_C * HEADS), jnp.float32, -lim_in, lim_in)
        Wout = jax.random.uniform(k_o, (IN_C * HEADS, HID_C), jnp.float32, -lim_out, lim_out)
        bout = jax.random.uniform(k_b, (HID_C,), jnp.float32, -lim_out, lim_out)
        return {'v': v, 'WQ': WQ, 'WK': WK, 'WV': WV, 'Wout': Wout, 'bout': bout}
    _L0_attn_all = _L0_attn_setup()
    _L0_attn_in = {k: v for k, v in _L0_attn_all.items() if k in ('WQ', 'WK', 'WV', 'Wout', 'bout')}
    del _L0_attn_all

    def _L0_ffn_setup():
        import jax, jax.numpy as jnp
        import numpy as np
        NUM_EXPERTS = 8
        TOP_K = 2
        B, S, D = (8, 2048, 64)

        def _moe(tokens, router_w, w1, b1, w2, b2):
            N = tokens.shape[0]
            E = router_w.shape[0]
            logits = tokens.astype(jnp.float32) @ router_w.astype(jnp.float32).T
            probs = jax.nn.softmax(logits, axis=-1)
            rw, re = jax.lax.top_k(probs, TOP_K)
            if TOP_K > 1:
                rw = rw / jnp.maximum(rw.sum(-1, keepdims=True), 1e-12)
            rw = rw.astype(tokens.dtype)
            combine = jnp.zeros((N, E), tokens.dtype).at[jnp.arange(N)[:, None], re].set(rw)
            out = tokens
            for e in range(E):
                h = jax.nn.gelu(tokens @ w1[e] + b1[e], approximate=False)
                y = h @ w2[e] + b2[e]
                out = out + combine[:, e:e + 1] * y
            return out
        key = jax.random.key(seed)
        ks = jax.random.split(key, 4)
        scale = 1.0 / np.sqrt(D).astype(np.float32)
        return {'input_embeddings': jax.random.normal(ks[0], (B, S, D), jnp.float32), 'router_w': jax.random.normal(ks[1], (NUM_EXPERTS, D), jnp.float32) * scale, 'w1': jax.random.normal(ks[2], (NUM_EXPERTS, D, D), jnp.float32) * scale, 'b1': jnp.zeros((NUM_EXPERTS, D), jnp.float32), 'w2': jax.random.normal(ks[3], (NUM_EXPERTS, D, D), jnp.float32) * scale, 'b2': jnp.zeros((NUM_EXPERTS, D), jnp.float32)}
    _L0_ffn_all = _L0_ffn_setup()
    _L0_ffn_in = {k: v for k, v in _L0_ffn_all.items() if k in ('router_w', 'w1', 'b1', 'w2', 'b2')}
    del _L0_ffn_all

    def _L1_attn_setup():
        import jax, jax.numpy as jnp
        import numpy as np
        EMBED_DIM = 64
        B, S = (4, 2048)
        key = jax.random.key(seed)
        ks = jax.random.split(key, 9)
        d = EMBED_DIM
        s = 1.0 / np.sqrt(d)
        return {'x': jax.random.normal(ks[0], (B, S, d), dtype=jnp.float32), 'Wq': jax.random.uniform(ks[1], (d, d), jnp.float32, -s, s), 'bq': jax.random.uniform(ks[2], (d,), jnp.float32, -s, s), 'Wk': jax.random.uniform(ks[3], (d, d), jnp.float32, -s, s), 'bk': jax.random.uniform(ks[4], (d,), jnp.float32, -s, s), 'Wv': jax.random.uniform(ks[5], (d, d), jnp.float32, -s, s), 'bv': jax.random.uniform(ks[6], (d,), jnp.float32, -s, s), 'Wo': jax.random.uniform(ks[7], (d, d), jnp.float32, -s, s), 'bo': jax.random.uniform(ks[8], (d,), jnp.float32, -s, s)}
    _L1_attn_all = _L1_attn_setup()
    _L1_attn_in = {k: v for k, v in _L1_attn_all.items() if k in ('Wq', 'bq', 'Wk', 'bk', 'Wv', 'bv', 'Wo', 'bo')}
    del _L1_attn_all

    def _L1_ffn_setup():
        import jax, jax.numpy as jnp
        import numpy as np
        B, T, C = (64, 96, 64)
        NH, NKV = (4, 2)
        HD = C // NH
        NREP = NH // NKV
        NE, TOPK = (8, 2)
        HID = int(8 / 3 * C)
        EPS_RMS = 1e-06

        def _rope_tables(t_len):
            inv_freq = 1.0 / 10000.0 ** (np.arange(0, HD, 2, dtype=np.float32) / HD)
            t = np.arange(t_len, dtype=np.float32)
            freqs = np.outer(t, inv_freq)
            emb = np.concatenate([freqs, freqs], axis=-1)
            return (jnp.asarray(np.cos(emb)), jnp.asarray(np.sin(emb)))

        def _rotate_half(x):
            h = x.shape[-1] // 2
            return jnp.concatenate([-x[..., h:], x[..., :h]], axis=-1)

        def _rmsnorm(v, w):
            return v * jax.lax.rsqrt(jnp.mean(v * v, axis=-1, keepdims=True) + EPS_RMS) * w
        key = jax.random.key(seed)
        ks = jax.random.split(key, 10)
        s = lambda k, shape: jax.random.normal(k, shape, jnp.float32) * 0.02
        return {'x': jax.random.normal(ks[0], (B, T, C), jnp.float32), 'ln1_w': jnp.ones((C,), jnp.float32), 'ln2_w': jnp.ones((C,), jnp.float32), 'wq': s(ks[1], (NH * HD, C)), 'wk': s(ks[2], (NKV * HD, C)), 'wv': s(ks[3], (NKV * HD, C)), 'wo': s(ks[4], (C, C)), 'router_w': s(ks[5], (NE, C)), 'w1': s(ks[6], (NE, HID, C)), 'w2': s(ks[7], (NE, C, HID)), 'w3': s(ks[8], (NE, HID, C))}
    _L1_ffn_all = _L1_ffn_setup()
    _L1_ffn_in = {k: v for k, v in _L1_ffn_all.items() if k in ('ln1_w', 'ln2_w', 'wq', 'wk', 'wv', 'wo', 'router_w', 'w1', 'w2', 'w3')}
    del _L1_ffn_all
    return {'x': x, 'L0_tok_W_q': _L0_tok_in['W_q'], 'L0_tok_W_k': _L0_tok_in['W_k'], 'L0_tok_W_v': _L0_tok_in['W_v'], 'L0_tok_W_o1': _L0_tok_in['W_o1'], 'L0_tok_b_o1': _L0_tok_in['b_o1'], 'L0_tok_ln_g': _L0_tok_in['ln_g'], 'L0_tok_ln_b': _L0_tok_in['ln_b'], 'L0_tok_W_o2': _L0_tok_in['W_o2'], 'L0_tok_b_o2': _L0_tok_in['b_o2'], 'L0_attn_WQ': _L0_attn_in['WQ'], 'L0_attn_WK': _L0_attn_in['WK'], 'L0_attn_WV': _L0_attn_in['WV'], 'L0_attn_Wout': _L0_attn_in['Wout'], 'L0_attn_bout': _L0_attn_in['bout'], 'L0_ffn_router_w': _L0_ffn_in['router_w'], 'L0_ffn_w1': _L0_ffn_in['w1'], 'L0_ffn_b1': _L0_ffn_in['b1'], 'L0_ffn_w2': _L0_ffn_in['w2'], 'L0_ffn_b2': _L0_ffn_in['b2'], 'L1_attn_Wq': _L1_attn_in['Wq'], 'L1_attn_bq': _L1_attn_in['bq'], 'L1_attn_Wk': _L1_attn_in['Wk'], 'L1_attn_bk': _L1_attn_in['bk'], 'L1_attn_Wv': _L1_attn_in['Wv'], 'L1_attn_bv': _L1_attn_in['bv'], 'L1_attn_Wo': _L1_attn_in['Wo'], 'L1_attn_bo': _L1_attn_in['bo'], 'L1_ffn_ln1_w': _L1_ffn_in['ln1_w'], 'L1_ffn_ln2_w': _L1_ffn_in['ln2_w'], 'L1_ffn_wq': _L1_ffn_in['wq'], 'L1_ffn_wk': _L1_ffn_in['wk'], 'L1_ffn_wv': _L1_ffn_in['wv'], 'L1_ffn_wo': _L1_ffn_in['wo'], 'L1_ffn_router_w': _L1_ffn_in['router_w'], 'L1_ffn_w1': _L1_ffn_in['w1'], 'L1_ffn_w2': _L1_ffn_in['w2'], 'L1_ffn_w3': _L1_ffn_in['w3']}

def reference(x, L0_tok_W_q, L0_tok_W_k, L0_tok_W_v, L0_tok_W_o1, L0_tok_b_o1, L0_tok_ln_g, L0_tok_ln_b, L0_tok_W_o2, L0_tok_b_o2, L0_attn_WQ, L0_attn_WK, L0_attn_WV, L0_attn_Wout, L0_attn_bout, L0_ffn_router_w, L0_ffn_w1, L0_ffn_b1, L0_ffn_w2, L0_ffn_b2, L1_attn_Wq, L1_attn_bq, L1_attn_Wk, L1_attn_bk, L1_attn_Wv, L1_attn_bv, L1_attn_Wo, L1_attn_bo, L1_ffn_ln1_w, L1_ffn_ln2_w, L1_ffn_wq, L1_ffn_wk, L1_ffn_wv, L1_ffn_wo, L1_ffn_router_w, L1_ffn_w1, L1_ffn_w2, L1_ffn_w3):
    import jax
    import jax.numpy as jnp

    def _L0_tok_ref(feature_map, W_q, W_k, W_v, W_o1, b_o1, ln_g, ln_b, W_o2, b_o2):
        import jax, jax.numpy as jnp
        import numpy as np
        D_MODEL = 64
        NHEAD = 8
        DS = 4
        OFFSET_SCALE = 4.0

        def bilinear_sample(fm, pts):
            B, C, H, W = fm.shape
            x = (pts[..., 0] + 1.0) * 0.5 * (W - 1)
            y = (pts[..., 1] + 1.0) * 0.5 * (H - 1)
            x0 = jnp.clip(jnp.floor(x), 0.0, W - 2)
            y0 = jnp.clip(jnp.floor(y), 0.0, H - 2)
            wx = jnp.clip(x - x0, 0.0, 1.0)
            wy = jnp.clip(y - y0, 0.0, 1.0)
            x0i = x0.astype(jnp.int32)
            y0i = y0.astype(jnp.int32)
            fm2 = fm.reshape(B, C, H * W)
            N, P = (pts.shape[1], pts.shape[2])

            def gather(yi, xi):
                idx = (yi * W + xi).reshape(B, N * P)
                g = jnp.take_along_axis(fm2, idx[:, None, :], axis=2)
                return g.reshape(B, C, N, P)
            v00 = gather(y0i, x0i)
            v01 = gather(y0i, x0i + 1)
            v10 = gather(y0i + 1, x0i)
            v11 = gather(y0i + 1, x0i + 1)
            wx_ = wx[:, None]
            wy_ = wy[:, None]
            out = v00 * (1 - wx_) * (1 - wy_) + v01 * wx_ * (1 - wy_) + v10 * (1 - wx_) * wy_ + v11 * wx_ * wy_
            return jnp.moveaxis(out, 1, -1)

        def layer_norm(x, g, b, eps=1e-05):
            mu = jnp.mean(x, axis=-1, keepdims=True)
            var = jnp.var(x, axis=-1, keepdims=True)
            return (x - mu) * jax.lax.rsqrt(var + eps) * g + b

        def reference_points(B, H, W):
            yc = jnp.linspace(-1.0, 1.0, H // DS)
            xc = jnp.linspace(-1.0, 1.0, W // DS)
            yg, xg = jnp.meshgrid(yc, xc, indexing='ij')
            ref = jnp.stack([xg.reshape(-1), yg.reshape(-1)], axis=-1)
            return jnp.broadcast_to(ref[None], (B,) + ref.shape)
        B, C, H, W = feature_map.shape
        dh = C // NHEAD
        ref = reference_points(B, H, W)
        Nq = ref.shape[1]
        q_feat = bilinear_sample(feature_map, ref[:, :, None, :])[:, :, 0]
        queries = q_feat @ W_q.T
        h = jax.nn.gelu(layer_norm(q_feat @ W_o1 + b_o1, ln_g, ln_b))
        off = (h @ W_o2 + b_o2).reshape(B, Nq, NHEAD, 2) * OFFSET_SCALE
        scale = jnp.array([2.0 / (W - 1), 2.0 / (H - 1)], jnp.float32)
        sampling_points = ref[:, :, None, :] + off * scale
        sampled = bilinear_sample(feature_map, sampling_points)
        keys = jnp.einsum('bnpc,dc->bnpd', sampled, W_k)
        values = jnp.einsum('bnpc,dc->bnpd', sampled, W_v)
        q = queries.reshape(B, Nq, NHEAD, dh)
        k = keys.reshape(B, Nq, NHEAD, NHEAD, dh)
        v = values.reshape(B, Nq, NHEAD, NHEAD, dh)
        scores = jnp.einsum('bnhd,bnphd->bnhp', q, k) / jnp.sqrt(jnp.float32(dh))
        attn = jax.nn.softmax(scores, axis=-1)
        out = jnp.einsum('bnhp,bnphd->bnhd', attn, v).reshape(B, Nq, C)
        return out

    def _L0_attn_ref(v, WQ, WK, WV, Wout, bout):
        import jax, jax.numpy as jnp
        import numpy as np
        IN_C = 64
        HID_C = 64
        HEADS = 8
        SCALE = 1.0 / np.sqrt(HID_C / HEADS).astype(np.float32)
        B, S, C = v.shape
        H = HEADS
        q = (v @ WQ).reshape(B, S, H, C)
        k = (v @ WK).reshape(B, S, H, C)
        val = (v @ WV).reshape(B, S, H, C)
        scores = jnp.einsum('bshc,bthc->bsth', q, k) * SCALE
        A = jax.nn.softmax(scores, axis=2)
        u = jnp.einsum('bsth,bthc->bshc', A, val).reshape(B, S, H * C)
        return u @ Wout + bout

    def _L0_ffn_ref(input_embeddings, router_w, w1, b1, w2, b2):
        import jax, jax.numpy as jnp
        import numpy as np
        NUM_EXPERTS = 8
        TOP_K = 2
        B, S, D = (8, 2048, 64)

        def _moe(tokens, router_w, w1, b1, w2, b2):
            N = tokens.shape[0]
            E = router_w.shape[0]
            logits = tokens.astype(jnp.float32) @ router_w.astype(jnp.float32).T
            probs = jax.nn.softmax(logits, axis=-1)
            rw, re = jax.lax.top_k(probs, TOP_K)
            if TOP_K > 1:
                rw = rw / jnp.maximum(rw.sum(-1, keepdims=True), 1e-12)
            rw = rw.astype(tokens.dtype)
            combine = jnp.zeros((N, E), tokens.dtype).at[jnp.arange(N)[:, None], re].set(rw)
            out = tokens
            for e in range(E):
                h = jax.nn.gelu(tokens @ w1[e] + b1[e], approximate=False)
                y = h @ w2[e] + b2[e]
                out = out + combine[:, e:e + 1] * y
            return out
        b, s, d = input_embeddings.shape
        tokens = input_embeddings.reshape(b * s, d)
        return _moe(tokens, router_w, w1, b1, w2, b2).reshape(b, s, d)

    def _L1_attn_ref(x, Wq, bq, Wk, bk, Wv, bv, Wo, bo):
        import jax, jax.numpy as jnp
        import numpy as np
        EMBED_DIM = 64
        B, S = (4, 2048)
        d = x.shape[-1]
        scaling = d ** (-0.5)
        q = x @ Wq.T + bq
        k = x @ Wk.T + bk
        v = x @ Wv.T + bv
        scores = jnp.einsum('bsd,btd->bst', q, k) * scaling
        weights = jax.nn.softmax(scores, axis=-1)
        attn = jnp.einsum('bst,btd->bsd', weights, v)
        return attn @ Wo.T + bo

    def _L1_ffn_ref(x, ln1_w, ln2_w, wq, wk, wv, wo, router_w, w1, w2, w3):
        import jax, jax.numpy as jnp
        import numpy as np
        B, T, C = (64, 96, 64)
        NH, NKV = (4, 2)
        HD = C // NH
        NREP = NH // NKV
        NE, TOPK = (8, 2)
        HID = int(8 / 3 * C)
        EPS_RMS = 1e-06

        def _rope_tables(t_len):
            inv_freq = 1.0 / 10000.0 ** (np.arange(0, HD, 2, dtype=np.float32) / HD)
            t = np.arange(t_len, dtype=np.float32)
            freqs = np.outer(t, inv_freq)
            emb = np.concatenate([freqs, freqs], axis=-1)
            return (jnp.asarray(np.cos(emb)), jnp.asarray(np.sin(emb)))

        def _rotate_half(x):
            h = x.shape[-1] // 2
            return jnp.concatenate([-x[..., h:], x[..., :h]], axis=-1)

        def _rmsnorm(v, w):
            return v * jax.lax.rsqrt(jnp.mean(v * v, axis=-1, keepdims=True) + EPS_RMS) * w
        Bx, Tx, Cx = x.shape
        h = _rmsnorm(x, ln1_w)
        q = (h @ wq.T).reshape(Bx, Tx, NH, HD).transpose(0, 2, 1, 3)
        k = (h @ wk.T).reshape(Bx, Tx, NKV, HD).transpose(0, 2, 1, 3)
        v = (h @ wv.T).reshape(Bx, Tx, NKV, HD).transpose(0, 2, 1, 3)
        cos, sin = _rope_tables(Tx)
        cos, sin = (cos[None, None], sin[None, None])
        q = q * cos + _rotate_half(q) * sin
        k = k * cos + _rotate_half(k) * sin
        k = jnp.repeat(k, NREP, axis=1)
        v = jnp.repeat(v, NREP, axis=1)
        scores = jnp.einsum('bhtd,bhsd->bhts', q, k) / jnp.sqrt(jnp.float32(HD))
        causal = jnp.tril(jnp.ones((Tx, Tx), dtype=bool))
        scores = jnp.where(causal[None, None], scores, jnp.float32(-1e+30))
        att = jax.nn.softmax(scores, axis=-1)
        y = jnp.einsum('bhts,bhsd->bhtd', att, v).transpose(0, 2, 1, 3).reshape(Bx, Tx, Cx)
        x = x + y @ wo.T
        flat = _rmsnorm(x, ln2_w).reshape(-1, Cx)
        probs = jax.nn.softmax(flat @ router_w.T, axis=-1)
        tp, ti = jax.lax.top_k(probs, TOPK)
        tp = tp / (jnp.sum(tp, axis=-1, keepdims=True) + 1e-09)
        weights = jnp.sum(tp[..., None] * jax.nn.one_hot(ti, NE, dtype=flat.dtype), axis=1)
        out = jnp.zeros_like(flat)
        for e in range(NE):
            hh = jax.nn.silu(flat @ w1[e].T) * (flat @ w3[e].T)
            out = out + weights[:, e:e + 1] * (hh @ w2[e].T)
        return x + out.reshape(Bx, Tx, Cx)
    h = _L0_tok_ref(x, L0_tok_W_q, L0_tok_W_k, L0_tok_W_v, L0_tok_W_o1, L0_tok_b_o1, L0_tok_ln_g, L0_tok_ln_b, L0_tok_W_o2, L0_tok_b_o2)
    h = h + _L0_attn_ref(_layernorm(h, axis=-1), L0_attn_WQ, L0_attn_WK, L0_attn_WV, L0_attn_Wout, L0_attn_bout)
    h = h + _L0_ffn_ref(_layernorm(h, axis=-1), L0_ffn_router_w, L0_ffn_w1, L0_ffn_b1, L0_ffn_w2, L0_ffn_b2)
    h = h + _L1_attn_ref(_layernorm(h, axis=-1), L1_attn_Wq, L1_attn_bq, L1_attn_Wk, L1_attn_bk, L1_attn_Wv, L1_attn_bv, L1_attn_Wo, L1_attn_bo)
    h = h + _L1_ffn_ref(_layernorm(h, axis=-1), L1_ffn_ln1_w, L1_ffn_ln2_w, L1_ffn_wq, L1_ffn_wk, L1_ffn_wv, L1_ffn_wo, L1_ffn_router_w, L1_ffn_w1, L1_ffn_w2, L1_ffn_w3)
    return h

_drawn_inputs = setup_inputs


def setup_inputs(seed=0):
    import zlib

    import numpy as np

    out = dict(_drawn_inputs(seed))
    spreads = {'L0_tok_b_o1': (0.0, 0.1),
     'L0_tok_ln_g': (1.0, 0.2),
     'L0_tok_ln_b': (0.0, 0.1),
     'L0_tok_b_o2': (0.0, 0.1),
     'L0_ffn_b1': (0.0, 0.1),
     'L0_ffn_b2': (0.0, 0.1),
     'L1_ffn_ln1_w': (1.0, 0.6),
     'L1_ffn_ln2_w': (1.0, 0.6)}
    factors = {'L1_attn_Wq': 3.989,
     'L1_attn_bq': 8.0,
     'L1_attn_Wk': 3.835,
     'L1_attn_bk': 8.0,
     'L1_ffn_wq': 8.0,
     'L1_ffn_wk': 8.0,
     'L1_ffn_wv': 8.0,
     'L1_ffn_wo': 8.0,
     'L1_ffn_router_w': 8.0,
     'L1_ffn_w1': 8.0,
     'L1_ffn_w2': 8.0,
     'L1_ffn_w3': 8.0}
    for name, (base, spread) in spreads.items():
        noise = np.random.default_rng([zlib.crc32(name.encode()), seed]).standard_normal(out[name].shape)
        drawn = base * np.exp(spread * noise) if base else spread * noise
        out[name] = jnp.asarray(drawn.astype(out[name].dtype))
    for name, factor in factors.items():
        out[name] = (out[name] * factor).astype(out[name].dtype)
    return out
```

```python
from contextlib import ExitStack

import concourse.bass as bass
from concourse import mybir

F32 = mybir.dt.float32
BF16 = mybir.dt.bfloat16
I32 = mybir.dt.int32
U32 = mybir.dt.uint32
ACT = mybir.ActivationFunctionType
ALU = mybir.AluOpType
AX = mybir.AxisListType

P = 128
B = 8
S = 1024
C = 64
T = S // P
NT = B * T
EPS = 1e-5
EPS_RMS = 1e-6
E = 8
HID1 = int(8 / 3 * C)
WD = 128
GRID = 32
OFFSET_SCALE = 4.0


class Scope:

    def __init__(self, nc, ctx, tag):
        self.nc, self.ctx, self.tag = nc, ctx, tag
        self.sems, self.held = [], ExitStack()
        ctx.callback(self.clear)

    def sb(self, name, shape, dt=F32):
        return self.ctx.enter_context(self.nc.sbuf_tensor(f"{self.tag}_{name}", shape, dt))

    def ps(self, name, shape, dt=F32):
        return self.ctx.enter_context(self.nc.psum_tensor(f"{self.tag}_{name}", shape, dt))

    def sem(self, name):
        self.sems.append(self.held.enter_context(self.nc.semaphore(f"{self.tag}_{name}")))
        return self.sems[-1]

    def clear(self):
        if self.sems:
            with self.nc.Block() as block:
                @block.sync
                def _(sp):
                    for s in self.sems:
                        sp.sem_clear(s)
        self.held.close()

    def counts(self, names):
        counting = [self.sem(n) for n in names.split()]
        with self.nc.Block() as block:
            @block.sync
            def _(sp):
                for s in counting:
                    sp.sem_inc(s, 1)
        return counting


def wait(eng, sem, n):
    eng.wait_ge(sem, n + 1)


def split(eng, sem, count, hi, mid, lo, x, rest):
    eng.tensor_copy(hi, x).then_inc(sem, 1)
    eng.wait_ge(sem, count + 1)
    eng.tensor_tensor(rest, x, hi, ALU.subtract).then_inc(sem, 1)
    eng.wait_ge(sem, count + 2)
    eng.tensor_copy(mid, rest).then_inc(sem, 1)
    eng.wait_ge(sem, count + 3)
    eng.tensor_tensor(lo, rest, mid, ALU.subtract).then_inc(sem, 1)


def attention_weights(nc, tag, H, scale, w, ident, A_all, W_aug):
    with ExitStack() as ctx:
        m = Scope(nc, ctx, tag + "w")
        raw = m.sb("raw", [C, 4, H, C])
        fold = m.sb("fold", [C, 3, H, C])
        v_two = m.sb("v_two", [C, H, 2, C])
        p_a = m.ps("p_a", [C, H, C])
        p_w = m.ps("p_w", [P, H, C])
        loaded, folded, zeroed, made_a, made_w, kept = (m.sem(n) for n in
                                                ("loaded", "folded", "zeroed", "made_a", "made_w", "kept"))
        bias = m.sb("bias", [C, 3]) if w["bq"] is not None else None
        block = ctx.enter_context(nc.Block())
        n_loads = 4 + (3 if bias is not None else 0)

        @block.sync
        def _(sp):
            for n, key in enumerate(("q", "k", "v", "o")):
                sp.dma_start(raw[:, n], w[key]).then_inc(loaded, 16)
            if bias is not None:
                for n, key in enumerate(("bq", "bk", "bv")):
                    sp.dma_start(bias[:, n:n + 1], w[key]).then_inc(loaded, 16)

        @block.gpsimd
        def _(pool):
            nc.gpsimd.memset(W_aug[:], 0.0).then_inc(zeroed, 1)
            pool.wait_ge(zeroed, 1)
            nc.gpsimd.memset(W_aug[0:1, :, 0, C:C + 1], 1.0).then_inc(zeroed, 1)
            nc.gpsimd.memset(W_aug[C:C + 1, :, 1, C:C + 1], 1.0).then_inc(zeroed, 1)

        @block.vector
        def _(dve):
            dve.wait_ge(loaded, 16 * n_loads)
            nc.vector.tensor_tensor(fold[:, 0:3], raw[:, 0:3], raw[:, 0:3, :, 0:1].broadcast_to([C, 3, H, C]),
                                    ALU.subtract).then_inc(folded, 1)
            dve.wait_ge(folded, 1)
            n = 1
            if bias is not None:
                nc.vector.tensor_copy(fold[:, 0:3, 0, 0], bias[:, :]).then_inc(folded, 1)
                n = 2
                dve.wait_ge(folded, 2)
            nc.vector.tensor_copy(v_two[:], fold[:, 2].unsqueeze(2).broadcast_to([C, H, 2, C])).then_inc(folded, 3 - n)
            dve.wait_ge(made_a, 1)
            nc.vector.tensor_scalar(A_all[:], p_a[:], scale, None, ALU.mult).then_inc(kept, 1)
            dve.wait_ge(made_w, 1)
            dve.wait_ge(zeroed, 3)
            nc.vector.tensor_copy(W_aug[0:C, :, 0, 0:C], p_w[0:C]).then_inc(kept, 1)
            nc.vector.tensor_copy(W_aug[C:P, :, 1, 0:C], p_w[C:P]).then_inc(kept, 1)
            dve.wait_ge(kept, 3)

        @block.tensor
        def _(pe):
            pe.wait_ge(folded, 3)
            for h in range(H):
                mm = nc.tensor.matmul(p_a[:, h, :], fold[:, 0, h, :], fold[:, 1, h, :], start=True, stop=True)
            mm.then_inc(made_a, 1)
            for h in range(H):
                mm = nc.tensor.matmul(p_w[:, h, :], v_two[:, h].rearrange("p e c -> p (e c)"), raw[:, 3, h, :], start=True, stop=True)
            mm.then_inc(made_w, 1)


def normed_tokens(nc, tag, hid, ident, V_all, K_all, KB_all, bias_row=None):
    with ExitStack() as ctx:
        m = Scope(nc, ctx, tag + "n")
        mean = m.sb("mean", [P, T])
        cen = m.sb("cen", [P, T, C])
        sq = m.sb("sq", [P, T, C])
        ssq = m.sb("ssq", [P, T])
        std = m.sb("std", [P, T])
        rstd = m.sb("rstd", [P, T])
        eps = m.sb("eps", [P, 1])
        xt = m.sb("xt", [P, T, P])
        brow = m.sb("brow", [P, C]) if bias_row is not None else None
        p_t = m.ps("p_t", [P, S])
        (step,
         stepped,
         turned,
         kept_k,
         kept_v,
         kept_b,
         ) = m.counts("step stepped turned kept_k kept_v kept_b")
        ones = m.sem("ones")
        loaded = m.sem("loaded")
        block = ctx.enter_context(nc.Block())
        NV = 7

        @block.sync
        def _(sp):
            if brow is not None:
                sp.dma_start(brow[:], bias_row.broadcast_to([P, C])).then_inc(loaded, 16)

        @block.gpsimd
        def _(pool):
            nc.gpsimd.memset(xt[:, :, C:P], 0.0).then_inc(ones, 1)
            nc.gpsimd.memset(xt[:, :, 0:1], 1.0).then_inc(ones, 1)
            nc.gpsimd.memset(eps[:], EPS).then_inc(ones, 1)
            pool.wait_ge(ones, 3)

        @block.vector
        def _(dve):
            dve.wait_ge(ones, 3)
            if brow is not None:
                dve.wait_ge(loaded, 16)
            with dve.Fori(0, B) as b:
                x = hid[:, bass.ds(b * T, T), :]
                nc.vector.tensor_reduce(mean[:], x, AX.X, ALU.add).then_inc(step, 1)
                wait(dve, step, b * NV + 1)
                nc.vector.tensor_scalar(mean[:], mean[:], 1.0 / C, None, ALU.mult).then_inc(step, 1)
                wait(dve, step, b * NV + 2)
                nc.vector.tensor_tensor(cen[:], x, mean[:].unsqueeze(2).broadcast_to([P, T, C]),
                                        ALU.subtract).then_inc(step, 1)
                wait(dve, step, b * NV + 3)
                nc.vector.tensor_tensor(sq[:], cen[:], cen[:], ALU.mult).then_inc(step, 1)
                wait(dve, step, b * NV + 4)
                nc.vector.tensor_reduce(ssq[:], sq[:], AX.X, ALU.add).then_inc(step, 1)
                if brow is not None:
                    nc.vector.tensor_tensor(x, x, brow[:].unsqueeze(1).broadcast_to([P, T, C]), ALU.add)
                wait(dve, stepped, b + 1)
                nc.vector.reciprocal(rstd[:], std[:]).then_inc(step, 1)
                wait(dve, step, b * NV + 6)
                wait(dve, turned, b)
                wait(dve, kept_v, b)
                nc.vector.tensor_tensor(xt[:, :, 1:C], cen[:, :, 1:C],
                                        rstd[:].unsqueeze(2).broadcast_to([P, T, C - 1]),
                                        ALU.mult).then_inc(step, 1)
                wait(dve, kept_k, b + 1)
                nc.vector.tensor_copy(KB_all[:, bass.ds(b * S, S)], p_t[:]).then_inc(kept_b, 1)
            wait(dve, kept_b, B)
            wait(dve, step, B * NV)

        @block.scalar
        def _(act):
            act.wait_ge(ones, 3)
            with act.Fori(0, B) as b:
                wait(act, step, b * NV + 5)
                nc.scalar.activation(std[:], ssq[:], ACT.Sqrt, bias=eps[:], scale=1.0 / C).then_inc(stepped, 1)
                wait(act, step, b * NV + 7)
                nc.scalar.copy(V_all[:, bass.ds(b * T, T), :], xt[:, :, 0:C]).then_inc(kept_v, 1)
                wait(act, turned, b + 1)
                nc.scalar.copy(K_all[:, bass.ds(b * S, S)], p_t[0:C]).then_inc(kept_k, 1)
            wait(act, kept_k, B)
            wait(act, kept_v, B)

        @block.tensor
        def _(pe):
            with pe.Fori(0, B) as b:
                wait(pe, step, b * NV + 7)
                wait(pe, kept_k, b)
                wait(pe, kept_b, b)
                for t in range(T):
                    mm = nc.tensor.transpose(p_t[:, t * P:(t + 1) * P], xt[:, t, :], ident[:])
                mm.then_inc(turned, 1)


def attention(nc, tag, H, hid, ident, A_all, W_aug, V_all, Q_all, K_all, KB_all, causal=None):
    N = B * H
    HS = S // 2
    chunks = [(t, e) for t in range(T) for e in range(2) if not causal or e >= t // (T // 2)]
    NC = len(chunks)
    of_tile = [[c for c, (t, e) in enumerate(chunks) if t == k] for k in range(T)]
    PR = (NC + 2 + 2) // 3 * 3
    RE = 4
    with ExitStack() as ctx:
        m = Scope(nc, ctx, tag + "a")
        A_st = [m.sb(f"A_st{u}", [C, P]) for u in range(2)]
        K_st = [m.sb(f"K_st{u}", [P, S]) for u in range(2)]
        V_st = [m.sb(f"V_st{u}", [P, T, C]) for u in range(2)]
        q_bf = [m.sb(f"q_bf{u}", [P, S], BF16) for u in range(2)]
        q_T = [m.sb(f"q_T{u}", [P, S]) for u in range(2)]
        neg = [m.sb(f"neg{u}", [P, T, P]) for u in range(2)]
        ex = m.sb("ex", [P, RE, HS])
        z = m.sb("z", [P, HS])
        rden = m.sb("rden", [P, 2, 2, 2])
        y = m.sb("y", [P, 2, 2, 2, C])
        p_q = m.ps("p_q", [P, S])
        p_m = m.ps("p_m", [P, S])
        p_s = [m.ps(f"p_s{r}", [P, HS]) for r in range(3)]
        p_z = m.ps("p_z", [P, HS])

        zeroed = m.sem("zeroed")
        (placed,
         q_made,
         q_cast,
         m_made,
         m_taken,
         q_less,
         q_kept,
         s_made,
         exp_done,
         pv_done,
         z_kept,
         y_made,
         y_read,
         r_done,
         h_done,
         ) = m.counts("placed q_made q_cast m_made m_taken q_less q_kept s_made "
                      "exp_done pv_done z_kept y_made y_read r_done h_done")
        block = ctx.enter_context(nc.Block())

        def slot(c):
            return c + 1 if c < 2 else c % 3

        def first_query(c):
            t, e = chunks[c]
            return (t % (T // 2)) * P if causal and e == t // (T // 2) else 0

        def keys_seen(t, e):
            return min(max((t + 1) * P - e * HS, 0), HS) if causal else HS

        @block.gpsimd
        def _(pool):
            for u in range(2):
                nc.gpsimd.memset(A_st[u][:, C:P], 0.0).then_inc(zeroed, 1)
                nc.gpsimd.memset(K_st[u][:], 0.0).then_inc(zeroed, 1)
                nc.gpsimd.memset(neg[u][:], 0.0).then_inc(zeroed, 1)
            pool.wait_ge(zeroed, 6)

            def place(i, u):
                b, h = i // H, i % H
                nc.gpsimd.tensor_copy(K_st[u][0:C, :], K_all[:, bass.ds(b * S, S)]).then_inc(placed, 1)
                nc.gpsimd.tensor_copy(V_st[u][:], V_all[:, bass.ds(b * T, T), :]).then_inc(placed, 1)
                nc.gpsimd.tensor_copy(A_st[u][:, 0:C],
                                      A_all[:, bass.ds(h, 1), :].rearrange("p a c -> p (a c)")).then_inc(placed, 1)

            def first():
                place(0, 0)
                place(1, 1)

            def body(i, u, more):
                wait(pool, pv_done, NC * (i + 1))
                place(i + 2, u)

            first()
            with pool.Fori(0, N // 2 - 1) as g:
                body(g * 2, 0, True)
                body(g * 2 + 1, 1, True)
            wait(pool, placed, 3 * N)

        @block.tensor
        def _(pe):
            pe.wait_ge(zeroed, 6)

            def project(i, u):
                wait(pe, placed, 3 * i + 3)
                wait(pe, q_kept, 2 * i)
                for e in range(2):
                    mm = nc.tensor.matmul(p_q[:, e * HS:(e + 1) * HS], A_st[u][:],
                                          Q_all[:, bass.ds((i // H) * S + e * HS, HS)], start=True, stop=True)
                mm.then_inc(q_made, 1)

            def rows(i, u, t):
                if t == 0:
                    wait(pe, q_cast, i + 1)
                wait(pe, m_taken, T * i + t)
                for e in range(2):
                    n = keys_seen(t, e)
                    diagonal = causal and e == t // (T // 2)
                    if n:
                        mm = nc.tensor.matmul(p_m[:, e * HS:e * HS + n], q_bf[u][:, t * P:(t + 1) * P],
                                              KB_all[:, bass.ds((i // H) * S + e * HS, n)],
                                              start=True, stop=not diagonal)
                    if diagonal:
                        mm = nc.tensor.matmul(p_m[:, t * P:(t + 1) * P], causal[0][:], causal[1][:],
                                              start=False, stop=True)
                mm.then_inc(m_made, 1)

            def subtract(i, u, e):
                wait(pe, m_taken, T * i + T // 2 * (e + 1))
                for t in range(T // 2 * e, T // 2 * (e + 1)):
                    mm = nc.tensor.matmul(p_q[:, t * P:(t + 1) * P], neg[u][:, t, :], ident[:],
                                          start=False, stop=True, skip_group_check=True)
                mm.then_inc(q_less, 1)

            def score(i, u, c, fresh=False):
                t, e = chunks[c]
                s0 = first_query(c)
                diagonal = causal and e == t // (T // 2)
                if c < 2:
                    if not fresh:
                        wait(pe, exp_done, NC * i + (PR - 4 + c - NC))
                elif c == 2:
                    wait(pe, exp_done, NC * i + 2)
                elif c in (3, 4):
                    wait(pe, y_read, 2 * i)
                else:
                    wait(pe, exp_done, NC * i + c - 2)
                if c < 2:
                    wait(pe, q_kept, 2 * i + c + 1)
                mm = nc.tensor.matmul(p_s[slot(c)][:, s0:HS], K_st[u][:, t * P:(t + 1) * P],
                                      q_T[u][:, e * HS + s0:(e + 1) * HS], start=True, stop=not diagonal)
                if diagonal:
                    mm = nc.tensor.matmul(p_s[slot(c)][:, s0:s0 + P], causal[0][:], causal[2][:],
                                          start=False, stop=True)
                mm.then_inc(s_made, 1)

            def total(i, u, t):
                wait(pe, exp_done, NC * i + of_tile[t][-1] + 1)
                if t == 0:
                    wait(pe, z_kept, i)
                for c in of_tile[t]:
                    e, s0 = chunks[c][1], first_query(c)
                    last = chunks[c] == (T - 1, 1) or (e == 0 and c == max(k for k in range(NC) if chunks[k][1] == 0))
                    nc.tensor.matmul(p_z[e * C:(e + 1) * C, s0:HS], V_st[u][:, t, :], ex[:, c % RE, s0:HS],
                                     start=(t == 0), stop=last).then_inc(pv_done, 1)

            def output(i):
                wait(pe, z_kept, i + 1)
                for k in range(2):
                    if k == 0:
                        wait(pe, exp_done, NC * i + NC)
                    for j in range(2):
                        mm = nc.tensor.matmul(p_s[k][:, j * 2 * (C + 1):(j + 1) * 2 * (C + 1)],
                                              z[:, (2 * k + j) * P:(2 * k + j + 1) * P],
                                              W_aug[:, bass.ds(i % H, 1), :, :].rearrange("p a e c -> p (a e c)"),
                                              start=True, stop=True)
                    mm.then_inc(y_made, 1)

            def body(i, u, more):
                n = 1 - u
                for t in range(T):
                    if t < T - 1:
                        for c in of_tile[t + 1]:
                            score(i, u, c)
                    elif more:
                        score(i + 1, n, 0)
                        score(i + 1, n, 1)
                    if more and t == 0:
                        project(i + 1, n)
                    before = {1: 0, 2: 2, 3: 3, 4: 5, 5: 6}
                    after = {1: 1, 3: 4, 5: 7}
                    if more and t in before:
                        rows(i + 1, n, before[t])
                    total(i, u, t)
                    if more and t == 3:
                        subtract(i + 1, n, 0)
                    if more and t in after:
                        rows(i + 1, n, after[t])
                    if more and t == 6:
                        subtract(i + 1, n, 1)
                if more:
                    wait(pe, exp_done, NC * i + NC + 1)
                output(i)

            project(0, 0)
            for t in range(T):
                rows(0, 0, t)
            subtract(0, 0, 0)
            subtract(0, 0, 1)
            score(0, 0, 0, fresh=True)
            score(0, 0, 1, fresh=True)
            with pe.Fori(0, N // 2 - 1) as g:
                body(g * 2, 0, True)
                body(g * 2 + 1, 1, True)
            body(N - 2, 0, True)
            body(N - 1, 1, False)

        @block.scalar
        def _(act):
            def cast(i, u):
                wait(act, q_made, i + 1)
                nc.scalar.copy(q_bf[u][:], p_q[:]).then_inc(q_cast, 1)

            def body(i, u, more):
                for c in range(NC):
                    wait(act, s_made, NC * i + c + 1)
                    wait(act, pv_done, NC * i + max(c - RE + 1, 0))
                    s0 = first_query(c)
                    nc.scalar.activation(ex[:, c % RE, s0:HS], p_s[slot(c)][:, s0:HS], ACT.Exp).then_inc(exp_done, 1)
                    if c == 1 and more:
                        cast(i + 1, 1 - u)

            cast(0, 0)
            with act.Fori(0, N // 2 - 1) as g:
                body(g * 2, 0, True)
                body(g * 2 + 1, 1, True)
            body(N - 2, 0, True)
            body(N - 1, 1, False)

        @block.vector
        def _(dve):
            dve.wait_ge(zeroed, 6)

            def maxima(i, u, t):
                wait(dve, m_made, T * i + t + 1)
                nc.vector.tensor_reduce(neg[u][:, t, 0:1], p_m[:, 0:sum(keys_seen(t, e) for e in range(2))], AX.X,
                                        ALU.max, negate=True).then_inc(m_taken, 1)

            def keep(i, u, e):
                wait(dve, q_less, 2 * i + e + 1)
                nc.vector.tensor_copy(q_T[u][:, e * HS:(e + 1) * HS], p_q[:, e * HS:(e + 1) * HS]).then_inc(q_kept, 1)

            def finish(i):
                wait(dve, pv_done, NC * (i + 1))
                wait(dve, y_made, 2 * i)
                nc.vector.tensor_copy(z[:], p_z[:]).then_inc(z_kept, 1)
                x = hid[:, bass.ds((i // H) * T, T), :].rearrange("p (e t) c -> p e t c", e=2)
                for k in range(2):
                    wait(dve, y_made, 2 * i + k + 1)
                    p = p_s[k][:, 0:4 * (C + 1)].rearrange("p (j e c) -> p e j c", j=2, e=2)
                    nc.vector.reciprocal(rden[:, k], p[:, :, :, C]).then_inc(r_done, 1)
                    wait(dve, r_done, 2 * i + k + 1)
                    nc.vector.tensor_tensor(y[:, k], p[:, :, :, 0:C],
                                            rden[:, k].unsqueeze(3).broadcast_to([P, 2, 2, C]),
                                            ALU.mult).then_inc(y_read, 1)
                    wait(dve, y_read, 2 * i + k + 1)
                    wait(dve, h_done, 2 * i)
                    out = x[:, :, 2 * k:2 * k + 2, :]
                    nc.vector.tensor_tensor(out, out, y[:, k], ALU.add).then_inc(h_done, 1)

            def body(i, u, more):
                if more:
                    for e in range(2):
                        for t in range(T // 2 * e, T // 2 * (e + 1)):
                            maxima(i + 1, 1 - u, t)
                        keep(i + 1, 1 - u, e)
                finish(i)

            for t in range(T):
                maxima(0, 0, t)
            keep(0, 0, 0)
            keep(0, 0, 1)
            with dve.Fori(0, N // 2 - 1) as g:
                body(g * 2, 0, True)
                body(g * 2 + 1, 1, True)
            body(N - 2, 0, True)
            body(N - 1, 1, False)
            wait(dve, h_done, 2 * N)


def layer_norm(nc, tag, hid, out):
    with ExitStack() as ctx:
        m = Scope(nc, ctx, tag)
        mean, ssq, std = (m.sb(n, [P, 2, T]) for n in ("mean", "ssq", "std"))
        sq = m.sb("sq", [P, T, C])
        eps = m.sb("eps", [P, 1])
        ready = m.sem("ready")
        (step,
         rooted,
         ) = m.counts("step rooted")
        block = ctx.enter_context(nc.Block())

        @block.gpsimd
        def _(pool):
            nc.gpsimd.memset(eps[:], EPS).then_inc(ready, 1)

        @block.vector
        def _(dve):
            with dve.Fori(0, B) as b:
                x = hid[:, bass.ds(b * T, T), :]
                y = out[:, bass.ds(b * T, T), :]
                nc.vector.tensor_reduce(mean[:, 0], x, AX.X, ALU.add).then_inc(step, 1)
                wait(dve, step, 7 * b + 1)
                nc.vector.tensor_scalar(mean[:, 1], mean[:, 0], 1.0 / C, None, ALU.mult).then_inc(step, 1)
                wait(dve, step, 7 * b + 2)
                nc.vector.tensor_tensor(y, x, mean[:, 1].unsqueeze(2).broadcast_to([P, T, C]),
                                        ALU.subtract).then_inc(step, 1)
                wait(dve, step, 7 * b + 3)
                nc.vector.tensor_tensor(sq[:], y, y, ALU.mult).then_inc(step, 1)
                wait(dve, step, 7 * b + 4)
                nc.vector.tensor_reduce(ssq[:, 0], sq[:], AX.X, ALU.add).then_inc(step, 1)
                wait(dve, rooted, b + 1)
                nc.vector.reciprocal(std[:, 1], std[:, 0]).then_inc(step, 1)
                wait(dve, step, 7 * b + 6)
                nc.vector.tensor_tensor(y, y, std[:, 1].unsqueeze(2).broadcast_to([P, T, C]),
                                        ALU.mult).then_inc(step, 1)
            wait(dve, step, 7 * B)

        @block.scalar
        def _(act):
            act.wait_ge(ready, 1)
            with act.Fori(0, B) as b:
                wait(act, step, 7 * b + 5)
                nc.scalar.activation(std[:, 0], ssq[:, 0], ACT.Sqrt, bias=eps[:], scale=1.0 / C).then_inc(rooted, 1)


def rotary_heads(nc, tag, xs, ident, ident_bf, norm_row, wqkv, rope, V_all, Q_all, K_all, KB_all):
    with ExitStack() as ctx:
        m = Scope(nc, ctx, tag + "r")
        sq, xr, xn, rest = (m.sb(n, [P, T, C]) for n in ("sq", "xr", "xn", "rest"))
        ssq, std, rstd = (m.sb(n, [P, T]) for n in ("ssq", "std", "rstd"))
        eps = m.sb("eps", [P, 1])
        w_n = m.sb("w_n", [P, C])
        x_p = [m.sb(f"x_p{k}", [P, T, P], BF16) for k in range(2)]
        x_T = [m.sb(f"x_T{k}", [P, S], BF16) for k in range(2)]
        w_raw, w_rest = m.sb("w_raw", [P, P]), m.sb("w_rest", [P, P])
        w_s = m.sb("w_s", [P, 3, P], BF16)
        w_lo = m.sb("w_lo", [P, P], BF16)
        tab = m.sb("tab", [P, 2, T, 16])
        qkv = m.sb("qkv", [P, T, P])
        t_cos, t_sin = m.sb("t_cos", [P, T, 96]), m.sb("t_sin", [P, T, 96])
        q_n, k_n = m.sb("q_n", [P, T, P]), m.sb("k_n", [P, T, P])
        p_x = [m.ps(f"p_x{k}", [P, S], BF16) for k in range(2)]
        p_p = m.ps("p_p", [P, T, P])
        p_q = m.ps("p_q", [P, S])
        p_k = m.ps("p_k", [P, S])
        ready, loaded, w_split = m.sem("ready"), m.sem("loaded"), m.sem("w_split")
        (step,
         rooted,
         x_turned,
         x_kept,
         projected,
         p_kept,
         v_kept,
         qk_turned,
         q_kept, k_kept, kb_kept,
         ) = m.counts("step rooted x_turned x_kept projected p_kept v_kept qk_turned q_kept k_kept kb_kept")
        block = ctx.enter_context(nc.Block())
        names = ["sq", "ssq", "rstd", "xr", "xn", "x_hi", "x_rest", "x_mid", "x_lo", "x_hi2", "cos", "sin0", "sin1", "q", "k"]
        at = {n: k + 1 for k, n in enumerate(names)}
        NV = len(names)

        @block.sync
        def _(sp):
            for h in range(2):
                sp.dma_start(w_raw[h * C:(h + 1) * C], wqkv).then_inc(loaded, 16)
            sp.dma_start(w_n[:], norm_row.broadcast_to([P, C])).then_inc(loaded, 16)
            sp.dma_start(tab[:], rope).then_inc(loaded, 16)

        @block.gpsimd
        def _(pool):
            nc.gpsimd.memset(eps[:], EPS_RMS).then_inc(ready, 1)
            nc.gpsimd.memset(q_n[:], 0.0).then_inc(ready, 1)
            nc.gpsimd.memset(k_n[:], 0.0).then_inc(ready, 1)
            nc.gpsimd.memset(V_all[:], 0.0).then_inc(ready, 1)
            pool.wait_ge(ready, 4)
            nc.gpsimd.memset(k_n[:, :, 0:1], 1.0).then_inc(ready, 1)
            nc.gpsimd.memset(V_all[:, :, 0:1], 1.0).then_inc(ready, 1)

        @block.vector
        def _(dve):
            dve.wait_ge(ready, 6)
            dve.wait_ge(loaded, 64)
            split(nc.vector, w_split, 0, w_s[:, 0], w_s[:, 1], w_lo[:], w_raw[:], w_rest[:])
            dve.wait_ge(w_split, 4)
            nc.vector.tensor_copy(w_s[0:C, 2], w_lo[0:C]).then_inc(w_split, 1)
            nc.vector.tensor_copy(w_s[C:P, 2], w_s[C:P, 0]).then_inc(w_split, 1)
            with dve.Fori(0, B) as b:
                def after(name):
                    wait(dve, step, b * NV + at[name])

                x = xs[:, bass.ds(b * T, T), :]
                nc.vector.tensor_tensor(sq[:], x, x, ALU.mult).then_inc(step, 1)
                after("sq")
                nc.vector.tensor_reduce(ssq[:], sq[:], AX.X, ALU.add).then_inc(step, 1)
                wait(dve, rooted, b + 1)
                nc.vector.reciprocal(rstd[:], std[:]).then_inc(step, 1)
                after("rstd")
                nc.vector.tensor_tensor(xr[:], x, rstd[:].unsqueeze(2).broadcast_to([P, T, C]), ALU.mult).then_inc(step, 1)
                after("xr")
                nc.vector.tensor_tensor(xn[:], xr[:], w_n[:].unsqueeze(1).broadcast_to([P, T, C]), ALU.mult).then_inc(step, 1)
                after("xn")
                wait(dve, x_turned, b)
                split(nc.vector, step, b * NV + at["xn"] + 1, x_p[0][:, :, 0:C], x_p[0][:, :, C:P], x_p[1][:, :, C:P],
                      xn[:], rest[:])
                nc.vector.tensor_copy(x_p[1][:, :, 0:C], x_p[0][:, :, 0:C]).then_inc(step, 1)
                wait(dve, p_kept, b + 1)
                of = qkv[:, :, 0:96].rearrange("p t (h d) -> p t h d", d=16)
                cs = lambda k, lo, hi: tab[:, k, :, lo:hi].unsqueeze(2).broadcast_to([P, T, 6, hi - lo])
                tc, ts = (v[:].rearrange("p t (h d) -> p t h d", d=16) for v in (t_cos, t_sin))
                nc.vector.tensor_tensor(tc, of, cs(0, 0, 16), ALU.mult).then_inc(step, 1)
                nc.vector.tensor_tensor(ts[:, :, :, 0:8], of[:, :, :, 8:16], cs(1, 0, 8), ALU.mult).then_inc(step, 1)
                nc.vector.tensor_tensor(ts[:, :, :, 8:16], of[:, :, :, 0:8], cs(1, 8, 16), ALU.mult).then_inc(step, 1)
                after("sin1")
                wait(dve, qk_turned, b)
                nc.vector.tensor_tensor(q_n[:, :, 0:C], t_cos[:, :, 0:C], t_sin[:, :, 0:C], ALU.add).then_inc(step, 1)
                two = lambda v: v[:, :, C:96].rearrange("p t (g d) -> p t g d", g=2)
                nc.vector.tensor_tensor(k_n[:, :, 0:C].rearrange("p t (g d) -> p t g d", g=2)[:, :, :, 1:17],
                                        two(t_cos), two(t_sin), ALU.add).then_inc(step, 1)
                wait(dve, k_kept, b + 1)
                nc.vector.tensor_copy(KB_all[:, bass.ds(b * S, S)], p_k[:]).then_inc(kb_kept, 1)
            wait(dve, kb_kept, B)

        @block.scalar
        def _(act):
            act.wait_ge(ready, 6)
            with act.Fori(0, B) as b:
                wait(act, step, b * NV + at["ssq"])
                nc.scalar.activation(std[:], ssq[:], ACT.Sqrt, bias=eps[:], scale=1.0 / C).then_inc(rooted, 1)
                wait(act, x_turned, b + 1)
                wait(act, projected, b)
                for k in range(2):
                    nc.scalar.copy(x_T[k][:], p_x[k][:]).then_inc(x_kept, 1)
                wait(act, projected, b + 1)
                wait(act, step, b * NV)
                wait(act, v_kept, b)
                nc.scalar.copy(qkv[:], p_p[:]).then_inc(p_kept, 1)
                wait(act, p_kept, b + 1)
                nc.scalar.copy(V_all[:, bass.ds(b * T, T), 1:33], qkv[:, :, 96:P]).then_inc(v_kept, 1)
                wait(act, qk_turned, b + 1)
                nc.scalar.copy(K_all[:, bass.ds(b * S, S)], p_k[0:C]).then_inc(k_kept, 1)
                nc.scalar.copy(Q_all[:, bass.ds(b * S, S)], p_q[0:C]).then_inc(q_kept, 1)
            wait(act, q_kept, B)
            wait(act, k_kept, B)
            wait(act, v_kept, B)

        @block.tensor
        def _(pe):
            pe.wait_ge(w_split, 6)
            with pe.Fori(0, B) as b:
                wait(pe, step, b * NV + at["x_hi2"])
                wait(pe, x_kept, 2 * b)
                for k in range(2):
                    for t in range(T):
                        mm = nc.tensor.transpose(p_x[k][:, t * P:(t + 1) * P], x_p[k][:, t, :], ident_bf[:])
                mm.then_inc(x_turned, 1)
                wait(pe, x_kept, 2 * b + 2)
                wait(pe, p_kept, b)
                for t in range(T):
                    for q in range(3):
                        mm = nc.tensor.matmul(p_p[:, t, :], x_T[q // 2][:, t * P:(t + 1) * P], w_s[:, q],
                                              start=(q == 0), stop=(q == 2))
                mm.then_inc(projected, 1)
                wait(pe, step, b * NV + at["k"])
                wait(pe, q_kept, b)
                wait(pe, kb_kept, b)
                for t in range(T):
                    nc.tensor.transpose(p_q[:, t * P:(t + 1) * P], q_n[:, t, :], ident[:])
                    mm = nc.tensor.transpose(p_k[:, t * P:(t + 1) * P], k_n[:, t, :], ident[:])
                mm.then_inc(qk_turned, 1)


def sampling_points(nc, tag, d, ident_bf, Q_all, I_all, F_all):
    G = 16
    N = C + G
    with ExitStack() as ctx:
        m = Scope(nc, ctx, tag + "s")
        patch = [m.sb(f"patch{u}", [P, T, 4, C]) for u in range(2)]
        f_ref = m.sb("f_ref", [P, T, 4])
        ref = m.sb("ref", [P, T, 2])
        half = m.sb("half", [P, T, 2, C])
        feat, rest = m.sb("feat", [P, T, C]), m.sb("rest", [P, T, C])
        x_p = [m.sb(f"x_p{k}", [P, T, P], BF16) for k in range(2)]
        x_T = [m.sb(f"x_T{k}", [P, S], BF16) for k in range(2)]
        w_raw, w_rest = m.sb("w_raw", [P, N]), m.sb("w_rest", [P, N])
        w_s, w_lo = m.sb("w_s", [P, 3, N], BF16), m.sb("w_lo", [P, N], BF16)
        o_raw, o_rest, o_sum = m.sb("o_raw", [P, G]), m.sb("o_rest", [P, G]), m.sb("o_sum", [P, 3, G])
        o_p = m.sb("o_p", [P, 3, G], BF16)
        o_s = m.sb("o_s", [P, G], BF16)
        o_rows = m.sb("o_rows", [P, 3])
        rows = m.sb("rows", [P, 4, G])
        o = m.sb("o", [P, T, G])
        cen, sq, lin = (m.sb(n, [P, T, G]) for n in ("cen", "sq", "lin"))
        mean, ssq, std, rstd = (m.sb(n, [P, T]) for n in ("mean", "ssq", "std", "rstd"))
        h, h_rest = m.sb("h", [P, T, G]), m.sb("h_rest", [P, T, G])
        h_p = m.sb("h_p", [P, T, P], BF16)
        h_T = m.sb("h_T", [P, S], BF16)
        eps = m.sb("eps", [P, 1])
        xy, lo, up, fr, om = (m.sb(n, [P, T, 8, 2]) for n in ("xy", "lo", "up", "fr", "om"))
        whole = m.sb("whole", [P, T, 8, 2], I32)
        row = m.sb("row", [P, T, 8])
        base = m.sb("base", [P, 1])
        p_x = [m.ps(f"p_x{k}", [P, S], BF16) for k in range(2)]
        p_p = m.ps("p_p", [P, T, P])
        p_h = m.ps("p_h", [P, S], BF16)
        p_o = m.ps("p_o", [P, T, G])
        ready, loaded, split_w, split_o = (m.sem(n) for n in ("ready", "loaded", "split_w", "split_o"))
        patch_in = [m.sem(f"patch_in{u}") for u in range(2)]
        (step,
         rooted, bent,
         x_turned, x_kept, projected, p_kept, o_kept, h_turned, h_kept, offset,
         ) = m.counts("step rooted bent x_turned x_kept projected p_kept o_kept h_turned h_kept offset")
        patch_read = m.counts("patch_read0 patch_read1")
        block = ctx.enter_context(nc.Block())
        names = ["prod", "feat", "x_hi", "x_rest", "x_mid", "x_lo", "x_hi2",
                 "o", "sum", "mean", "cen", "sq", "ssq", "rstd", "unit", "scaled", "lin",
                 "h_hi", "h_rest", "h_mid", "h_lo", "h_hi2", "h_mid2", "h_hi3",
                 "biased", "moved", "placed", "unit2", "grown", "clipped", "whole", "back", "over",
                 "floor", "cap", "fr", "om", "row", "idx0", "idx", "f00", "f01", "f10", "f11"]
        at = {n: k + 1 for k, n in enumerate(names)}
        NV = len(names)

        @block.sync
        def _(sp):
            loads = [(w_raw[k * C:(k + 1) * C], d["w_qo"]) for k in range(2)]
            loads += [(o_raw[k * G:(k + 1) * G], d["w_o2"]) for k in range(6)]
            loads += [(rows[:, k], d[n].broadcast_to([P, G])) for k, n in enumerate(("b_o1", "ln_g", "ln_b", "b_o2"))]
            loads += [(f_ref[:], d["f_ref"]), (ref[:], d["ref"]), (o_rows[:], d["o_rows"])]
            assert len(loads) == 15
            sp.wait_ge(ready, 4)
            for dst, src in loads:
                sp.dma_start(dst, src).then_inc(loaded, 16)
            with sp.Fori(0, B // 2) as g:
                for u in range(2):
                    wait(sp, patch_read[u], g)
                    src = d["patches"][bass.ds((2 * g + u) * S, S), :].rearrange("(t p) c -> p t c", p=P)
                    sp.dma_start(patch[u][:].rearrange("p t k c -> p t (k c)"), src).then_inc(patch_in[u], 16)

        @block.gpsimd
        def _(pool):
            nc.gpsimd.memset(o_raw[:], 0.0).then_inc(ready, 1)
            nc.gpsimd.memset(h_p[:], 0.0).then_inc(ready, 1)
            nc.gpsimd.memset(eps[:], EPS).then_inc(ready, 1)
            nc.gpsimd.memset(base[:], 0.0).then_inc(ready, 1)

        @block.vector
        def _(dve):
            dve.wait_ge(ready, 4)
            dve.wait_ge(loaded, 16 * 15)
            split(nc.vector, split_w, 0, w_s[:, 0], w_s[:, 1], w_lo[:], w_raw[:], w_rest[:])
            dve.wait_ge(split_w, 4)
            nc.vector.tensor_copy(w_s[0:C, 2], w_lo[0:C]).then_inc(split_w, 1)
            nc.vector.tensor_copy(w_s[C:P, 2], w_s[C:P, 0]).then_inc(split_w, 1)
            split(nc.vector, split_o, 0, o_p[:, 0], o_p[:, 1], o_p[:, 2], o_raw[:], o_rest[:])
            dve.wait_ge(split_o, 4)
            nc.vector.tensor_tensor(o_sum[:], o_p[:], o_rows[:].unsqueeze(2).broadcast_to([P, 3, G]),
                                    ALU.mult).then_inc(split_o, 1)
            dve.wait_ge(split_o, 5)
            nc.vector.tensor_tensor(o_sum[:, 0], o_sum[:, 0], o_sum[:, 1], ALU.add).then_inc(split_o, 1)
            dve.wait_ge(split_o, 6)
            nc.vector.tensor_tensor(o_s[:], o_sum[:, 0], o_sum[:, 2], ALU.add).then_inc(split_o, 1)

            def batch(b, u, lap):
                def after(name):
                    wait(dve, step, b * NV + at[name])

                def do(name, ins):
                    ins.then_inc(step, 1)
                    assert at[name] == do.n + 1
                    do.n += 1

                do.n = 0
                on = lambda k: rows[:, k].unsqueeze(1).broadcast_to([P, T, G])
                along = lambda v, n: v[:].unsqueeze(2).broadcast_to([P, T, n])
                tt, ts = nc.vector.tensor_tensor, nc.vector.tensor_scalar
                dve.wait_ge(patch_in[u], lap * 16)
                do("prod", tt(patch[u][:], patch[u][:], f_ref[:].unsqueeze(3).broadcast_to([P, T, 4, C]), ALU.mult))
                after("prod")
                tt(half[:], patch[u][:, :, 0:2], patch[u][:, :, 2:4], ALU.add).then_inc(patch_read[u], 1)
                wait(dve, patch_read[u], lap)
                do("feat", tt(feat[:], half[:, :, 0], half[:, :, 1], ALU.add))
                after("feat")
                wait(dve, x_turned, b)
                split(nc.vector, step, b * NV + at["feat"] + 1, x_p[0][:, :, 0:C], x_p[0][:, :, C:P],
                      x_p[1][:, :, C:P], feat[:], rest[:])
                nc.vector.tensor_copy(x_p[1][:, :, 0:C], x_p[0][:, :, 0:C]).then_inc(step, 1)
                do.n += 5
                wait(dve, p_kept, b + 1)
                do("o", tt(o[:], lin[:], on(0), ALU.add))
                after("o")
                do("sum", nc.vector.tensor_reduce(mean[:], o[:], AX.X, ALU.add))
                after("sum")
                do("mean", ts(mean[:], mean[:], 1.0 / G, None, ALU.mult))
                after("mean")
                do("cen", tt(cen[:], o[:], along(mean, G), ALU.subtract))
                after("cen")
                do("sq", tt(sq[:], cen[:], cen[:], ALU.mult))
                after("sq")
                do("ssq", nc.vector.tensor_reduce(ssq[:], sq[:], AX.X, ALU.add))
                wait(dve, rooted, b + 1)
                do("rstd", nc.vector.reciprocal(rstd[:], std[:]))
                after("rstd")
                do("unit", tt(o[:], cen[:], along(rstd, G), ALU.mult))
                after("unit")
                do("scaled", tt(sq[:], o[:], on(1), ALU.mult))
                after("scaled")
                do("lin", tt(cen[:], sq[:], on(2), ALU.add))
                wait(dve, bent, b + 1)
                wait(dve, h_turned, b)
                g = lambda k: h_p[:, :, k * G:(k + 1) * G]
                split(nc.vector, step, b * NV + at["lin"] + 1, g(0), g(1), g(2), h[:], h_rest[:])
                for k, s in ((3, 0), (4, 1), (5, 0)):
                    nc.vector.tensor_copy(g(k), g(s)).then_inc(step, 1)
                do.n += 7
                wait(dve, offset, b + 1)
                flat = lambda v: v[:].rearrange("p t n k -> p t (n k)")
                do("biased", tt(flat(xy), p_o[:], on(3), ALU.add))
                after("biased")
                do("moved", ts(xy[:], xy[:], OFFSET_SCALE, 2.0 / (WD - 1), ALU.mult, ALU.mult))
                after("moved")
                do("placed", tt(xy[:], xy[:], ref[:].unsqueeze(2).broadcast_to([P, T, 8, 2]), ALU.add))
                after("placed")
                do("unit2", ts(xy[:], xy[:], 1.0, 0.5, ALU.add, ALU.mult))
                after("unit2")
                do("grown", ts(xy[:], xy[:], float(WD - 1), 0.0, ALU.mult, ALU.max))
                after("grown")
                do("clipped", ts(xy[:], xy[:], float(WD - 1), None, ALU.min))
                after("clipped")
                do("whole", nc.vector.tensor_copy(whole[:], xy[:]))
                after("whole")
                do("back", nc.vector.tensor_copy(lo[:], whole[:]))
                after("back")
                do("over", tt(up[:], lo[:], xy[:], ALU.is_gt))
                after("over")
                do("floor", tt(lo[:], lo[:], up[:], ALU.subtract))
                after("floor")
                do("cap", ts(lo[:], lo[:], float(WD - 2), None, ALU.min))
                after("cap")
                do("fr", tt(fr[:], xy[:], lo[:], ALU.subtract))
                after("fr")
                do("om", ts(om[:], fr[:], -1.0, 1.0, ALU.mult, ALU.add))
                do("row", ts(row[:], lo[:, :, :, 1], float(WD), base[:, 0:1], ALU.mult, ALU.add))
                after("row")
                do("idx0", tt(row[:], row[:], lo[:, :, :, 0], ALU.add))
                after("idx0")
                do("idx", nc.vector.tensor_copy(I_all[:, bass.ds(b * T, T), :], row[:]))
                nc.vector.tensor_scalar(base[:], base[:], float((WD - 1) * WD), None, ALU.add)
                out = F_all[:, bass.ds(b * T, T), :, :]
                for n, (fx, fy) in enumerate(((om, om), (om, fr), (fr, om), (fr, fr))):
                    do(f"f{n // 2}{n % 2}", tt(out[:, :, :, n], fx[:, :, :, 0], fy[:, :, :, 1], ALU.mult))
                after("f11")

            with dve.Fori(0, B // 2) as g:
                for u in range(2):
                    batch(2 * g + u, u, g + 1)

        @block.scalar
        def _(act):
            act.wait_ge(ready, 4)
            with act.Fori(0, B) as b:
                wait(act, x_turned, b + 1)
                wait(act, projected, b)
                for k in range(2):
                    nc.scalar.copy(x_T[k][:], p_x[k][:]).then_inc(x_kept, 1)
                wait(act, projected, b + 1)
                nc.scalar.copy(lin[:], p_p[:, :, C:N]).then_inc(p_kept, 1)
                nc.scalar.copy(Q_all[:, bass.ds(b * T, T), :], p_p[:, :, 0:C]).then_inc(o_kept, 1)
                wait(act, step, b * NV + at["ssq"])
                nc.scalar.activation(std[:], ssq[:], ACT.Sqrt, bias=eps[:], scale=1.0 / G).then_inc(rooted, 1)
                wait(act, step, b * NV + at["lin"])
                nc.scalar.activation(h[:], cen[:], ACT.Gelu_apprx_tanh).then_inc(bent, 1)
                wait(act, h_turned, b + 1)
                wait(act, offset, b)
                nc.scalar.copy(h_T[:], p_h[:]).then_inc(h_kept, 1)
            wait(act, o_kept, B)

        @block.tensor
        def _(pe):
            pe.wait_ge(split_w, 6)
            pe.wait_ge(split_o, 7)
            with pe.Fori(0, B) as b:
                wait(pe, step, b * NV + at["x_hi2"])
                wait(pe, x_kept, 2 * b)
                for k in range(2):
                    for t in range(T):
                        mm = nc.tensor.transpose(p_x[k][:, t * P:(t + 1) * P], x_p[k][:, t, :], ident_bf[:])
                mm.then_inc(x_turned, 1)
                wait(pe, x_kept, 2 * b + 2)
                wait(pe, o_kept, b)
                for t in range(T):
                    for q in range(3):
                        mm = nc.tensor.matmul(p_p[:, t, 0:N], x_T[q // 2][:, t * P:(t + 1) * P], w_s[:, q],
                                              start=(q == 0), stop=(q == 2))
                mm.then_inc(projected, 1)
                wait(pe, step, b * NV + at["h_hi3"])
                wait(pe, h_kept, b)
                for t in range(T):
                    mm = nc.tensor.transpose(p_h[:, t * P:(t + 1) * P], h_p[:, t, :], ident_bf[:])
                mm.then_inc(h_turned, 1)
                wait(pe, h_kept, b + 1)
                for t in range(T):
                    mm = nc.tensor.matmul(p_o[:, t, :], h_T[:, t * P:(t + 1) * P], o_s[:], start=True, stop=True)
                mm.then_inc(offset, 1)


def deformable_attention(nc, tag, d, ident, Q_all, I_all, F_all, hid):
    U = 4
    R = 4
    NP = 8
    with ExitStack() as ctx:
        m = Scope(nc, ctx, tag + "d")
        patch = [m.sb(f"patch{r}", [P, NP, 4 * C]) for r in range(R)]
        rows = [m.sb(f"rows{r}", [P, NP], I32) for r in range(R)]
        half = m.sb("half", [P, NP, 2 * C])
        point = [m.sb(f"point{r}", [P, NP, C]) for r in range(2)]
        p_sb = [m.sb(f"p_sb{r}", [P, NP // 2, P]) for r in range(2)]
        w_kv = m.sb("w_kv", [P, 2, 2 * C])
        prod = m.sb("prod", [P, NP, C])
        score = m.sb("score", [P, U, NP, NP])
        top, tot = m.sb("top", [P, U, NP]), m.sb("tot", [P, U, NP])
        shifted, ex, attn = (m.sb(n, [P, U, NP, NP]) for n in ("shifted", "ex", "attn"))
        val = [m.sb(f"val{k}", [P, NP, C]) for k in range(U)]
        p_t = [m.ps(f"p_t{r}", [P, NP // 2, P]) for r in range(2)]
        p_kv = [m.ps(f"p_kv{r}", [P, NP, 2 * C]) for r in range(2)]
        fetched = [m.sem(f"fetched{r}") for r in range(R)]
        ready, loaded = m.sem("ready"), m.sem("loaded")
        (step,
         rows_set, turned, t_kept, projected, v_kept, raised,
         ) = m.counts("step rows_set turned t_kept projected v_kept raised")
        freed = m.counts(" ".join(f"freed{r}" for r in range(R)))
        block = ctx.enter_context(nc.Block())
        names = []
        for k in range(U):
            names += [f"prod{k}", f"point{k}"]
            if k:
                names += [f"qk{k - 1}", f"score{k - 1}"]
        names += [f"qk{U - 1}", f"score{U - 1}", "top", "shifted", "tot", "rtot", "attn"]
        for k in range(U):
            names += [f"av{k}", f"out{k}"]
        at = {n: k + 1 for k, n in enumerate(names)}
        NV = len(names)

        @block.sync
        def _(sp):
            sp.wait_ge(ready, 1)
            for e in range(2):
                sp.dma_start(w_kv[e * C:(e + 1) * C, e], d["w_kv"]).then_inc(loaded, 16)

        @block.gpsimd
        def _(pool):
            nc.gpsimd.memset(w_kv[:], 0.0).then_inc(ready, 1)
            with pool.Fori(0, NT // U) as g:
                for k in range(U):
                    wait(pool, freed[k], g)
                    nc.gpsimd.tensor_copy(rows[k][:], I_all[:, bass.ds(g * U + k, 1), :].rearrange("p a n -> p (a n)")).then_inc(rows_set, 1)
                    wait(pool, rows_set, g * U + k + 1)
                    nc.gpsimd.nop(nofuse=True)
                    for n in range(NP):
                        nc.gpsimd.indirect_dma_start(
                            out=patch[k][:, n, :], out_offset=None, in_=d["pixels"],
                            in_offset=bass.IndirectOffsetOnAxis(ap=rows[k][:, n:n + 1], axis=0),
                        ).then_inc(fetched[k], 16)

        @block.vector
        def _(dve):
            with dve.Fori(0, NT // U) as g:
                def after(name):
                    wait(dve, step, g * NV + at[name])

                def do(name, ins):
                    ins.then_inc(step, 1)
                    assert at[name] == do.n + 1, name
                    do.n += 1

                do.n = 0
                tt = nc.vector.tensor_tensor
                wait(dve, step, g * NV)

                def sample(k):
                    dve.wait_ge(fetched[k], (g + 1) * (16 * NP))
                    f = F_all[:, bass.ds(g * U + k, 1), :, :].rearrange("p a n k -> p (a n k)")
                    x = patch[k][:].rearrange("p n (k c) -> p (n k) c", c=C)
                    do(f"prod{k}", tt(x, x, f.unsqueeze(2).broadcast_to([P, 4 * NP, C]), ALU.mult))
                    after(f"prod{k}")
                    if k:
                        after(f"point{k - 1}")
                    tt(half[:], patch[k][:, :, 0:2 * C], patch[k][:, :, 2 * C:4 * C], ALU.add).then_inc(freed[k], 1)
                    wait(dve, freed[k], g + 1)
                    wait(dve, turned, g * U + max(k - 1, 0))
                    do(f"point{k}", tt(point[k % 2][:], half[:, :, 0:C], half[:, :, C:2 * C], ALU.add))

                def scores(k):
                    wait(dve, v_kept, g * U + k + 1)
                    if k:
                        after(f"score{k - 1}")
                    q = Q_all[:, bass.ds(g * U + k, 1), :].broadcast_to([P, NP, C])
                    do(f"qk{k}", tt(prod[:], p_kv[k % 2][:, :, 0:C], q, ALU.mult))
                    after(f"qk{k}")
                    do(f"score{k}", nc.vector.tensor_reduce(
                        score[:, k].rearrange("p n h -> p (n h)"),
                        prod[:].rearrange("p n (h d) -> p (n h) d", h=NP), AX.X, ALU.add))

                for k in range(U):
                    sample(k)
                    if k:
                        scores(k - 1)
                scores(U - 1)
                after(f"score{U - 1}")
                do("top", nc.vector.tensor_reduce(top[:], score[:].rearrange("p t n h -> p t h n"), AX.X, ALU.max))
                after("top")
                do("shifted", tt(shifted[:], score[:], top[:].unsqueeze(2).broadcast_to([P, U, NP, NP]), ALU.subtract))
                wait(dve, raised, g + 1)
                do("tot", nc.vector.tensor_reduce(tot[:], ex[:].rearrange("p t n h -> p t h n"), AX.X, ALU.add))
                after("tot")
                do("rtot", nc.vector.reciprocal(tot[:], tot[:]))
                after("rtot")
                do("attn", tt(attn[:], ex[:], tot[:].unsqueeze(2).broadcast_to([P, U, NP, NP]), ALU.mult))
                after("attn")
                for k in range(U):
                    v = val[k][:].rearrange("p n (h d) -> p (n h) d", h=NP)
                    do(f"av{k}", tt(v, v, attn[:, k].rearrange("p n h -> p (n h)").unsqueeze(2).broadcast_to([P, NP * NP, C // NP]),
                                    ALU.mult))
                    after(f"av{k}")
                    do(f"out{k}", nc.vector.tensor_reduce(
                        hid[:, bass.ds(g * U + k, 1), :].rearrange("p a c -> p (a c)"),
                        val[k][:].rearrange("p n c -> p c n"), AX.X, ALU.add))
            wait(dve, step, NV * (NT // U))

        @block.scalar
        def _(act):
            with act.Fori(0, NT // U) as g:
                for k in range(U):
                    i = g * U + k
                    r = k % 2
                    wait(act, turned, i + 1)
                    wait(act, projected, g * U + max(k - 1, 0))
                    nc.scalar.copy(p_sb[r][:], p_t[r][:]).then_inc(t_kept, 1)
                    wait(act, projected, i + 1)
                    if k == 0:
                        wait(act, step, g * NV)
                    nc.scalar.copy(val[k][:], p_kv[r][:, :, C:2 * C]).then_inc(v_kept, 1)
                wait(act, step, g * NV + at["shifted"])
                nc.scalar.activation(ex[:], shifted[:], ACT.Exp, scale=float((C // NP) ** -0.5)).then_inc(raised, 1)

        @block.tensor
        def _(pe):
            pe.wait_ge(loaded, 32)
            with pe.Fori(0, NT // U) as g:
                def point_step(k):
                    return g * NV + at[f"point{k}"]

                for k in range(U):
                    i = g * U + k
                    r = k % 2
                    wait(pe, step, point_step(k))
                    wait(pe, t_kept, g * U + max(k - 1, 0))
                    for j in range(NP // 2):
                        mm = nc.tensor.transpose(p_t[r][:, j, :], point[r][:, 2 * j:2 * j + 2, :].rearrange("p n c -> p (n c)"),
                                                 ident[:])
                    mm.then_inc(turned, 1)
                    wait(pe, t_kept, i + 1)
                    if k >= 2:
                        wait(pe, step, g * NV + at[f"qk{k - 2}"])
                    for j in range(NP // 2):
                        mm = nc.tensor.matmul(p_kv[r][:, 2 * j:2 * j + 2, :], p_sb[r][:, j, :],
                                              w_kv[:].rearrange("p e n -> p (e n)"), start=True, stop=True)
                    mm.then_inc(projected, 1)


def gates(nc, tag, kind, hid, ident_bf, router, norm_row, X_all, G_all):
    layer = kind == "layer"
    with ExitStack() as ctx:
        m = Scope(nc, ctx, tag + "g")
        mean = m.sb("mean", [P, T])
        cen = m.sb("cen", [P, T, C])
        sq = m.sb("sq", [P, T, C])
        ssq = m.sb("ssq", [P, T])
        std = m.sb("std", [P, T])
        rstd = m.sb("rstd", [P, T])
        eps = m.sb("eps", [P, 1])
        xn = m.sb("xn", [P, T, C])
        rest = m.sb("rest", [P, T, C])
        x_hm = m.sb("x_hm", [P, T, P], BF16)
        x_hl = m.sb("x_hl", [P, T, P], BF16)
        w_raw = m.sb("w_raw", [P, E])
        w_rest = m.sb("w_rest", [P, E])
        w_s = m.sb("w_s", [P, 3, E], BF16)
        w_lo = m.sb("w_lo", [P, E], BF16)
        w_n = m.sb("w_n", [P, C])
        top = m.sb("top", [P, T])
        ex = m.sb("ex", [P, T, E])
        prob = m.sb("prob", [P, T, E])
        tot = m.sb("tot", [P, T])
        best = m.sb("best", [P, T, 8])
        which = m.sb("which", [P, T, 8], U32)
        where = m.sb("where", [P, T, 8])
        order = m.sb("order", [P, T, E])
        hit = m.sb("hit", [P, 2, T, E])
        gate = m.sb("gate", [P, T, E])
        g_rest = m.sb("g_rest", [P, T, E])
        g_s = m.sb("g_s", [P, T, P], BF16)
        p_t = [m.ps(f"p_t{k}", [P, S], BF16) for k in range(2)]
        p_l = m.ps("p_l", [P, T, E])
        p_g = m.ps("p_g", [P, S], BF16)
        (step,
         rooted,
         turned,
         kept,
         scored,
         raised,
         gates_turned,
         gates_kept,
         ) = m.counts("step rooted turned kept scored raised gates_turned gates_kept")
        ready, loaded, w_split = m.sem("ready"), m.sem("loaded"), m.sem("w_split")
        block = ctx.enter_context(nc.Block())

        @block.sync
        def _(sp):
            for h in range(2):
                sp.dma_start(w_raw[h * C:(h + 1) * C], router).then_inc(loaded, 16)
            if not layer:
                sp.dma_start(w_n[:], norm_row.broadcast_to([P, C])).then_inc(loaded, 16)

        @block.gpsimd
        def _(pool):
            nc.gpsimd.memset(g_s[:], 0.0).then_inc(ready, 1)
            nc.gpsimd.memset(eps[:], EPS if layer else EPS_RMS).then_inc(ready, 1)
            nc.gpsimd.iota(order[:], pattern=[[0, T], [1, E]], base=0, channel_multiplier=0,
                           allow_small_or_imprecise_dtypes=True).then_inc(ready, 1)
            pool.wait_ge(ready, 3)

        names = ["sum", "mean", "cen", "sq", "ssq", "rstd", "xn", "x_hi", "x_rest", "x_mid", "x_lo", "x_hi2", "top", "sub", "tot", "rtot", "prob"] + \
                [f"best{t}" for t in range(T)] + [f"which{t}" for t in range(T)] + \
                ["where", "norm", "rnorm", "hit0", "hit1", "val0", "val1", "sum2", "gate",
                 "g_hi", "g_rest", "g_mid", "g_lo", "g_hi2"]
        if not layer:
            names[0:3] = []
            names.insert(names.index("xn"), "scaled")
        at = {n: k + 1 for k, n in enumerate(names)}
        NV = len(names)

        @block.vector
        def _(dve):
            dve.wait_ge(ready, 3)
            dve.wait_ge(loaded, 32 if layer else 48)
            split(nc.vector, w_split, 0, w_s[:, 0], w_s[:, 1], w_lo[:], w_raw[:], w_rest[:])
            dve.wait_ge(w_split, 4)
            nc.vector.tensor_copy(w_s[0:C, 2], w_lo[0:C]).then_inc(w_split, 1)
            nc.vector.tensor_copy(w_s[C:P, 2], w_s[C:P, 0]).then_inc(w_split, 1)
            bc = lambda ap, shape: ap.unsqueeze(2).broadcast_to(shape)
            with dve.Fori(0, B) as b:
                def after(name):
                    wait(dve, step, b * NV + at[name])

                x = hid[:, bass.ds(b * T, T), :]
                if layer:
                    nc.vector.tensor_reduce(mean[:], x, AX.X, ALU.add).then_inc(step, 1)
                    after("sum")
                    nc.vector.tensor_scalar(mean[:], mean[:], 1.0 / C, None, ALU.mult).then_inc(step, 1)
                    after("mean")
                    nc.vector.tensor_tensor(cen[:], x, bc(mean[:], [P, T, C]), ALU.subtract).then_inc(step, 1)
                    after("cen")
                    nc.vector.tensor_tensor(sq[:], cen[:], cen[:], ALU.mult).then_inc(step, 1)
                else:
                    nc.vector.tensor_tensor(sq[:], x, x, ALU.mult).then_inc(step, 1)
                after("sq")
                nc.vector.tensor_reduce(ssq[:], sq[:], AX.X, ALU.add).then_inc(step, 1)
                wait(dve, rooted, b + 1)
                nc.vector.reciprocal(rstd[:], std[:]).then_inc(step, 1)
                after("rstd")
                if layer:
                    nc.vector.tensor_tensor(xn[:, :, 0:C], cen[:], bc(rstd[:], [P, T, C]), ALU.mult).then_inc(step, 1)
                    after("xn")
                    nc.vector.tensor_tensor(x, x, xn[:, :, 0:C], ALU.add)
                else:
                    nc.vector.tensor_tensor(cen[:], x, bc(rstd[:], [P, T, C]), ALU.mult).then_inc(step, 1)
                    after("scaled")
                    nc.vector.tensor_tensor(xn[:, :, 0:C], cen[:], w_n[:].unsqueeze(1).broadcast_to([P, T, C]),
                                            ALU.mult).then_inc(step, 1)
                after("xn")
                wait(dve, turned, b)
                split(nc.vector, step, b * NV + at["xn"] + 1, x_hm[:, :, 0:C], x_hm[:, :, C:P], x_hl[:, :, C:P],
                      xn[:], rest[:])
                nc.vector.tensor_copy(x_hl[:, :, 0:C], x_hm[:, :, 0:C]).then_inc(step, 1)
                wait(dve, scored, b + 1)
                nc.vector.tensor_reduce(top[:], p_l[:], AX.X, ALU.max).then_inc(step, 1)
                after("top")
                nc.vector.tensor_tensor(ex[:], p_l[:], bc(top[:], [P, T, E]), ALU.subtract).then_inc(step, 1)
                wait(dve, raised, b + 1)
                nc.vector.tensor_reduce(tot[:], ex[:], AX.X, ALU.add).then_inc(step, 1)
                after("tot")
                nc.vector.reciprocal(tot[:], tot[:]).then_inc(step, 1)
                after("rtot")
                nc.vector.tensor_tensor(prob[:], ex[:], bc(tot[:], [P, T, E]), ALU.mult).then_inc(step, 1)
                after("prob")
                nc.vector.nop(nofuse=True)
                for t in range(T):
                    nc.vector.max(best[:, t], prob[:, t]).then_inc(step, 1)
                after(f"best{T - 1}")
                nc.vector.nop(nofuse=True)
                for t in range(T):
                    nc.vector.max_index(which[:, t], best[:, t], prob[:, t]).then_inc(step, 1)
                after(f"which{T - 1}")
                nc.vector.tensor_copy(where[:], which[:]).then_inc(step, 1)
                nc.vector.tensor_tensor(tot[:], best[:, :, 0], best[:, :, 1], ALU.add).then_inc(step, 1)
                after("norm")
                if layer:
                    nc.vector.tensor_scalar(tot[:], tot[:], 1e-12, None, ALU.max).then_inc(step, 1)
                else:
                    nc.vector.tensor_scalar(tot[:], tot[:], 1e-9, None, ALU.add).then_inc(step, 1)
                after("rnorm")
                for k in range(2):
                    nc.vector.tensor_tensor(hit[:, k], order[:], where[:, :, k:k + 1].broadcast_to([P, T, E]),
                                            ALU.is_equal).then_inc(step, 1)
                after("hit1")
                for k in range(2):
                    nc.vector.tensor_tensor(hit[:, k], hit[:, k], best[:, :, k:k + 1].broadcast_to([P, T, E]),
                                            ALU.mult).then_inc(step, 1)
                after("val1")
                nc.vector.reciprocal(tot[:], tot[:])
                nc.vector.tensor_tensor(hit[:, 0], hit[:, 0], hit[:, 1], ALU.add).then_inc(step, 1)
                after("sum2")
                nc.vector.tensor_tensor(gate[:], hit[:, 0], bc(tot[:], [P, T, E]), ALU.mult).then_inc(step, 1)
                after("gate")
                wait(dve, gates_turned, b)
                split(nc.vector, step, b * NV + at["gate"] + 1, g_s[:, :, 0:E], g_s[:, :, 32:32 + E],
                      g_s[:, :, 64:64 + E], gate[:], g_rest[:])
                nc.vector.tensor_copy(g_s[:, :, 96:96 + E], g_s[:, :, 0:E]).then_inc(step, 1)
                wait(dve, gates_turned, b + 1)
                nc.vector.tensor_copy(G_all[:, bass.ds(b * S, S)], p_g[:]).then_inc(gates_kept, 1)
            wait(dve, gates_kept, B)

        @block.scalar
        def _(act):
            act.wait_ge(ready, 3)
            with act.Fori(0, B) as b:
                wait(act, step, b * NV + at["ssq"])
                nc.scalar.activation(std[:], ssq[:], ACT.Sqrt, bias=eps[:], scale=1.0 / C).then_inc(rooted, 1)
                wait(act, turned, b + 1)
                for k in range(2):
                    nc.scalar.copy(X_all[:, k, bass.ds(b * S, S)], p_t[k][:]).then_inc(kept, 1)
                wait(act, step, b * NV + at["sub"])
                nc.scalar.activation(ex[:], ex[:], ACT.Exp).then_inc(raised, 1)
            wait(act, kept, 2 * B)

        @block.tensor
        def _(pe):
            pe.wait_ge(w_split, 6)
            with pe.Fori(0, B) as b:
                wait(pe, step, b * NV + at["x_hi2"])
                wait(pe, kept, 2 * b)
                for k, x in enumerate((x_hm, x_hl)):
                    for t in range(T):
                        mm = nc.tensor.transpose(p_t[k][:, t * P:(t + 1) * P], x[:, t, :], ident_bf[:])
                mm.then_inc(turned, 1)
                wait(pe, kept, 2 * b + 2)
                for t in range(T):
                    for k in range(3):
                        mm = nc.tensor.matmul(p_l[:, t, :], X_all[:, k // 2, bass.ds(b * S + t * P, P)], w_s[:, k],
                                              start=(k == 0), stop=(k == 2))
                mm.then_inc(scored, 1)
                wait(pe, step, b * NV + at["g_hi2"])
                wait(pe, gates_kept, b)
                for t in range(T):
                    mm = nc.tensor.transpose(p_g[:, t * P:(t + 1) * P], g_s[:, t, :], ident_bf[:])
                mm.then_inc(gates_turned, 1)


def experts(nc, tag, kind, hid, ident, w, X_all, G_all):
    gelu = kind == "gelu"
    hidden = w["w2"].shape[0]
    NK = (hidden + P - 1) // P
    full, over = hidden // P, hidden % P
    CH = 512
    NCH = B * S // CH
    J = CH // P
    with ExitStack() as ctx:
        m = Scope(nc, ctx, tag + "e")
        NW = 1 if gelu else 2
        w_raw = m.sb("w_raw", [P, NK * P])
        w_rest = m.sb("w_rest", [P, NK * P])
        w_lo = m.sb("w_lo", [P, NK * P], BF16)
        w_in = [[m.sb(f"w_in{n}{k}", [P, NK * P], BF16) for k in range(3)] for n in range(NW)]
        w2 = m.sb("w2", [P, NK, P])
        b1 = m.sb("b1", [P, NK]) if gelu else None
        b2_raw = m.sb("b2_raw", [P, C])
        b2_rest = m.sb("b2_rest", [P, C])
        b2_part = m.sb("b2_part", [P, 3, C], BF16)
        b2 = m.sb("b2", [P, 2, P], BF16)
        spread_raw = m.sb("spread_raw", [P, NK * P])
        spread = m.sb("spread", [P, NK * P], BF16)
        act_h = m.sb("act_h", [P, 2, CH])
        up = m.sb("up", [P, 2, CH])
        gated = m.sb("gated", [P, 2, CH])
        yT = m.sb("yT", [P, CH])
        p_a = [m.ps(f"p_a{r}", [P, CH]) for r in range(2)]
        p_b = [m.ps(f"p_b{r}", [P, CH]) for r in range(2)]
        p_g = [m.ps(f"p_g{r}", [P, CH]) for r in range(2)]
        p_y = m.ps("p_y", [P, CH])
        p_o = m.ps("p_o", [P, J, P])
        (a_made,
         b_made,
         act_done,
         up_done,
         gated_done,
         y_done,
         y_kept,
         turned,
         added,
         ) = m.counts("a_made b_made act_done up_done gated_done y_done y_kept turned added")
        loaded, loaded3, zeroed, w_split, b_split = (m.sem(n) for n in
                                                     ("loaded", "loaded3", "zeroed", "w_split", "b_split"))
        block = ctx.enter_context(nc.Block())
        loads = [(spread_raw[k * 32:k * 32 + E, 0:hidden], w["spread"]) for k in range(3)]
        loads.append((w2[:, 0:full, 0:C], w["w2"][0:full * P, :].rearrange("(k p) c -> p k c", p=P)))
        loads += [(w_raw[h * C:(h + 1) * C, 0:hidden], w["w1"]) for h in range(2)]
        if over:
            loads.append((w2[0:over, full, 0:C], w["w2"][full * P:hidden, :]))
        if gelu:
            loads.append((b1[:], w["b1"]))
            loads += [(b2_raw[k * 32:k * 32 + E], w["b2"]) for k in range(4)]
        zeroing = [spread_raw, w_raw, w2, b2_raw, b2]

        @block.sync
        def _(sp):
            sp.wait_ge(zeroed, len(zeroing))
            for dst, src in loads:
                sp.dma_start(dst, src).then_inc(loaded, 16)
            if not gelu:
                sp.wait_ge(w_split, 6)
                for h in range(2):
                    sp.dma_start(w_raw[h * C:(h + 1) * C, 0:hidden], w["w3"]).then_inc(loaded3, 16)

        @block.gpsimd
        def _(pool):
            for x in zeroing:
                nc.gpsimd.memset(x[:], 0.0).then_inc(zeroed, 1)

        @block.tensor
        def _(pe):
            pe.wait_ge(w_split, 6 * NW)
            pe.wait_ge(b_split, 8 if gelu else 1)

            def second(n, k):
                wait(pe, gated_done, n * NK + k + 1)
                mm = nc.tensor.matmul(p_y[:], w2[:, k, :], gated[:, k % 2, :], start=(k == 0 and not gelu),
                                      stop=(k == NK - 1))
                mm.then_inc(y_done, 1)

            def first(out, w, n, k):
                for q in range(3):
                    mm = nc.tensor.matmul(out, w[q][:, k * P:(k + 1) * P], X_all[:, q // 2, bass.ds(n * CH, CH)],
                                          start=(q == 0), stop=(q == 2))
                return mm

            with pe.Fori(0, NCH) as n:
                wait(pe, y_kept, n)
                if gelu:
                    for q in range(2):
                        nc.tensor.matmul(p_y[:], b2[:, q], G_all[:, bass.ds(n * CH, CH)], start=(q == 0), stop=False)
                for k in range(NK):
                    u = k % 2
                    last = n * NK + max(k - 1, 0)
                    wait(pe, act_done, last)
                    first(p_a[u][:], w_in[0], n, k).then_inc(a_made, 1)
                    wait(pe, gated_done, last)
                    if not gelu:
                        first(p_b[u][:], w_in[1], n, k)
                    nc.tensor.matmul(p_g[u][:], spread[:, k * P:(k + 1) * P], G_all[:, bass.ds(n * CH, CH)],
                                     start=True, stop=True).then_inc(b_made, 1)
                    if k:
                        second(n, k - 1)
                second(n, NK - 1)
                wait(pe, y_kept, n + 1)
                wait(pe, added, n)
                for j in range(J):
                    mm = nc.tensor.transpose(p_o[:, j, :], yT[:, j * P:(j + 1) * P], ident[:])
                mm.then_inc(turned, 1)

        @block.scalar
        def _(act):
            act.wait_ge(loaded, 16 * len(loads))
            with act.Fori(0, NCH) as n:
                for k in range(NK):
                    u = k % 2
                    wait(act, a_made, n * NK + k + 1)
                    wait(act, gated_done if gelu else up_done, n * NK + max(k - 1, 0))
                    if gelu:
                        nc.scalar.activation(act_h[:, u, :], p_a[u][:], ACT.Gelu,
                                             bias=b1[:, k:k + 1]).then_inc(act_done, 1)
                    else:
                        nc.scalar.activation(act_h[:, u, :], p_a[u][:], ACT.Silu).then_inc(act_done, 1)
                wait(act, y_done, NK * (n + 1))
                wait(act, turned, n)
                nc.scalar.copy(yT[:], p_y[:]).then_inc(y_kept, 1)

        @block.vector
        def _(dve):
            for n in range(NW):
                dve.wait_ge(loaded if n == 0 else loaded3, 16 * len(loads) if n == 0 else 32)
                split(nc.vector, w_split, 6 * n, w_in[n][0][:], w_in[n][1][:], w_lo[:], w_raw[:], w_rest[:])
                dve.wait_ge(w_split, 6 * n + 4)
                nc.vector.tensor_copy(w_in[n][2][0:C], w_lo[0:C]).then_inc(w_split, 1)
                nc.vector.tensor_copy(w_in[n][2][C:P], w_in[n][0][C:P]).then_inc(w_split, 1)
                dve.wait_ge(w_split, 6 * n + 6)
            nc.vector.tensor_copy(spread[:], spread_raw[:]).then_inc(b_split, 1)
            if gelu:
                split(nc.vector, b_split, 1, b2_part[:, 0], b2_part[:, 1], b2_part[:, 2], b2_raw[:], b2_rest[:])
                dve.wait_ge(b_split, 5)
                nc.vector.tensor_copy(b2[0:96, 0, 0:C], b2_part[0:96, 0])
                nc.vector.tensor_copy(b2[96:P, 0, 0:C], b2_part[96:P, 1]).then_inc(b_split, 1)
                nc.vector.tensor_copy(b2[0:32, 1, 0:C], b2_part[0:32, 2]).then_inc(b_split, 1)
                nc.vector.tensor_copy(b2[32:64, 1, 0:C], b2_part[32:64, 1]).then_inc(b_split, 1)
            with dve.Fori(0, NCH) as n:
                for k in range(NK):
                    u = k % 2
                    wait(dve, act_done, n * NK + k + 1)
                    wait(dve, b_made, n * NK + k + 1)
                    wait(dve, y_done, n * NK + max(k - 1, 0))
                    if gelu:
                        nc.vector.tensor_tensor(gated[:, u, :], act_h[:, u, :], p_g[u][:],
                                                ALU.mult).then_inc(gated_done, 1)
                    else:
                        nc.vector.tensor_tensor(up[:, u, :], act_h[:, u, :], p_b[u][:],
                                                ALU.mult).then_inc(up_done, 1)
                        wait(dve, up_done, n * NK + k + 1)
                        nc.vector.tensor_tensor(gated[:, u, :], up[:, u, :], p_g[u][:],
                                                ALU.mult).then_inc(gated_done, 1)
                wait(dve, turned, n + 1)
                x = hid[:, bass.ds(n * J, J), :]
                nc.vector.tensor_tensor(x, x, p_o[:, :, 0:C], ALU.add).then_inc(added, 1)
            wait(dve, added, NCH)


def build(nc, ins, out, stages):
    with ExitStack() as ctx:
        g = Scope(nc, ctx, "g")
        hid = g.sb("hid", [P, NT, C])
        ident = g.sb("ident", [P, P])
        ident_bf = g.sb("ident_bf", [P, P], BF16)
        loaded, made, stored = g.sem("loaded"), g.sem("made"), g.sem("stored")
        summed = g.sem("summed")
        with nc.Block() as block:
            @block.gpsimd
            def _(pool):
                nc.gpsimd.memset(ident[:], 0.0).then_inc(made, 1)
                pool.wait_ge(made, 1)
                nc.gpsimd.affine_select(out=ident[:], in_=ident[:], compare_op=ALU.not_equal, fill=1.0,
                                        base=0, pattern=[[-1, P]], channel_multiplier=1).then_inc(made, 1)
                pool.wait_ge(made, 2)
                nc.gpsimd.tensor_copy(ident_bf[:], ident[:]).then_inc(made, 1)
                pool.wait_ge(made, 3)

            @block.sync
            def _(sp):
                if "h" in ins:
                    sp.dma_start(hid[:], ins["h"].rearrange("(t p) c -> p t c", p=P)).then_inc(loaded, 16)
                    sp.wait_ge(loaded, 16)

        def attn_layer(tag, H, scale, w, bias_row):
            with ExitStack() as sub:
                m = Scope(nc, sub, tag)
                A_all = m.sb("A_all", [C, H, C])
                W_aug = m.sb("W_aug", [P, H, 2, C + 1])
                V_all = m.sb("V_all", [P, NT, C])
                K_all = m.sb("K_all", [C, B * S])
                KB_all = m.sb("KB_all", [P, B * S], BF16)
                attention_weights(nc, tag, H, scale, w, ident, A_all, W_aug)
                normed_tokens(nc, tag, hid, ident, V_all, K_all, KB_all, bias_row)
                attention(nc, tag, H, hid, ident, A_all, W_aug, V_all, K_all, K_all, KB_all)

        if "tok" in stages:
            with ExitStack() as sub:
                m = Scope(nc, sub, "tk")
                Q_all = m.sb("Q_all", [P, NT, C])
                I_all = m.sb("I_all", [P, NT, 8], I32)
                F_all = m.sb("F_all", [P, NT, 8, 4])
                sampling_points(nc, "tk", ins, ident_bf, Q_all, I_all, F_all)
                deformable_attention(nc, "tk", ins, ident, Q_all, I_all, F_all, hid)
        if "attn0" in stages:
            attn_layer("l0", 8, 8 ** -0.5, {"q": ins["WQT"], "k": ins["WKT"], "v": ins["WVT"], "o": ins["Wout"],
                                            "bq": None}, ins["bout"])
        def moe_layer(tag, kinds, hid, router, norm_row, w):
            with ExitStack() as sub:
                m = Scope(nc, sub, tag)
                X_all = m.sb("X_all", [P, 2, B * S], BF16)
                G_all = m.sb("G_all", [P, B * S], BF16)
                gates(nc, tag, kinds[0], hid, ident_bf, router, norm_row, X_all, G_all)
                experts(nc, tag, kinds[1], hid, ident, w, X_all, G_all)

        if "moe0" in stages:
            moe_layer("m0", ("layer", "gelu"), hid, ins["router0"], None,
                      {"w1": ins["w1_0"], "w2": ins["w2_0"], "b1": ins["b1_0"], "b2": ins["b2_0"],
                       "spread": ins["spread0"]})
        if "attn1" in stages:
            attn_layer("l1", 1, C ** -0.5, {"q": ins["Wq1"], "k": ins["Wk1"], "v": ins["Wv1"], "o": ins["Wo1T"],
                                            "bq": ins["bq1"], "bk": ins["bk1"], "bv": ins["bv1"]}, ins["bo1"])

        xs = g.sb("xs", [P, NT, C])
        last = "moe1" in stages or "gqa" in stages
        if last:
            layer_norm(nc, "n1", hid, xs)
        if "gqa" in stages:
            with ExitStack() as sub:
                m = Scope(nc, sub, "q1")
                A_all = m.sb("A_all", [C, 4, C])
                W_aug = m.sb("W_aug", [P, 4, 2, C + 1])
                V_all = m.sb("V_all", [P, NT, C])
                Q_all = m.sb("Q_all", [C, B * S])
                K_all = m.sb("K_all", [C, B * S])
                KB_all = m.sb("KB_all", [P, B * S], BF16)
                masks = m.sb("masks", [P, 2, P], BF16)
                masks_32 = m.sb("masks_32", [P, 2, P])
                w_loaded, w_ready = m.sem("w_loaded"), m.sem("w_ready")
                with nc.Block() as block:
                    @block.gpsimd
                    def _(pool):
                        nc.gpsimd.memset(W_aug[:], 0.0).then_inc(w_ready, 1)
                        nc.gpsimd.memset(masks_32[:], 0.0).then_inc(w_ready, 1)
                        pool.wait_ge(w_ready, 2)
                        for k, sign in enumerate((1, -1)):
                            nc.gpsimd.affine_select(out=masks_32[:, k], in_=masks_32[:, k], compare_op=ALU.is_ge,
                                                    fill=-1e30, base=0, pattern=[[-sign, P]],
                                                    channel_multiplier=sign).then_inc(w_ready, 1)
                        pool.wait_ge(w_ready, 4)
                        nc.gpsimd.tensor_copy(masks[:], masks_32[:]).then_inc(w_ready, 1)
                        pool.wait_ge(w_ready, 5)
                        nc.gpsimd.memset(W_aug[0:1, :, 0, C:C + 1], 1.0).then_inc(w_ready, 1)
                        pool.wait_ge(w_ready, 6)
                        nc.gpsimd.memset(W_aug[C:C + 1, :, 1, C:C + 1], 1.0).then_inc(w_ready, 1)
                        pool.wait_ge(w_ready, 7)

                    @block.sync
                    def _(sp):
                        sp.dma_start(A_all[:], ins["pick"]).then_inc(w_loaded, 16)
                        sp.wait_ge(w_ready, 7)
                        for h in range(4):
                            for e in range(2):
                                o = e * C + 1 + 16 * (h // 2)
                                sp.dma_start(W_aug[o:o + 16, h, e, 0:C], ins["woT"][h * 16:(h + 1) * 16]).then_inc(w_loaded, 16)
                        sp.wait_ge(w_loaded, 16 * 9)
                rotary_heads(nc, "q1", xs, ident, ident_bf, ins["ln1"], ins["wqkv"], ins["rope"], V_all, Q_all, K_all, KB_all)
                attention(nc, "q1", 4, xs, ident, A_all, W_aug, V_all, Q_all, K_all, KB_all,
                          (ident_bf, masks[:, 0], masks[:, 1]))
        if "moe1" in stages:
            moe_layer("m1", ("rms", "silu"), xs, ins["router1"], ins["ln2"],
                      {"w1": ins["w1_1"], "w3": ins["w3_1"], "w2": ins["w2_1"], "spread": ins["spread1"]})

        with nc.Block() as block:
            @block.sync
            def _(sp):
                if last:
                    sp.wait_ge(summed, 1)
                sp.dma_start(out.rearrange("(t p) c -> p t c", p=P), hid[:] if not last or "attn0" in stages else xs[:]).then_inc(stored, 16)
                sp.wait_ge(stored, 16)

            @block.vector
            def _(dve):
                if last:
                    nc.vector.tensor_tensor(hid[:], hid[:], xs[:], ALU.add).then_inc(summed, 1)


def host_layout(v, np):
    ins = {}
    if "x" in v:
        image = v["x"].transpose(0, 2, 3, 1)
        ins["pixels"] = np.stack([image[:, :-1], image[:, 1:]], 3).reshape(B * (WD - 1) * WD, 2 * C)
        line = np.linspace(-1.0, 1.0, GRID, dtype=np.float32)
        at = (line + np.float32(1)) * np.float32(0.5) * np.float32(WD - 1)
        lo = np.clip(np.floor(at), 0, WD - 2)
        fr = np.clip(at - lo, 0, 1).astype(np.float32)
        lo = lo.astype(np.int64)
        corner = [image[:, lo + dy][:, :, lo + dx] for dx in (0, 1) for dy in (0, 1)]
        ins["patches"] = np.stack(corner, 3).reshape(B * S, 4 * C)
        tokens = lambda a: a.reshape(T, P, a.shape[-1]).transpose(1, 0, 2)
        fx, fy = np.meshgrid(fr, fr)
        ins["f_ref"] = tokens(np.stack([(1 - fx) * (1 - fy), (1 - fx) * fy, fx * (1 - fy), fx * fy], -1))
        ins["ref"] = tokens(np.stack(np.meshgrid(line, line), -1))
        ins["w_qo"] = np.concatenate([v["L0_tok_W_q"].T, v["L0_tok_W_o1"]], 1)
        ins["w_kv"] = np.concatenate([v["L0_tok_W_k"].T, v["L0_tok_W_v"].T], 1)
        ins["w_o2"] = v["L0_tok_W_o2"]
        for n in ("b_o1", "ln_g", "ln_b", "b_o2"):
            ins[n] = v[f"L0_tok_{n}"].reshape(1, 16)
        ins["o_rows"] = (np.array([0, 0, 0, 1, 1, 2, 3, 3]).repeat(16)[:, None] == np.arange(3)).astype(np.float32)
    heads = lambda w: w.T.reshape(8, C, C).transpose(1, 0, 2)
    for n in "QKV":
        ins[f"W{n}T"] = heads(v[f"L0_attn_W{n}"])
    ins["Wout"] = v["L0_attn_Wout"].reshape(8, C, C).transpose(1, 0, 2)
    ins["bout"] = v["L0_attn_bout"].reshape(1, C)
    for n in "qkv":
        ins[f"W{n}1"] = v[f"L1_attn_W{n}"].reshape(C, 1, C)
        ins[f"b{n}1"] = v[f"L1_attn_b{n}"].reshape(C, 1)
    ins["Wo1T"] = v["L1_attn_Wo"].T.reshape(C, 1, C)
    ins["bo1"] = v["L1_attn_bo"].reshape(1, C)
    of_expert = lambda n: (np.arange(E)[:, None] == np.arange(E * n)[None, :] // n).astype(np.float32)
    ins["router0"] = v["L0_ffn_router_w"].T
    ins["w1_0"] = v["L0_ffn_w1"].transpose(1, 0, 2).reshape(C, E * C)
    ins["w2_0"] = v["L0_ffn_w2"].reshape(E * C, C)
    ins["b1_0"] = v["L0_ffn_b1"].reshape(E * C // P, P).T
    ins["b2_0"] = v["L0_ffn_b2"]
    ins["spread0"] = of_expert(C)
    pick = np.zeros((C, 4, C), np.float32)
    for h in range(4):
        for d in range(16):
            pick[16 * h + d, h, 1 + 32 * (h // 2) + d] = 0.25
    ins["pick"] = pick
    freq = 1.0 / 10000.0 ** (np.arange(0, 16, 2, dtype=np.float32) / 16)
    angle = np.outer(np.arange(S, dtype=np.float32), freq)
    rope = np.stack([np.cos(np.concatenate([angle, angle], -1)),
                     np.sin(np.concatenate([angle, angle], -1)) * np.repeat(np.float32([-1, 1]), 8)])
    ins["rope"] = rope.astype(np.float32).reshape(2, T, P, 16).transpose(2, 0, 1, 3)
    ins["wqkv"] = np.concatenate([v["L1_ffn_wq"], v["L1_ffn_wk"], v["L1_ffn_wv"]]).T
    ins["woT"] = v["L1_ffn_wo"].T
    ins["ln1"] = v["L1_ffn_ln1_w"].reshape(1, C)
    ins["router1"] = v["L1_ffn_router_w"].T
    ins["ln2"] = v["L1_ffn_ln2_w"].reshape(1, C)
    for n in ("w1", "w3"):
        ins[n + "_1"] = v["L1_ffn_" + n].transpose(2, 0, 1).reshape(C, E * HID1)
    ins["w2_1"] = v["L1_ffn_w2"].transpose(0, 2, 1).reshape(E * HID1, C)
    ins["spread1"] = of_expert(HID1)
    return ins


def kernel(**inputs):
    import numpy as np
    import concourse.bacc as bacc
    from concourse.bass_utils import run_bass_kernel_spmd

    v = {k: np.asarray(a) for k, a in inputs.items()}
    ins = host_layout(v, np)
    if "h" in v:
        ins["h"] = v["h"].reshape(B * S, C)
    nc = bacc.Bacc("TRN2", target_bir_lowering=False, num_devices=1)
    arrays, aps = {}, {}
    for name, a in ins.items():
        arrays[name] = np.ascontiguousarray(a)
        aps[name] = nc.dram_tensor(name, arrays[name].shape, mybir.dt.from_np(arrays[name].dtype),
                                   kind="ExternalInput").ap()
    out = nc.dram_tensor("out_tokens", (B * S, C), F32, kind="ExternalOutput").ap()
    build(nc, aps, out, STAGES)
    res = run_bass_kernel_spmd(nc, [arrays], core_ids=[0])
    return res.results[0]["out_tokens"].reshape(B, S, C)


STAGES = ("tok", "attn0", "moe0", "attn1", "gqa", "moe1")
```

```python
from contextlib import ExitStack

import concourse.bass as bass
from concourse import mybir

F32 = mybir.dt.float32
BF16 = mybir.dt.bfloat16
I32 = mybir.dt.int32
U32 = mybir.dt.uint32
ACT = mybir.ActivationFunctionType
ALU = mybir.AluOpType
AX = mybir.AxisListType

P = 128
B = 8
S = 1024
C = 64
T = S // P
NT = B * T
EPS = 1e-5
EPS_RMS = 1e-6
E = 8
HID1 = int(8 / 3 * C)
WD = 128
GRID = 32
OFFSET_SCALE = 4.0


class Scope:

    def __init__(self, nc, ctx, tag):
        self.nc, self.ctx, self.tag = nc, ctx, tag
        self.sems, self.held = [], ExitStack()
        ctx.push(self.clear)

    def sb(self, name, shape, dt=F32):
        return self.ctx.enter_context(self.nc.sbuf_tensor(f"{self.tag}_{name}", shape, dt))

    def ps(self, name, shape, dt=F32):
        return self.ctx.enter_context(self.nc.psum_tensor(f"{self.tag}_{name}", shape, dt))

    def sem(self, name):
        self.sems.append(self.held.enter_context(self.nc.semaphore(f"{self.tag}_{name}")))
        return self.sems[-1]

    def clear(self, failed=None, *_):
        if self.sems and failed is None:
            with self.nc.Block() as block:
                @block.sync
                def _(sp):
                    for s in self.sems:
                        sp.sem_clear(s)
        self.held.close()

    def counts(self, names):
        counting = [self.sem(n) for n in names.split()]
        with self.nc.Block() as block:
            @block.sync
            def _(sp):
                for s in counting:
                    sp.sem_inc(s, 1)
        return counting


def wait(eng, sem, n):
    eng.wait_ge(sem, n + 1)


def split(eng, sem, count, hi, mid, lo, x, rest):
    eng.tensor_copy(hi, x).then_inc(sem, 1)
    eng.wait_ge(sem, count + 1)
    eng.tensor_tensor(rest, x, hi, ALU.subtract).then_inc(sem, 1)
    eng.wait_ge(sem, count + 2)
    eng.tensor_copy(mid, rest).then_inc(sem, 1)
    eng.wait_ge(sem, count + 3)
    eng.tensor_tensor(lo, rest, mid, ALU.subtract).then_inc(sem, 1)


def attention_weights(nc, tag, H, scale, w, ident, A_all, W_aug):
    with ExitStack() as ctx:
        m = Scope(nc, ctx, tag + "w")
        raw = m.sb("raw", [C, 4, H, C])
        fold = m.sb("fold", [C, 3, H, C])
        v_two = m.sb("v_two", [C, H, 2, C])
        p_a = m.ps("p_a", [C, H, C])
        p_w = m.ps("p_w", [P, H, C])
        loaded, folded, zeroed, made_a, made_w, kept = (m.sem(n) for n in
                                                ("loaded", "folded", "zeroed", "made_a", "made_w", "kept"))
        bias = m.sb("bias", [C, 3]) if w["bq"] is not None else None
        block = ctx.enter_context(nc.Block())
        n_loads = 4 + (3 if bias is not None else 0)

        @block.sync
        def _(sp):
            for n, key in enumerate(("q", "k", "v", "o")):
                sp.dma_start(raw[:, n], w[key]).then_inc(loaded, 16)
            if bias is not None:
                for n, key in enumerate(("bq", "bk", "bv")):
                    sp.dma_start(bias[:, n:n + 1], w[key]).then_inc(loaded, 16)

        @block.gpsimd
        def _(pool):
            nc.gpsimd.memset(W_aug[:], 0.0).then_inc(zeroed, 1)
            pool.wait_ge(zeroed, 1)
            nc.gpsimd.memset(W_aug[0:1, :, 0, C:C + 1], 1.0).then_inc(zeroed, 1)
            nc.gpsimd.memset(W_aug[C:C + 1, :, 1, C:C + 1], 1.0).then_inc(zeroed, 1)

        @block.vector
        def _(dve):
            dve.wait_ge(loaded, 16 * n_loads)
            nc.vector.tensor_tensor(fold[:, 0:3], raw[:, 0:3], raw[:, 0:3, :, 0:1].broadcast_to([C, 3, H, C]),
                                    ALU.subtract).then_inc(folded, 1)
            dve.wait_ge(folded, 1)
            n = 1
            if bias is not None:
                nc.vector.tensor_copy(fold[:, 0:3, 0, 0], bias[:, :]).then_inc(folded, 1)
                n = 2
                dve.wait_ge(folded, 2)
            nc.vector.tensor_copy(v_two[:], fold[:, 2].unsqueeze(2).broadcast_to([C, H, 2, C])).then_inc(folded, 3 - n)
            dve.wait_ge(made_a, 1)
            nc.vector.tensor_scalar(A_all[:], p_a[:], scale, None, ALU.mult).then_inc(kept, 1)
            dve.wait_ge(made_w, 1)
            dve.wait_ge(zeroed, 3)
            nc.vector.tensor_copy(W_aug[0:C, :, 0, 0:C], p_w[0:C]).then_inc(kept, 1)
            nc.vector.tensor_copy(W_aug[C:P, :, 1, 0:C], p_w[C:P]).then_inc(kept, 1)
            dve.wait_ge(kept, 3)

        @block.tensor
        def _(pe):
            pe.wait_ge(folded, 3)
            for h in range(H):
                mm = nc.tensor.matmul(p_a[:, h, :], fold[:, 0, h, :], fold[:, 1, h, :], start=True, stop=True)
            mm.then_inc(made_a, 1)
            for h in range(H):
                mm = nc.tensor.matmul(p_w[:, h, :], v_two[:, h].rearrange("p e c -> p (e c)"), raw[:, 3, h, :], start=True, stop=True)
            mm.then_inc(made_w, 1)


def normalise(nc, tag, x, out, rms=False, weight_row=None, bias_row=None, one=False):
    HT = NT // 2
    with ExitStack() as ctx:
        m = Scope(nc, ctx, tag)
        sq = m.sb("sq", [P, NT, C])
        mean, ssq, std = (m.sb(n, [P, NT]) for n in ("mean", "ssq", "std"))
        eps = m.sb("eps", [P, 1])
        row = m.sb("row", [P, C]) if weight_row is not None or bias_row is not None else None
        ready, loaded = m.sem("ready"), m.sem("loaded")
        step = m.sem("step")
        squared = m.sem("squared")
        rooted = m.sem("rooted")
        block = ctx.enter_context(nc.Block())
        names = [] if rms else ["sum0", "sum1", "mean0", "mean1", "cen0", "cen1"]
        names += ["ssq0", "ssq1", "rstd0", "rstd1", "out0", "out1"]
        at = {n: k + 1 for k, n in enumerate(names)}
        of = lambda v, h: v[:, h * HT:(h + 1) * HT]
        along = lambda v: v.unsqueeze(2).broadcast_to([P, HT, C])
        on = lambda n: row[:].unsqueeze(1).broadcast_to([P, n, C])

        @block.sync
        def _(sp):
            if row is not None:
                src = weight_row if weight_row is not None else bias_row
                sp.dma_start(row[:], src.broadcast_to([P, C])).then_inc(loaded, 16)

        @block.vector
        def _(dve):
            if not rms:
                for h in range(2):
                    nc.vector.tensor_reduce(of(mean, h), of(x, h), AX.X, ALU.add).then_inc(step, 1)
                for h in range(2):
                    dve.wait_ge(step, at[f"sum{h}"])
                    nc.vector.tensor_scalar(of(mean, h), of(mean, h), 1.0 / C, None, ALU.mult).then_inc(step, 1)
                for h in range(2):
                    dve.wait_ge(step, at[f"mean{h}"])
                    nc.vector.tensor_tensor(of(out, h), of(x, h), along(of(mean, h)), ALU.subtract).then_inc(step, 1)
            if bias_row is not None:
                dve.wait_ge(loaded, 16)
                dve.wait_ge(step, at["cen1"])
                nc.vector.tensor_tensor(x[:], x[:], on(NT), ALU.add)
            for h in range(2):
                dve.wait_ge(squared, h + 1)
                nc.vector.tensor_reduce(of(ssq, h), of(sq, h), AX.X, ALU.add).then_inc(step, 1)
            for h in range(2):
                dve.wait_ge(rooted, h + 1)
                nc.vector.reciprocal(of(std, h), of(std, h)).then_inc(step, 1)
            for h in range(2):
                dve.wait_ge(step, at[f"rstd{h}"])
                a = x if rms else out
                b = sq if weight_row is not None else out
                nc.vector.tensor_tensor(of(b, h), of(a, h), along(of(std, h)), ALU.mult).then_inc(step, 1)
            dve.wait_ge(step, at["out1"])
            if weight_row is not None:
                dve.wait_ge(loaded, 16)
                nc.vector.tensor_tensor(out[:], sq[:], on(NT), ALU.mult)

        @block.scalar
        def _(act):
            act.wait_ge(ready, 1)
            for h in range(2):
                if not rms:
                    act.wait_ge(step, at[f"cen{h}"])
                nc.scalar.activation(of(sq, h), of(x if rms else out, h), ACT.Square).then_inc(squared, 1)
            for h in range(2):
                act.wait_ge(step, at[f"ssq{h}"])
                nc.scalar.activation(of(std, h), of(ssq, h), ACT.Sqrt, bias=eps[:], scale=1.0 / C).then_inc(rooted, 1)

        @block.gpsimd
        def _(pool):
            nc.gpsimd.memset(eps[:], EPS_RMS if rms else EPS).then_inc(ready, 1)
            if one:
                pool.wait_ge(step, at["out1"])
                nc.gpsimd.memset(out[:, :, 0:1], 1.0).then_inc(ready, 1)
                pool.wait_ge(ready, 2)


def key_parts(dve, sem, count, b, K_all, keys, rest):
    into = lambda k, a, z: K_all[a:z, k, bass.ds(b * S, S)]
    dve.tensor_tensor(rest, keys, into(0, 0, P), ALU.subtract).then_inc(sem, 1)
    dve.tensor_copy(into(2, C, P), into(0, C, P)).then_inc(sem, 1)
    wait(dve, sem, count + 2)
    dve.tensor_copy(into(1, 0, P), rest).then_inc(sem, 1)
    wait(dve, sem, count + 3)
    dve.tensor_tensor(into(2, 0, C), rest[0:C], into(1, 0, C), ALU.subtract).then_inc(sem, 1)


def channel_major(nc, tag, ident, V_all, Q_all, K_all):
    with ExitStack() as ctx:
        m = Scope(nc, ctx, tag + "n")
        xt = [m.sb(f"xt{u}", [P, T, 2, C]) for u in range(2)]
        k_rest = [m.sb(f"k_rest{u}", [P, S]) for u in range(2)]
        p_t = [m.ps(f"p_t{u}", [P, S]) for u in range(2)]
        doubled = m.counts("doubled0 doubled1")
        turned = m.counts("turned0 turned1")
        q_kept = m.counts("q_kept0 q_kept1")
        k_high = m.counts("k_high0 k_high1")
        k_parts = m.counts("k_parts0 k_parts1")
        block = ctx.enter_context(nc.Block())

        @block.scalar
        def _(act):
            def double(g, u):
                wait(act, turned[u], g)
                src = V_all[:, bass.ds((2 * g + u) * T, T), :].unsqueeze(2).broadcast_to([P, T, 2, C])
                nc.scalar.copy(xt[u][:], src).then_inc(doubled[u], 1)

            def keep(g, u):
                b = 2 * g + u
                wait(act, turned[u], g + 1)
                nc.scalar.copy(K_all[:, 0, bass.ds(b * S, S)], p_t[u][:]).then_inc(k_high[u], 1)
                nc.scalar.copy(Q_all[:, bass.ds(b * S, S)], p_t[u][0:C]).then_inc(q_kept[u], 1)

            double(0, 0)
            with act.Fori(0, B // 2 - 1) as g:
                double(g, 1)
                keep(g, 0)
                double(g + 1, 0)
                keep(g, 1)
            g = B // 2 - 1
            double(g, 1)
            keep(g, 0)
            keep(g, 1)
            for u in range(2):
                wait(act, q_kept[u], B // 2)

        @block.tensor
        def _(pe):
            with pe.Fori(0, B // 2) as g:
                for u in range(2):
                    wait(pe, doubled[u], g + 1)
                    wait(pe, q_kept[u], g)
                    wait(pe, k_parts[u], 4 * g)
                    for t in range(T):
                        mm = nc.tensor.transpose(p_t[u][:, t * P:(t + 1) * P],
                                                 xt[u][:, t].rearrange("p e c -> p (e c)"), ident[:])
                    mm.then_inc(turned[u], 1)

        @block.vector
        def _(dve):
            with dve.Fori(0, B // 2) as g:
                for u in range(2):
                    wait(dve, k_high[u], g + 1)
                    wait(dve, q_kept[u], g + 1)
                    key_parts(nc.vector, k_parts[u], 4 * g, 2 * g + u, K_all, p_t[u][:], k_rest[u][:])
            for u in range(2):
                wait(dve, k_parts[u], 4 * (B // 2))


def attention(nc, tag, H, hid, ident_bf, A_all, W_aug, V_all, Q_all, K_all, causal=None):
    N = B * H
    HS = S // 2
    chunks = [(t, e) for t in range(T) for e in range(2) if not causal or e >= t // (T // 2)]
    NC = len(chunks)
    of_tile = [[c for c, (t, e) in enumerate(chunks) if t == k] for k in range(T)]
    row_chunks = [(t, e) for t in range(T) for e in range(2) if not causal or e <= t // (T // 2)]
    NR = len(row_chunks)
    half_rows = len([r for r in row_chunks if r[0] < T // 2])
    PR = (NC + 2 + 2) // 3 * 3
    RE = 4
    less_after = (of_tile[3][-1], of_tile[6][0]) if causal else (of_tile[5][0], of_tile[7][-1])
    first_part = 6 if causal else 10
    with ExitStack() as ctx:
        m = Scope(nc, ctx, tag + "a")
        A_st = [m.sb(f"A_st{u}", [C, 2, C]) for u in range(2)]
        V_st = [m.sb(f"V_st{u}", [P, T, C]) for u in range(2)]
        q_bf = [m.sb(f"q_bf{u}", [P, S], BF16) for u in range(2)]
        q_hm = [m.sb(f"q_hm{u}", [P, S], BF16) for u in range(2)]
        q_hl = [m.sb(f"q_hl{u}", [P, S], BF16) for u in range(2)]
        q_rest = m.sb("q_rest", [P, S])
        peak = [m.sb(f"peak{u}", [P, T, 2]) for u in range(2)]
        down = m.sb("down", [P, T])
        neg = [m.sb(f"neg{u}", [P, 2, T, P], BF16) for u in range(2)]
        ex = m.sb("ex", [P, RE, HS])
        z = m.sb("z", [P, HS])
        rden = m.sb("rden", [P, 2, 2, 2])
        y = m.sb("y", [P, 2, 2, 2, C])
        p_q = m.ps("p_q", [P, S])
        p_m = [m.ps(f"p_m{r}", [P, HS]) for r in range(2)]
        p_s = [m.ps(f"p_s{r}", [P, HS]) for r in range(3)]
        p_z = m.ps("p_z", [P, HS])

        zeroed = m.sem("zeroed")
        (A_placed,
         V_placed,
         q_made,
         q_cast,
         m_made,
         m_taken,
         n_step,
         q_less,
         q_high,
         q_top,
         q_step,
         s_made,
         exp_done,
         pv_done,
         z_kept,
         y_made,
         y_read,
         r_done,
         h_done,
         ) = m.counts("A_placed V_placed q_made q_cast m_made m_taken n_step q_less q_high q_top q_step s_made "
                      "exp_done pv_done z_kept y_made y_read r_done h_done")
        block = ctx.enter_context(nc.Block())

        def slot(c):
            return (c + 1) % 3 if c < 3 else c % 3

        def first_query(c):
            t, e = chunks[c]
            return (t % (T // 2)) * P if causal and e == t // (T // 2) else 0

        def keys_seen(t, e):
            return min(max((t + 1) * P - e * HS, 0), HS) if causal else HS

        @block.gpsimd
        def _(pool):
            for u in range(2):
                nc.gpsimd.memset(q_bf[u][:], 0.0).then_inc(zeroed, 1)
                nc.gpsimd.memset(neg[u][:], 0.0).then_inc(zeroed, 1)
                nc.gpsimd.memset(peak[u][:], -3e38).then_inc(zeroed, 1)

            def place_A(i, u):
                nc.gpsimd.tensor_copy(A_st[u][:], A_all[:, bass.ds(i % H, 1), :].broadcast_to([C, 2, C])).then_inc(A_placed, 1)

            def place_V(i, u):
                nc.gpsimd.tensor_copy(V_st[u][:], V_all[:, bass.ds((i // H) * T, T), :]).then_inc(V_placed, 1)

            def top(i, u, e):
                wait(pool, q_high, 2 * i + e + 1)
                nc.gpsimd.nop(nofuse=True)
                nc.gpsimd.tensor_copy(q_hl[u][0:C, e * HS:(e + 1) * HS],
                                      q_hm[u][0:C, e * HS:(e + 1) * HS]).then_inc(q_top, 1)

            def body(i, u, more):
                if more == 2:
                    wait(pool, q_made, i + 1)
                    nc.gpsimd.nop(nofuse=True)
                    place_A(i + 2, u)
                if more >= 1:
                    top(i + 1, 1 - u, 0)
                    top(i + 1, 1 - u, 1)
                if more == 2:
                    wait(pool, pv_done, NC * (i + 1))
                    nc.gpsimd.nop(nofuse=True)
                    place_V(i + 2, u)

            for u in range(2):
                place_A(u, u)
                place_V(u, u)
            top(0, 0, 0)
            top(0, 0, 1)
            with pool.Fori(0, N // 2 - 1) as g:
                body(g * 2, 0, 2)
                body(g * 2 + 1, 1, 2)
            body(N - 2, 0, 1)
            wait(pool, A_placed, N)
            wait(pool, V_placed, N)

        @block.tensor
        def _(pe):
            pe.wait_ge(zeroed, 6)

            def project(i, u):
                wait(pe, A_placed, i + 1)
                wait(pe, q_step, 6 * i)
                for e in range(2):
                    mm = nc.tensor.matmul(p_q[:, e * HS:(e + 1) * HS], A_st[u][:].rearrange("p a c -> p (a c)"),
                                          Q_all[:, bass.ds((i // H) * S + e * HS, HS)], start=True, stop=True)
                mm.then_inc(q_made, 1)

            def rows(i, u, k):
                t, e = row_chunks[k]
                n = keys_seen(t, e)
                diagonal = causal and e == t // (T // 2)
                if k == 0:
                    wait(pe, q_cast, i + 1)
                wait(pe, m_taken, NR * i + max(k - 1, 0))
                mm = nc.tensor.matmul(p_m[k % 2][:, 0:n], q_bf[u][:, t * P:(t + 1) * P],
                                      K_all[:, 0, bass.ds((i // H) * S + e * HS, n)], start=True, stop=not diagonal)
                if diagonal:
                    mm = nc.tensor.matmul(p_m[k % 2][:, n - P:n], ident_bf[:], causal[0], start=False, stop=True)
                mm.then_inc(m_made, 1)

            def subtract(i, u, e):
                wait(pe, n_step, 6 * i + 3 * e + 3)
                for t in range(T // 2 * e, T // 2 * (e + 1)):
                    for k in range(2):
                        mm = nc.tensor.matmul(p_q[:, t * P:(t + 1) * P], neg[u][:, k, t, :], ident_bf[:],
                                              start=False, stop=True, skip_group_check=True)
                mm.then_inc(q_less, 1)

            def score(i, u, c, fresh=False):
                t, e = chunks[c]
                s0 = first_query(c)
                diagonal = causal and e == t // (T // 2)
                if c < 3:
                    if not fresh:
                        wait(pe, exp_done, NC * i + (min(PR - 4 + c, NC) - NC))
                elif c == 3:
                    wait(pe, exp_done, NC * i + 3)
                elif c in (4, 5):
                    wait(pe, y_read, 2 * i)
                else:
                    wait(pe, exp_done, NC * i + c - 2)
                if c < 2:
                    wait(pe, q_top, 2 * i + c + 1)
                    wait(pe, q_step, 6 * i + 3 * c + 3)
                for k, q in enumerate((q_hm[u], q_hm[u], q_hl[u])):
                    mm = nc.tensor.matmul(p_s[slot(c)][:, s0:HS], K_all[:, k, bass.ds((i // H) * S + t * P, P)],
                                          q[:, e * HS + s0:(e + 1) * HS], start=(k == 0), stop=(k == 2 and not diagonal))
                if diagonal:
                    mm = nc.tensor.matmul(p_s[slot(c)][:, s0:s0 + P], ident_bf[:], causal[1],
                                          start=False, stop=True)
                mm.then_inc(s_made, 1)

            def total(i, u, t):
                wait(pe, exp_done, NC * i + of_tile[t][-1] + 1)
                if t == 0:
                    wait(pe, V_placed, i + 1)
                    wait(pe, z_kept, i)
                for c in of_tile[t]:
                    e, s0 = chunks[c][1], first_query(c)
                    last = c == max(k for k in range(NC) if chunks[k][1] == e)
                    nc.tensor.matmul(p_z[e * C:(e + 1) * C, s0:HS], V_st[u][:, t, :], ex[:, c % RE, s0:HS],
                                     start=(t == 0), stop=last).then_inc(pv_done, 1)

            def output(i, more):
                wait(pe, z_kept, i + 1)
                wait(pe, exp_done, NC * i + NC + (2 if more else 0))
                for k in range(2):
                    for j in range(2):
                        mm = nc.tensor.matmul(p_s[k + 1][:, j * 2 * (C + 1):(j + 1) * 2 * (C + 1)],
                                              z[:, (2 * k + j) * P:(2 * k + j + 1) * P],
                                              W_aug[:, bass.ds(i % H, 1), :, :].rearrange("p a e c -> p (a e c)"),
                                              start=True, stop=True)
                    mm.then_inc(y_made, 1)

            per_tile = 4 if causal else 3

            def body(i, u, more):
                n = 1 - u
                left = list(range(NR)) if more else []

                def rows_now(k):
                    for _ in range(min(k, len(left))):
                        rows(i + 1, n, left.pop(0))

                total(i, u, 0)
                rows_now(1)
                score(i, u, 3)
                for t in range(1, T):
                    quota = per_tile if t <= 5 else 0
                    for c in of_tile[t + 1] if t < T - 1 else []:
                        score(i, u, c)
                        if more and c in less_after:
                            subtract(i + 1, n, less_after.index(c))
                        rows_now(min(quota, 1))
                        quota -= min(quota, 1)
                    total(i, u, t)
                    rows_now(quota)
                assert not left
                if more:
                    for c in range(3):
                        score(i + 1, n, c)
                if more == 2:
                    project(i + 2, u)
                output(i, more)

            project(0, 0)
            for k in range(NR):
                rows(0, 0, k)
            subtract(0, 0, 0)
            subtract(0, 0, 1)
            for c in range(3):
                score(0, 0, c, fresh=True)
            project(1, 1)
            with pe.Fori(0, N // 2 - 1) as g:
                body(g * 2, 0, 2)
                body(g * 2 + 1, 1, 2)
            body(N - 2, 0, 1)
            body(N - 1, 1, 0)

        @block.scalar
        def _(act):
            act.wait_ge(zeroed, 6)

            def cast(i, u):
                wait(act, q_made, i + 1)
                nc.scalar.copy(q_bf[u][0:C, :], p_q[0:C, :]).then_inc(q_cast, 1)

            def high(i, u, e):
                wait(act, q_less, 2 * i + e + 1)
                nc.scalar.copy(q_hm[u][:, e * HS:(e + 1) * HS], p_q[:, e * HS:(e + 1) * HS]).then_inc(q_high, 1)

            def body(i, u, more):
                for c in range(NC):
                    wait(act, s_made, NC * i + c + 1)
                    wait(act, pv_done, NC * i + max(c - RE + 1, 0))
                    s0 = first_query(c)
                    nc.scalar.activation(ex[:, c % RE, s0:HS], p_s[slot(c)][:, s0:HS], ACT.Exp).then_inc(exp_done, 1)
                    if more and c == 2:
                        cast(i + 1, 1 - u)
                    if more and c in less_after:
                        high(i + 1, 1 - u, less_after.index(c))

            cast(0, 0)
            high(0, 0, 0)
            high(0, 0, 1)
            with act.Fori(0, N // 2 - 1) as g:
                body(g * 2, 0, 2)
                body(g * 2 + 1, 1, 2)
            body(N - 2, 0, 1)
            body(N - 1, 1, 0)

        @block.vector
        def _(dve):
            dve.wait_ge(zeroed, 6)

            def maxima(i, u, k):
                t, e = row_chunks[k]
                wait(dve, m_made, NR * i + k + 1)
                nc.vector.tensor_reduce(peak[u][:, t, e:e + 1], p_m[k % 2][:, 0:keys_seen(t, e)], AX.X,
                                        ALU.max).then_inc(m_taken, 1)

            def negate(i, u, e):
                a, b = T // 2 * e, T // 2 * (e + 1)
                two = lambda v: v[:, a:b].unsqueeze(2).broadcast_to([P, T // 2, 2])
                at = lambda k: neg[u][:, k, a:b, :].rearrange("p t (e c) -> p t e c", e=2)[:, :, :, 0]
                wait(dve, m_taken, NR * i + (half_rows if e == 0 else NR))
                wait(dve, n_step, 6 * i + 3 * e)
                nc.vector.tensor_reduce(down[:, a:b], peak[u][:, a:b, :], AX.X, ALU.max, negate=True).then_inc(n_step, 1)
                wait(dve, n_step, 6 * i + 3 * e + 1)
                nc.vector.tensor_copy(at(0), two(down)).then_inc(n_step, 1)
                wait(dve, n_step, 6 * i + 3 * e + 2)
                nc.vector.tensor_tensor(at(1), two(down), at(0), ALU.subtract).then_inc(n_step, 1)

            def part(i, u, e, n):
                h = slice(e * HS, (e + 1) * HS)
                k = 6 * i + 3 * e
                if n == 0:
                    wait(dve, q_high, 2 * i + e + 1)
                    wait(dve, q_top, 2 * i)
                wait(dve, q_step, k + n)
                if n == 0:
                    op = nc.vector.tensor_tensor(q_rest[C:P, h], p_q[C:P, h], q_hm[u][C:P, h], ALU.subtract)
                elif n == 1:
                    op = nc.vector.tensor_copy(q_hm[u][C:P, h], q_rest[C:P, h])
                else:
                    op = nc.vector.tensor_tensor(q_hl[u][C:P, h], q_rest[C:P, h], q_hm[u][C:P, h], ALU.subtract)
                op.then_inc(q_step, 1)

            def finish(i):
                wait(dve, pv_done, NC * (i + 1))
                wait(dve, y_made, 2 * i)
                nc.vector.tensor_copy(z[:], p_z[:]).then_inc(z_kept, 1)
                x = hid[:, bass.ds((i // H) * T, T), :].rearrange("p (e t) c -> p e t c", e=2)
                for k in range(2):
                    wait(dve, y_made, 2 * i + k + 1)
                    p = p_s[k + 1][:, 0:4 * (C + 1)].rearrange("p (j e c) -> p e j c", j=2, e=2)
                    nc.vector.reciprocal(rden[:, k], p[:, :, :, C]).then_inc(r_done, 1)
                    wait(dve, r_done, 2 * i + k + 1)
                    nc.vector.tensor_tensor(y[:, k], p[:, :, :, 0:C],
                                            rden[:, k].unsqueeze(3).broadcast_to([P, 2, 2, C]),
                                            ALU.mult).then_inc(y_read, 1)
                wait(dve, y_read, 2 * i + 2)
                wait(dve, h_done, 2 * i)
                for k in range(2):
                    out = x[:, :, 2 * k:2 * k + 2, :]
                    nc.vector.tensor_tensor(out, out, y[:, k], ALU.add).then_inc(h_done, 1)

            def queries(i, u):
                for k in range(NR):
                    maxima(i, u, k)
                    if k == half_rows:
                        negate(i, u, 0)
                    if first_part <= k < first_part + 3:
                        part(i, u, 0, k - first_part)
                negate(i, u, 1)
                for n in range(3):
                    part(i, u, 1, n)

            for k in range(NR):
                maxima(0, 0, k)
            for e in range(2):
                negate(0, 0, e)
            for e in range(2):
                for n in range(3):
                    part(0, 0, e, n)
            with dve.Fori(0, N // 2 - 1) as g:
                for u in range(2):
                    queries(g * 2 + (u + 1), 1 - u)
                    finish(g * 2 + u)
            queries(N - 1, 1)
            finish(N - 2)
            finish(N - 1)
            wait(dve, h_done, 2 * N)


def rotary_heads(nc, tag, xs, ident, ident_bf, norm_row, wqkv, rope, V_all, Q_all, K_all):
    with ExitStack() as ctx:
        m = Scope(nc, ctx, tag + "r")
        sq, xr, xn, rest = (m.sb(n, [P, T, C]) for n in ("sq", "xr", "xn", "rest"))
        ssq, std, rstd = (m.sb(n, [P, T]) for n in ("ssq", "std", "rstd"))
        eps = m.sb("eps", [P, 1])
        w_n = m.sb("w_n", [P, C])
        x_p = [m.sb(f"x_p{k}", [P, T, P], BF16) for k in range(2)]
        x_T = [m.sb(f"x_T{k}", [P, S], BF16) for k in range(2)]
        w_raw, w_rest = m.sb("w_raw", [P, P]), m.sb("w_rest", [P, P])
        w_s = m.sb("w_s", [P, 3, P], BF16)
        w_lo = m.sb("w_lo", [P, P], BF16)
        tab = m.sb("tab", [P, 2, T, 16])
        qkv = m.sb("qkv", [P, T, P])
        t_cos, t_sin = m.sb("t_cos", [P, T, 96]), m.sb("t_sin", [P, T, 96])
        q_n, k_n = m.sb("q_n", [P, T, P]), m.sb("k_n", [P, T, P])
        k_rest = m.sb("k_rest", [P, S])
        p_x = [m.ps(f"p_x{k}", [P, S], BF16) for k in range(2)]
        p_p = m.ps("p_p", [P, T, P])
        p_q = m.ps("p_q", [P, S])
        p_k = m.ps("p_k", [P, S])
        ready, loaded, w_split = m.sem("ready"), m.sem("loaded"), m.sem("w_split")
        (step,
         rooted,
         x_turned,
         x_kept,
         projected,
         p_kept,
         v_kept,
         qk_turned,
         q_kept, k_kept,
         ) = m.counts("step rooted x_turned x_kept projected p_kept v_kept qk_turned q_kept k_kept")
        block = ctx.enter_context(nc.Block())
        names = ["sq", "ssq", "rstd", "xr", "xn", "x_hi", "x_rest", "x_mid", "x_lo", "x_hi2", "cos", "sin0", "sin1", "q", "k0", "k"]
        at = {n: k + 1 for k, n in enumerate(names)}
        NV = len(names)

        @block.sync
        def _(sp):
            for h in range(2):
                sp.dma_start(w_raw[h * C:(h + 1) * C], wqkv).then_inc(loaded, 16)
            sp.dma_start(w_n[:], norm_row.broadcast_to([P, C])).then_inc(loaded, 16)
            sp.dma_start(tab[:], rope).then_inc(loaded, 16)

        @block.gpsimd
        def _(pool):
            nc.gpsimd.memset(eps[:], EPS_RMS).then_inc(ready, 1)
            nc.gpsimd.memset(q_n[:], 0.0).then_inc(ready, 1)
            nc.gpsimd.memset(k_n[:], 0.0).then_inc(ready, 1)
            nc.gpsimd.memset(V_all[:], 0.0).then_inc(ready, 1)
            pool.wait_ge(ready, 4)
            for e in range(2):
                nc.gpsimd.memset(k_n[:, :, e * C:e * C + 1], 1.0).then_inc(ready, 1)
            nc.gpsimd.memset(V_all[:, :, 0:1], 1.0).then_inc(ready, 1)

        @block.vector
        def _(dve):
            dve.wait_ge(ready, 7)
            dve.wait_ge(loaded, 64)
            split(nc.vector, w_split, 0, w_s[:, 0], w_s[:, 1], w_lo[:], w_raw[:], w_rest[:])
            dve.wait_ge(w_split, 4)
            nc.vector.tensor_copy(w_s[0:C, 2], w_lo[0:C]).then_inc(w_split, 1)
            nc.vector.tensor_copy(w_s[C:P, 2], w_s[C:P, 0]).then_inc(w_split, 1)
            with dve.Fori(0, B) as b:
                def after(name):
                    wait(dve, step, b * NV + at[name])

                x = xs[:, bass.ds(b * T, T), :]
                nc.vector.tensor_tensor(sq[:], x, x, ALU.mult).then_inc(step, 1)
                after("sq")
                nc.vector.tensor_reduce(ssq[:], sq[:], AX.X, ALU.add).then_inc(step, 1)
                wait(dve, rooted, b + 1)
                nc.vector.reciprocal(rstd[:], std[:]).then_inc(step, 1)
                after("rstd")
                nc.vector.tensor_tensor(xr[:], x, rstd[:].unsqueeze(2).broadcast_to([P, T, C]), ALU.mult).then_inc(step, 1)
                after("xr")
                nc.vector.tensor_tensor(xn[:], xr[:], w_n[:].unsqueeze(1).broadcast_to([P, T, C]), ALU.mult).then_inc(step, 1)
                after("xn")
                wait(dve, x_turned, b)
                split(nc.vector, step, b * NV + at["xn"] + 1, x_p[0][:, :, 0:C], x_p[0][:, :, C:P], x_p[1][:, :, C:P],
                      xn[:], rest[:])
                nc.vector.tensor_copy(x_p[1][:, :, 0:C], x_p[0][:, :, 0:C]).then_inc(step, 1)
                wait(dve, p_kept, b + 1)
                of = qkv[:, :, 0:96].rearrange("p t (h d) -> p t h d", d=16)
                cs = lambda k, lo, hi: tab[:, k, :, lo:hi].unsqueeze(2).broadcast_to([P, T, 6, hi - lo])
                tc, ts = (v[:].rearrange("p t (h d) -> p t h d", d=16) for v in (t_cos, t_sin))
                nc.vector.tensor_tensor(tc, of, cs(0, 0, 16), ALU.mult).then_inc(step, 1)
                nc.vector.tensor_tensor(ts[:, :, :, 0:8], of[:, :, :, 8:16], cs(1, 0, 8), ALU.mult).then_inc(step, 1)
                nc.vector.tensor_tensor(ts[:, :, :, 8:16], of[:, :, :, 0:8], cs(1, 8, 16), ALU.mult).then_inc(step, 1)
                after("sin1")
                wait(dve, qk_turned, b)
                nc.vector.tensor_tensor(q_n[:, :, 0:C], t_cos[:, :, 0:C], t_sin[:, :, 0:C], ALU.add).then_inc(step, 1)
                two = lambda v: v[:, :, C:96].rearrange("p t (g d) -> p t g d", g=2)
                for e in range(2):
                    nc.vector.tensor_tensor(
                        k_n[:, :, e * C:(e + 1) * C].rearrange("p t (g d) -> p t g d", g=2)[:, :, :, 1:17],
                        two(t_cos), two(t_sin), ALU.add).then_inc(step, 1)
                wait(dve, qk_turned, b + 1)
                nc.vector.tensor_copy(K_all[:, 0, bass.ds(b * S, S)], p_k[:]).then_inc(k_kept, 1)
                wait(dve, k_kept, 5 * b + 1)
                key_parts(nc.vector, k_kept, 5 * b + 1, b, K_all, p_k[:], k_rest[:])
            wait(dve, k_kept, 5 * B)

        @block.scalar
        def _(act):
            act.wait_ge(ready, 7)
            with act.Fori(0, B) as b:
                wait(act, step, b * NV + at["ssq"])
                nc.scalar.activation(std[:], ssq[:], ACT.Sqrt, bias=eps[:], scale=1.0 / C).then_inc(rooted, 1)
                wait(act, x_turned, b + 1)
                wait(act, projected, b)
                for k in range(2):
                    nc.scalar.copy(x_T[k][:], p_x[k][:]).then_inc(x_kept, 1)
                wait(act, projected, b + 1)
                wait(act, step, b * NV)
                wait(act, v_kept, b)
                nc.scalar.copy(qkv[:], p_p[:]).then_inc(p_kept, 1)
                wait(act, p_kept, b + 1)
                nc.scalar.copy(V_all[:, bass.ds(b * T, T), 1:33], qkv[:, :, 96:P]).then_inc(v_kept, 1)
                wait(act, qk_turned, b + 1)
                nc.scalar.copy(Q_all[:, bass.ds(b * S, S)], p_q[0:C]).then_inc(q_kept, 1)
            wait(act, q_kept, B)
            wait(act, v_kept, B)

        @block.tensor
        def _(pe):
            pe.wait_ge(w_split, 6)
            with pe.Fori(0, B) as b:
                wait(pe, step, b * NV + at["x_hi2"])
                wait(pe, x_kept, 2 * b)
                for k in range(2):
                    for t in range(T):
                        mm = nc.tensor.transpose(p_x[k][:, t * P:(t + 1) * P], x_p[k][:, t, :], ident_bf[:])
                mm.then_inc(x_turned, 1)
                wait(pe, x_kept, 2 * b + 2)
                wait(pe, p_kept, b)
                for t in range(T):
                    for q in range(3):
                        mm = nc.tensor.matmul(p_p[:, t, :], x_T[q // 2][:, t * P:(t + 1) * P], w_s[:, q],
                                              start=(q == 0), stop=(q == 2))
                mm.then_inc(projected, 1)
                wait(pe, step, b * NV + at["k"])
                wait(pe, q_kept, b)
                wait(pe, k_kept, 5 * b)
                for t in range(T):
                    nc.tensor.transpose(p_q[:, t * P:(t + 1) * P], q_n[:, t, :], ident[:])
                    mm = nc.tensor.transpose(p_k[:, t * P:(t + 1) * P], k_n[:, t, :], ident[:])
                mm.then_inc(qk_turned, 1)


def sampling_points(nc, tag, d, ident_bf, Q_all, I_all, F_all):
    G = 16
    N = C + G
    with ExitStack() as ctx:
        m = Scope(nc, ctx, tag + "s")
        patch = [m.sb(f"patch{u}", [P, T, 4, C]) for u in range(2)]
        f_ref = m.sb("f_ref", [P, T, 4])
        ref = m.sb("ref", [P, T, 2])
        half = m.sb("half", [P, T, 2, C])
        feat, rest = m.sb("feat", [P, T, C]), m.sb("rest", [P, T, C])
        x_p = [m.sb(f"x_p{k}", [P, T, P], BF16) for k in range(2)]
        x_T = [m.sb(f"x_T{k}", [P, S], BF16) for k in range(2)]
        w_raw, w_rest = m.sb("w_raw", [P, N]), m.sb("w_rest", [P, N])
        w_s, w_lo = m.sb("w_s", [P, 3, N], BF16), m.sb("w_lo", [P, N], BF16)
        o_raw, o_rest, o_sum = m.sb("o_raw", [P, G]), m.sb("o_rest", [P, G]), m.sb("o_sum", [P, 3, G])
        o_p = m.sb("o_p", [P, 3, G], BF16)
        o_s = m.sb("o_s", [P, G], BF16)
        o_rows = m.sb("o_rows", [P, 3])
        rows = m.sb("rows", [P, 4, G])
        o = m.sb("o", [P, T, G])
        cen, sq, lin = (m.sb(n, [P, T, G]) for n in ("cen", "sq", "lin"))
        mean, ssq, std, rstd = (m.sb(n, [P, T]) for n in ("mean", "ssq", "std", "rstd"))
        h, h_rest = m.sb("h", [P, T, G]), m.sb("h_rest", [P, T, G])
        h_p = m.sb("h_p", [P, T, P], BF16)
        h_T = m.sb("h_T", [P, S], BF16)
        eps = m.sb("eps", [P, 1])
        xy, lo, up, fr, om = (m.sb(n, [P, T, 8, 2]) for n in ("xy", "lo", "up", "fr", "om"))
        whole = m.sb("whole", [P, T, 8, 2], I32)
        row = m.sb("row", [P, T, 8])
        base = m.sb("base", [P, 1])
        p_x = [m.ps(f"p_x{k}", [P, S], BF16) for k in range(2)]
        p_p = m.ps("p_p", [P, T, P])
        p_h = m.ps("p_h", [P, S], BF16)
        p_o = m.ps("p_o", [P, T, G])
        ready, loaded, split_w, split_o = (m.sem(n) for n in ("ready", "loaded", "split_w", "split_o"))
        patch_in = [m.sem(f"patch_in{u}") for u in range(2)]
        (step,
         rooted, bent,
         x_turned, x_kept, projected, p_kept, o_kept, h_turned, h_kept, offset,
         ) = m.counts("step rooted bent x_turned x_kept projected p_kept o_kept h_turned h_kept offset")
        patch_read = m.counts("patch_read0 patch_read1")
        block = ctx.enter_context(nc.Block())
        names = ["prod", "feat", "x_hi", "x_rest", "x_mid", "x_lo", "x_hi2",
                 "o", "sum", "mean", "cen", "sq", "ssq", "rstd", "unit", "scaled", "lin",
                 "h_hi", "h_rest", "h_mid", "h_lo", "h_hi2", "h_mid2", "h_hi3",
                 "biased", "moved", "placed", "unit2", "grown", "clipped", "whole", "back", "over",
                 "floor", "cap", "fr", "om", "row", "idx0", "idx", "f00", "f01", "f10", "f11"]
        at = {n: k + 1 for k, n in enumerate(names)}
        NV = len(names)

        @block.sync
        def _(sp):
            loads = [(w_raw[k * C:(k + 1) * C], d["w_qo"]) for k in range(2)]
            loads += [(o_raw[k * G:(k + 1) * G], d["w_o2"]) for k in range(6)]
            loads += [(rows[:, k], d[n].broadcast_to([P, G])) for k, n in enumerate(("b_o1", "ln_g", "ln_b", "b_o2"))]
            loads += [(f_ref[:], d["f_ref"]), (ref[:], d["ref"]), (o_rows[:], d["o_rows"])]
            assert len(loads) == 15
            sp.wait_ge(ready, 4)
            for dst, src in loads:
                sp.dma_start(dst, src).then_inc(loaded, 16)
            with sp.Fori(0, B // 2) as g:
                for u in range(2):
                    wait(sp, patch_read[u], g)
                    src = d["patches"][bass.ds((2 * g + u) * S, S), :].rearrange("(t p) c -> p t c", p=P)
                    sp.dma_start(patch[u][:].rearrange("p t k c -> p t (k c)"), src).then_inc(patch_in[u], 16)

        @block.gpsimd
        def _(pool):
            nc.gpsimd.memset(o_raw[:], 0.0).then_inc(ready, 1)
            nc.gpsimd.memset(h_p[:], 0.0).then_inc(ready, 1)
            nc.gpsimd.memset(eps[:], EPS).then_inc(ready, 1)
            nc.gpsimd.memset(base[:], 0.0).then_inc(ready, 1)

        @block.vector
        def _(dve):
            dve.wait_ge(ready, 4)
            dve.wait_ge(loaded, 16 * 15)
            split(nc.vector, split_w, 0, w_s[:, 0], w_s[:, 1], w_lo[:], w_raw[:], w_rest[:])
            dve.wait_ge(split_w, 4)
            nc.vector.tensor_copy(w_s[0:C, 2], w_lo[0:C]).then_inc(split_w, 1)
            nc.vector.tensor_copy(w_s[C:P, 2], w_s[C:P, 0]).then_inc(split_w, 1)
            split(nc.vector, split_o, 0, o_p[:, 0], o_p[:, 1], o_p[:, 2], o_raw[:], o_rest[:])
            dve.wait_ge(split_o, 4)
            nc.vector.tensor_tensor(o_sum[:], o_p[:], o_rows[:].unsqueeze(2).broadcast_to([P, 3, G]),
                                    ALU.mult).then_inc(split_o, 1)
            dve.wait_ge(split_o, 5)
            nc.vector.tensor_tensor(o_sum[:, 0], o_sum[:, 0], o_sum[:, 1], ALU.add).then_inc(split_o, 1)
            dve.wait_ge(split_o, 6)
            nc.vector.tensor_tensor(o_s[:], o_sum[:, 0], o_sum[:, 2], ALU.add).then_inc(split_o, 1)

            def batch(b, u, lap):
                def after(name):
                    wait(dve, step, b * NV + at[name])

                def do(name, ins):
                    ins.then_inc(step, 1)
                    assert at[name] == do.n + 1
                    do.n += 1

                do.n = 0
                on = lambda k: rows[:, k].unsqueeze(1).broadcast_to([P, T, G])
                along = lambda v, n: v[:].unsqueeze(2).broadcast_to([P, T, n])
                tt, ts = nc.vector.tensor_tensor, nc.vector.tensor_scalar
                dve.wait_ge(patch_in[u], lap * 16)
                do("prod", tt(patch[u][:], patch[u][:], f_ref[:].unsqueeze(3).broadcast_to([P, T, 4, C]), ALU.mult))
                after("prod")
                tt(half[:], patch[u][:, :, 0:2], patch[u][:, :, 2:4], ALU.add).then_inc(patch_read[u], 1)
                wait(dve, patch_read[u], lap)
                do("feat", tt(feat[:], half[:, :, 0], half[:, :, 1], ALU.add))
                after("feat")
                wait(dve, x_turned, b)
                split(nc.vector, step, b * NV + at["feat"] + 1, x_p[0][:, :, 0:C], x_p[0][:, :, C:P],
                      x_p[1][:, :, C:P], feat[:], rest[:])
                nc.vector.tensor_copy(x_p[1][:, :, 0:C], x_p[0][:, :, 0:C]).then_inc(step, 1)
                do.n += 5
                wait(dve, p_kept, b + 1)
                do("o", tt(o[:], lin[:], on(0), ALU.add))
                after("o")
                do("sum", nc.vector.tensor_reduce(mean[:], o[:], AX.X, ALU.add))
                after("sum")
                do("mean", ts(mean[:], mean[:], 1.0 / G, None, ALU.mult))
                after("mean")
                do("cen", tt(cen[:], o[:], along(mean, G), ALU.subtract))
                after("cen")
                do("sq", tt(sq[:], cen[:], cen[:], ALU.mult))
                after("sq")
                do("ssq", nc.vector.tensor_reduce(ssq[:], sq[:], AX.X, ALU.add))
                wait(dve, rooted, b + 1)
                do("rstd", nc.vector.reciprocal(rstd[:], std[:]))
                after("rstd")
                do("unit", tt(o[:], cen[:], along(rstd, G), ALU.mult))
                after("unit")
                do("scaled", tt(sq[:], o[:], on(1), ALU.mult))
                after("scaled")
                do("lin", tt(cen[:], sq[:], on(2), ALU.add))
                wait(dve, bent, b + 1)
                wait(dve, h_turned, b)
                g = lambda k: h_p[:, :, k * G:(k + 1) * G]
                split(nc.vector, step, b * NV + at["lin"] + 1, g(0), g(1), g(2), h[:], h_rest[:])
                for k, s in ((3, 0), (4, 1), (5, 0)):
                    nc.vector.tensor_copy(g(k), g(s)).then_inc(step, 1)
                do.n += 7
                wait(dve, offset, b + 1)
                flat = lambda v: v[:].rearrange("p t n k -> p t (n k)")
                do("biased", tt(flat(xy), p_o[:], on(3), ALU.add))
                after("biased")
                do("moved", ts(xy[:], xy[:], OFFSET_SCALE, 2.0 / (WD - 1), ALU.mult, ALU.mult))
                after("moved")
                do("placed", tt(xy[:], xy[:], ref[:].unsqueeze(2).broadcast_to([P, T, 8, 2]), ALU.add))
                after("placed")
                do("unit2", ts(xy[:], xy[:], 1.0, 0.5, ALU.add, ALU.mult))
                after("unit2")
                do("grown", ts(xy[:], xy[:], float(WD - 1), 0.0, ALU.mult, ALU.max))
                after("grown")
                do("clipped", ts(xy[:], xy[:], float(WD - 1), None, ALU.min))
                after("clipped")
                do("whole", nc.vector.tensor_copy(whole[:], xy[:]))
                after("whole")
                do("back", nc.vector.tensor_copy(lo[:], whole[:]))
                after("back")
                do("over", tt(up[:], lo[:], xy[:], ALU.is_gt))
                after("over")
                do("floor", tt(lo[:], lo[:], up[:], ALU.subtract))
                after("floor")
                do("cap", ts(lo[:], lo[:], float(WD - 2), None, ALU.min))
                after("cap")
                do("fr", tt(fr[:], xy[:], lo[:], ALU.subtract))
                after("fr")
                do("om", ts(om[:], fr[:], -1.0, 1.0, ALU.mult, ALU.add))
                do("row", ts(row[:], lo[:, :, :, 1], float(WD), base[:, 0:1], ALU.mult, ALU.add))
                after("row")
                do("idx0", tt(row[:], row[:], lo[:, :, :, 0], ALU.add))
                after("idx0")
                do("idx", nc.vector.tensor_copy(I_all[:, bass.ds(b * T, T), :], row[:]))
                nc.vector.tensor_scalar(base[:], base[:], float((WD - 1) * WD), None, ALU.add)
                out = F_all[:, bass.ds(b * T, T), :, :]
                for n, (fx, fy) in enumerate(((om, om), (om, fr), (fr, om), (fr, fr))):
                    do(f"f{n // 2}{n % 2}", tt(out[:, :, :, n], fx[:, :, :, 0], fy[:, :, :, 1], ALU.mult))
                after("f11")

            with dve.Fori(0, B // 2) as g:
                for u in range(2):
                    batch(2 * g + u, u, g + 1)

        @block.scalar
        def _(act):
            act.wait_ge(ready, 4)
            with act.Fori(0, B) as b:
                wait(act, x_turned, b + 1)
                wait(act, projected, b)
                for k in range(2):
                    nc.scalar.copy(x_T[k][:], p_x[k][:]).then_inc(x_kept, 1)
                wait(act, projected, b + 1)
                nc.scalar.copy(lin[:], p_p[:, :, C:N]).then_inc(p_kept, 1)
                nc.scalar.copy(Q_all[:, bass.ds(b * T, T), :], p_p[:, :, 0:C]).then_inc(o_kept, 1)
                wait(act, step, b * NV + at["ssq"])
                nc.scalar.activation(std[:], ssq[:], ACT.Sqrt, bias=eps[:], scale=1.0 / G).then_inc(rooted, 1)
                wait(act, step, b * NV + at["lin"])
                nc.scalar.activation(h[:], cen[:], ACT.Gelu_apprx_tanh).then_inc(bent, 1)
                wait(act, h_turned, b + 1)
                wait(act, offset, b)
                nc.scalar.copy(h_T[:], p_h[:]).then_inc(h_kept, 1)
            wait(act, o_kept, B)

        @block.tensor
        def _(pe):
            pe.wait_ge(split_w, 6)
            pe.wait_ge(split_o, 7)
            with pe.Fori(0, B) as b:
                wait(pe, step, b * NV + at["x_hi2"])
                wait(pe, x_kept, 2 * b)
                for k in range(2):
                    for t in range(T):
                        mm = nc.tensor.transpose(p_x[k][:, t * P:(t + 1) * P], x_p[k][:, t, :], ident_bf[:])
                mm.then_inc(x_turned, 1)
                wait(pe, x_kept, 2 * b + 2)
                wait(pe, o_kept, b)
                for t in range(T):
                    for q in range(3):
                        mm = nc.tensor.matmul(p_p[:, t, 0:N], x_T[q // 2][:, t * P:(t + 1) * P], w_s[:, q],
                                              start=(q == 0), stop=(q == 2))
                mm.then_inc(projected, 1)
                wait(pe, step, b * NV + at["h_hi3"])
                wait(pe, h_kept, b)
                for t in range(T):
                    mm = nc.tensor.transpose(p_h[:, t * P:(t + 1) * P], h_p[:, t, :], ident_bf[:])
                mm.then_inc(h_turned, 1)
                wait(pe, h_kept, b + 1)
                for t in range(T):
                    mm = nc.tensor.matmul(p_o[:, t, :], h_T[:, t * P:(t + 1) * P], o_s[:], start=True, stop=True)
                mm.then_inc(offset, 1)


def deformable_attention(nc, tag, d, ident, Q_all, I_all, F_all, hid, fetched):
    U = 4
    R = len(fetched)
    NP = 8
    with ExitStack() as ctx:
        m = Scope(nc, ctx, tag + "d")
        patch = [m.sb(f"patch{r}", [P, NP, 4 * C]) for r in range(R)]
        rows = [m.sb(f"rows{r}", [P, NP], I32) for r in range(R)]
        half = m.sb("half", [P, NP, 2 * C])
        point = [m.sb(f"point{r}", [P, NP, C]) for r in range(2)]
        p_sb = [m.sb(f"p_sb{r}", [P, NP // 2, P]) for r in range(2)]
        w_kv = m.sb("w_kv", [P, 2, 2 * C])
        prod = m.sb("prod", [P, NP, C])
        score = m.sb("score", [P, U, NP, NP])
        top, tot = m.sb("top", [P, U, NP]), m.sb("tot", [P, U, NP])
        shifted, ex, attn = (m.sb(n, [P, U, NP, NP]) for n in ("shifted", "ex", "attn"))
        val = [m.sb(f"val{k}", [P, NP, C]) for k in range(U)]
        p_t = [m.ps(f"p_t{r}", [P, NP // 2, P]) for r in range(2)]
        p_kv = [m.ps(f"p_kv{r}", [P, NP, 2 * C]) for r in range(2)]
        ready, loaded = m.sem("ready"), m.sem("loaded")
        (step,
         rows_set, turned, t_kept, projected, v_kept, raised,
         ) = m.counts("step rows_set turned t_kept projected v_kept raised")
        freed = m.counts(" ".join(f"freed{r}" for r in range(R)))
        block = ctx.enter_context(nc.Block())
        names = []
        for k in range(U):
            names += [f"prod{k}", f"point{k}"]
            if k:
                names += [f"qk{k - 1}", f"score{k - 1}"]
        names += [f"qk{U - 1}", f"score{U - 1}", "top", "shifted", "tot", "rtot", "attn"]
        for k in range(U):
            names += [f"av{k}", f"out{k}"]
        at = {n: k + 1 for k, n in enumerate(names)}
        NV = len(names)

        @block.sync
        def _(sp):
            sp.wait_ge(ready, 1)
            for e in range(2):
                sp.dma_start(w_kv[e * C:(e + 1) * C, e], d["w_kv"]).then_inc(loaded, 16)

        @block.gpsimd
        def _(pool):
            nc.gpsimd.memset(w_kv[:], 0.0).then_inc(ready, 1)
            with pool.Fori(0, NT // U) as g:
                for k in range(U):
                    wait(pool, freed[k], g)
                    nc.gpsimd.tensor_copy(rows[k][:], I_all[:, bass.ds(g * U + k, 1), :].rearrange("p a n -> p (a n)")).then_inc(rows_set, 1)
                    wait(pool, rows_set, g * U + k + 1)
                    nc.gpsimd.nop(nofuse=True)
                    for n in range(NP):
                        nc.gpsimd.indirect_dma_start(
                            out=patch[k][:, n, :], out_offset=None, in_=d["pixels"],
                            in_offset=bass.IndirectOffsetOnAxis(ap=rows[k][:, n:n + 1], axis=0),
                        ).then_inc(fetched[k], 16)

        @block.vector
        def _(dve):
            with dve.Fori(0, NT // U) as g:
                def after(name):
                    wait(dve, step, g * NV + at[name])

                def do(name, ins):
                    ins.then_inc(step, 1)
                    assert at[name] == do.n + 1, name
                    do.n += 1

                do.n = 0
                tt = nc.vector.tensor_tensor
                wait(dve, step, g * NV)

                def sample(k):
                    dve.wait_ge(fetched[k], (g + 1) * (16 * NP))
                    f = F_all[:, bass.ds(g * U + k, 1), :, :].rearrange("p a n k -> p (a n k)")
                    x = patch[k][:].rearrange("p n (k c) -> p (n k) c", c=C)
                    do(f"prod{k}", tt(x, x, f.unsqueeze(2).broadcast_to([P, 4 * NP, C]), ALU.mult))
                    after(f"prod{k}")
                    if k:
                        after(f"point{k - 1}")
                    tt(half[:], patch[k][:, :, 0:2 * C], patch[k][:, :, 2 * C:4 * C], ALU.add).then_inc(freed[k], 1)
                    wait(dve, freed[k], g + 1)
                    wait(dve, turned, g * U + max(k - 1, 0))
                    do(f"point{k}", tt(point[k % 2][:], half[:, :, 0:C], half[:, :, C:2 * C], ALU.add))

                def scores(k):
                    wait(dve, v_kept, g * U + k + 1)
                    if k:
                        after(f"score{k - 1}")
                    q = Q_all[:, bass.ds(g * U + k, 1), :].broadcast_to([P, NP, C])
                    do(f"qk{k}", tt(prod[:], p_kv[k % 2][:, :, 0:C], q, ALU.mult))
                    after(f"qk{k}")
                    do(f"score{k}", nc.vector.tensor_reduce(
                        score[:, k].rearrange("p n h -> p (n h)"),
                        prod[:].rearrange("p n (h d) -> p (n h) d", h=NP), AX.X, ALU.add))

                for k in range(U):
                    sample(k)
                    if k:
                        scores(k - 1)
                scores(U - 1)
                after(f"score{U - 1}")
                do("top", nc.vector.tensor_reduce(top[:], score[:].rearrange("p t n h -> p t h n"), AX.X, ALU.max))
                after("top")
                do("shifted", tt(shifted[:], score[:], top[:].unsqueeze(2).broadcast_to([P, U, NP, NP]), ALU.subtract))
                wait(dve, raised, g + 1)
                do("tot", nc.vector.tensor_reduce(tot[:], ex[:].rearrange("p t n h -> p t h n"), AX.X, ALU.add))
                after("tot")
                do("rtot", nc.vector.reciprocal(tot[:], tot[:]))
                after("rtot")
                do("attn", tt(attn[:], ex[:], tot[:].unsqueeze(2).broadcast_to([P, U, NP, NP]), ALU.mult))
                after("attn")
                for k in range(U):
                    v = val[k][:].rearrange("p n (h d) -> p (n h) d", h=NP)
                    do(f"av{k}", tt(v, v, attn[:, k].rearrange("p n h -> p (n h)").unsqueeze(2).broadcast_to([P, NP * NP, C // NP]),
                                    ALU.mult))
                    after(f"av{k}")
                    do(f"out{k}", nc.vector.tensor_reduce(
                        hid[:, bass.ds(g * U + k, 1), :].rearrange("p a c -> p (a c)"),
                        val[k][:].rearrange("p n c -> p c n"), AX.X, ALU.add))
            wait(dve, step, NV * (NT // U))

        @block.scalar
        def _(act):
            with act.Fori(0, NT // U) as g:
                for k in range(U):
                    i = g * U + k
                    r = k % 2
                    wait(act, turned, i + 1)
                    wait(act, projected, g * U + max(k - 1, 0))
                    nc.scalar.copy(p_sb[r][:], p_t[r][:]).then_inc(t_kept, 1)
                    wait(act, projected, i + 1)
                    if k == 0:
                        wait(act, step, g * NV)
                    nc.scalar.copy(val[k][:], p_kv[r][:, :, C:2 * C]).then_inc(v_kept, 1)
                wait(act, step, g * NV + at["shifted"])
                nc.scalar.activation(ex[:], shifted[:], ACT.Exp, scale=float((C // NP) ** -0.5)).then_inc(raised, 1)

        @block.tensor
        def _(pe):
            pe.wait_ge(loaded, 32)
            with pe.Fori(0, NT // U) as g:
                def point_step(k):
                    return g * NV + at[f"point{k}"]

                for k in range(U):
                    i = g * U + k
                    r = k % 2
                    wait(pe, step, point_step(k))
                    wait(pe, t_kept, g * U + max(k - 1, 0))
                    for j in range(NP // 2):
                        mm = nc.tensor.transpose(p_t[r][:, j, :], point[r][:, 2 * j:2 * j + 2, :].rearrange("p n c -> p (n c)"),
                                                 ident[:])
                    mm.then_inc(turned, 1)
                    wait(pe, t_kept, i + 1)
                    if k >= 2:
                        wait(pe, step, g * NV + at[f"qk{k - 2}"])
                    for j in range(NP // 2):
                        mm = nc.tensor.matmul(p_kv[r][:, 2 * j:2 * j + 2, :], p_sb[r][:, j, :],
                                              w_kv[:].rearrange("p e n -> p (e n)"), start=True, stop=True)
                    mm.then_inc(projected, 1)


def gates(nc, tag, kind, hid, xn, ident_bf, router, X_all, G_all):
    layer = kind == "layer"
    with ExitStack() as ctx:
        m = Scope(nc, ctx, tag + "g")
        rest = m.sb("rest", [P, T, C])
        x_hm = [m.sb(f"x_hm{u}", [P, T, P], BF16) for u in range(2)]
        x_hl = [m.sb(f"x_hl{u}", [P, T, P], BF16) for u in range(2)]
        w_raw = m.sb("w_raw", [P, E])
        w_rest = m.sb("w_rest", [P, E])
        w_s = m.sb("w_s", [P, 3, E], BF16)
        w_lo = m.sb("w_lo", [P, E], BF16)
        logits, ex, prob, others, eq, named, gate, g_rest = (m.sb(n, [P, NT, E]) for n in (
            "logits", "ex", "prob", "others", "eq", "named", "gate", "g_rest"))
        top, tot, rtot, norm, rnorm = (m.sb(n, [P, NT]) for n in ("top", "tot", "rtot", "norm", "rnorm"))
        best = m.sb("best", [P, 2, NT])
        lead = m.sb("lead", [P, 2, NT])
        rank = m.sb("rank", [P, NT, E])
        hit = m.sb("hit", [P, 2, NT, E])
        g_s = m.sb("g_s", [P, NT, P], BF16)
        p_t = [m.ps(f"p_t{u}", [P, 2, S], BF16) for u in range(2)]
        p_l = [m.ps(f"p_l{u}", [P, T, E]) for u in range(2)]
        p_g = [m.ps(f"p_g{u}", [P, S], BF16) for u in range(2)]
        (x_split,
         ) = m.counts("x_split")
        turned = m.counts("turned0 turned1")
        kept = m.counts("kept0 kept1")
        scored = m.counts("scored0 scored1")
        logits_kept = m.counts("logits_kept0 logits_kept1")
        gates_turned = m.counts("gates_turned0 gates_turned1")
        gates_kept = m.counts("gates_kept0 gates_kept1")
        ready, loaded, w_split = m.sem("ready"), m.sem("loaded"), m.sem("w_split")
        step = m.sem("step")
        raised = m.sem("raised")
        joined = m.sem("joined")
        block = ctx.enter_context(nc.Block())

        @block.sync
        def _(sp):
            for h in range(2):
                sp.dma_start(w_raw[h * C:(h + 1) * C], router).then_inc(loaded, 16)

        @block.gpsimd
        def _(pool):
            nc.gpsimd.memset(g_s[:], 0.0).then_inc(ready, 1)
            nc.gpsimd.iota(rank[:], pattern=[[0, NT], [-1, E]], base=E, channel_multiplier=0,
                           allow_small_or_imprecise_dtypes=True).then_inc(ready, 1)
            pool.wait_ge(ready, 2)
            if layer:
                nc.gpsimd.tensor_tensor(hid[:], hid[:], xn[:], ALU.add).then_inc(joined, 1)
                pool.wait_ge(joined, 1)

        names = ["top", "shifted", "tot", "rtot", "prob", "best0", "eq0", "named0", "lead0", "hit0", "less",
                 "others", "best1", "eq1", "named1", "lead1", "hit1", "norm", "floor", "rnorm",
                 "val0", "val1", "both", "gate", "g_hi", "g_rest", "g_mid", "g_lo", "g_hi2"]
        at = {n: k + 1 for k, n in enumerate(names)}

        @block.vector
        def _(dve):
            dve.wait_ge(loaded, 32)
            split(nc.vector, w_split, 0, w_s[:, 0], w_s[:, 1], w_lo[:], w_raw[:], w_rest[:])
            dve.wait_ge(w_split, 4)
            nc.vector.tensor_copy(w_s[0:C, 2], w_lo[0:C]).then_inc(w_split, 1)
            nc.vector.tensor_copy(w_s[C:P, 2], w_s[C:P, 0]).then_inc(w_split, 1)
            with dve.Fori(0, B // 2) as g:
                for u in range(2):
                    b = 2 * g + u
                    wait(dve, turned[u], g)
                    split(nc.vector, x_split, 5 * b + 1, x_hm[u][:, :, 0:C], x_hm[u][:, :, C:P], x_hl[u][:, :, C:P],
                          xn[:, bass.ds(b * T, T), :], rest[:])
                    nc.vector.tensor_copy(x_hl[u][:, :, 0:C], x_hm[u][:, :, 0:C]).then_inc(x_split, 1)

            def do(name, ins):
                ins.then_inc(step, 1)
                assert at[name] == do.n + 1, name
                do.n += 1
                dve.wait_ge(step, do.n)

            do.n = 0
            tt, ts = nc.vector.tensor_tensor, nc.vector.tensor_scalar
            reduce = nc.vector.tensor_reduce
            along = lambda v: v.unsqueeze(2).broadcast_to([P, NT, E])
            for u in range(2):
                wait(dve, logits_kept[u], B // 2)
            do("top", reduce(top[:], logits[:], AX.X, ALU.max))
            do("shifted", tt(ex[:], logits[:], along(top[:]), ALU.subtract))
            dve.wait_ge(raised, 1)
            do("tot", reduce(tot[:], prob[:], AX.X, ALU.add))
            do("rtot", nc.vector.reciprocal(rtot[:], tot[:]))
            do("prob", tt(prob[:], prob[:], along(rtot[:]), ALU.mult))
            dve.wait_ge(ready, 2)
            for k, p in enumerate((prob, others)):
                do(f"best{k}", reduce(best[:, k], p[:], AX.X, ALU.max))
                do(f"eq{k}", tt(eq[:], p[:], along(best[:, k]), ALU.is_equal))
                do(f"named{k}", tt(named[:], eq[:], rank[:], ALU.mult))
                do(f"lead{k}", reduce(lead[:, k], named[:], AX.X, ALU.max))
                do(f"hit{k}", tt(hit[:, k], rank[:], along(lead[:, k]), ALU.is_equal))
                if k == 0:
                    do("less", ts(eq[:], hit[:, 0], -2.0, None, ALU.mult))
                    do("others", tt(others[:], prob[:], eq[:], ALU.add))
            do("norm", tt(norm[:], best[:, 0], best[:, 1], ALU.add))
            do("floor", ts(norm[:], norm[:], 1e-12 if layer else 1e-9, None, ALU.max if layer else ALU.add))
            do("rnorm", nc.vector.reciprocal(rnorm[:], norm[:]))
            for k in range(2):
                do(f"val{k}", tt(hit[:, k], hit[:, k], along(best[:, k]), ALU.mult))
            do("both", tt(eq[:], hit[:, 0], hit[:, 1], ALU.add))
            do("gate", tt(gate[:], eq[:], along(rnorm[:]), ALU.mult))
            split(nc.vector, step, at["gate"], g_s[:, :, 0:E], g_s[:, :, 32:32 + E],
                  g_s[:, :, 64:64 + E], gate[:], g_rest[:])
            nc.vector.tensor_copy(g_s[:, :, 96:96 + E], g_s[:, :, 0:E]).then_inc(step, 1)
            with dve.Fori(0, B // 2) as g:
                wait(dve, gates_turned[0], g + 1)
                nc.vector.tensor_copy(G_all[:, bass.ds(2 * g * S, S)], p_g[0][:]).then_inc(gates_kept[0], 1)
            wait(dve, gates_kept[0], B // 2)

        @block.scalar
        def _(act):
            def keep(g, u):
                wait(act, turned[u], g + 1)
                for k in range(2):
                    nc.scalar.copy(X_all[:, k, bass.ds((2 * g + u) * S, S)], p_t[u][:, k]).then_inc(kept[u], 1)

            def keep_logits(g, u):
                wait(act, scored[u], g + 1)
                nc.scalar.copy(logits[:, bass.ds((2 * g + u) * T, T), :], p_l[u][:]).then_inc(logits_kept[u], 1)

            keep(0, 0)
            with act.Fori(0, B // 2 - 1) as g:
                keep(g, 1)
                keep_logits(g, 0)
                keep(g + 1, 0)
                keep_logits(g, 1)
            g = B // 2 - 1
            keep(g, 1)
            keep_logits(g, 0)
            keep_logits(g, 1)
            act.wait_ge(step, at["shifted"])
            nc.scalar.activation(prob[:], ex[:], ACT.Exp).then_inc(raised, 1)
            with act.Fori(0, B // 2) as g:
                wait(act, gates_turned[1], g + 1)
                nc.scalar.copy(G_all[:, bass.ds((2 * g + 1) * S, S)], p_g[1][:]).then_inc(gates_kept[1], 1)
            wait(act, gates_kept[1], B // 2)

        @block.tensor
        def _(pe):
            def turn(g, u):
                wait(pe, x_split, 5 * (2 * g + u) + 5)
                wait(pe, kept[u], 2 * g)
                for k, x in enumerate((x_hm[u], x_hl[u])):
                    for t in range(T):
                        mm = nc.tensor.transpose(p_t[u][:, k, t * P:(t + 1) * P], x[:, t, :], ident_bf[:])
                mm.then_inc(turned[u], 1)

            def score(g, u):
                wait(pe, kept[u], 2 * g + 2)
                wait(pe, logits_kept[u], g)
                b = 2 * g + u
                for t in range(T):
                    for k in range(3):
                        mm = nc.tensor.matmul(p_l[u][:, t, :], X_all[:, k // 2, bass.ds(b * S + t * P, P)], w_s[:, k],
                                              start=(k == 0), stop=(k == 2))
                mm.then_inc(scored[u], 1)

            pe.wait_ge(w_split, 6)
            turn(0, 0)
            with pe.Fori(0, B // 2 - 1) as g:
                turn(g, 1)
                score(g, 0)
                turn(g + 1, 0)
                score(g, 1)
            g = B // 2 - 1
            turn(g, 1)
            score(g, 0)
            score(g, 1)
            pe.wait_ge(step, at["g_hi2"])
            with pe.Fori(0, B // 2) as g:
                for u in range(2):
                    wait(pe, gates_kept[u], g)
                    for t in range(T):
                        mm = nc.tensor.transpose(p_g[u][:, t * P:(t + 1) * P],
                                                 g_s[:, bass.ds((2 * g + u) * T + t, 1), :].rearrange("p a c -> p (a c)"),
                                                 ident_bf[:])
                    mm.then_inc(gates_turned[u], 1)


def experts(nc, tag, kind, hid, ident, w, X_all, G_all):
    gelu = kind == "gelu"
    hidden = w["w2"].shape[0]
    NK = (hidden + P - 1) // P
    full, over = hidden // P, hidden % P
    CH = 512
    NCH = B * S // CH
    J = CH // P
    with ExitStack() as ctx:
        m = Scope(nc, ctx, tag + "e")
        NW = 1 if gelu else 2
        w_raw = m.sb("w_raw", [P, NK * P])
        w_rest = m.sb("w_rest", [P, NK * P])
        w_lo = m.sb("w_lo", [P, NK * P], BF16)
        w_in = [[m.sb(f"w_in{n}{k}", [P, NK * P], BF16) for k in range(3)] for n in range(NW)]
        w2 = m.sb("w2", [P, NK, P])
        b1 = m.sb("b1", [P, NK]) if gelu else None
        b2_raw = m.sb("b2_raw", [P, C])
        b2_rest = m.sb("b2_rest", [P, C])
        b2_part = m.sb("b2_part", [P, 3, C], BF16)
        b2 = m.sb("b2", [P, 2, P], BF16)
        spread_raw = m.sb("spread_raw", [P, NK * P])
        spread = m.sb("spread", [P, NK * P], BF16)
        act_h = m.sb("act_h", [P, 2, CH])
        up = m.sb("up", [P, 2, CH])
        gated = m.sb("gated", [P, 2, CH])
        yT = m.sb("yT", [P, CH])
        p_a = [m.ps(f"p_a{r}", [P, CH]) for r in range(2)]
        p_b = [m.ps(f"p_b{r}", [P, CH]) for r in range(2)]
        p_g = [m.ps(f"p_g{r}", [P, CH]) for r in range(2)]
        p_y = m.ps("p_y", [P, CH])
        p_o = m.ps("p_o", [P, J, P])
        (a_made,
         b_made,
         act_done,
         up_done,
         gated_done,
         y_done,
         y_kept,
         turned,
         added,
         ) = m.counts("a_made b_made act_done up_done gated_done y_done y_kept turned added")
        loaded, loaded3, zeroed, w_split, b_split = (m.sem(n) for n in
                                                     ("loaded", "loaded3", "zeroed", "w_split", "b_split"))
        block = ctx.enter_context(nc.Block())
        loads = [(spread_raw[k * 32:k * 32 + E, 0:hidden], w["spread"]) for k in range(3)]
        loads.append((w2[:, 0:full, 0:C], w["w2"][0:full * P, :].rearrange("(k p) c -> p k c", p=P)))
        loads += [(w_raw[h * C:(h + 1) * C, 0:hidden], w["w1"]) for h in range(2)]
        if over:
            loads.append((w2[0:over, full, 0:C], w["w2"][full * P:hidden, :]))
        if gelu:
            loads.append((b1[:], w["b1"]))
            loads += [(b2_raw[k * 32:k * 32 + E], w["b2"]) for k in range(4)]
        zeroing = [spread_raw, w_raw, w2, b2_raw, b2]

        @block.sync
        def _(sp):
            sp.wait_ge(zeroed, len(zeroing))
            for dst, src in loads:
                sp.dma_start(dst, src).then_inc(loaded, 16)
            if not gelu:
                sp.wait_ge(w_split, 6)
                for h in range(2):
                    sp.dma_start(w_raw[h * C:(h + 1) * C, 0:hidden], w["w3"]).then_inc(loaded3, 16)

        @block.gpsimd
        def _(pool):
            for x in zeroing:
                nc.gpsimd.memset(x[:], 0.0).then_inc(zeroed, 1)

        @block.tensor
        def _(pe):
            pe.wait_ge(w_split, 6 * NW)
            pe.wait_ge(b_split, 8 if gelu else 1)

            def second(n, k):
                wait(pe, gated_done, n * NK + k + 1)
                mm = nc.tensor.matmul(p_y[:], w2[:, k, :], gated[:, k % 2, :], start=(k == 0 and not gelu),
                                      stop=(k == NK - 1))
                mm.then_inc(y_done, 1)

            def first(out, w, n, k):
                for q in range(3):
                    mm = nc.tensor.matmul(out, w[q][:, k * P:(k + 1) * P], X_all[:, q // 2, bass.ds(n * CH, CH)],
                                          start=(q == 0), stop=(q == 2))
                return mm

            with pe.Fori(0, NCH) as n:
                wait(pe, y_kept, n)
                if gelu:
                    for q in range(2):
                        nc.tensor.matmul(p_y[:], b2[:, q], G_all[:, bass.ds(n * CH, CH)], start=(q == 0), stop=False)
                for k in range(NK):
                    u = k % 2
                    last = n * NK + max(k - 1, 0)
                    wait(pe, act_done, last)
                    first(p_a[u][:], w_in[0], n, k).then_inc(a_made, 1)
                    wait(pe, gated_done, last)
                    if not gelu:
                        first(p_b[u][:], w_in[1], n, k)
                    nc.tensor.matmul(p_g[u][:], spread[:, k * P:(k + 1) * P], G_all[:, bass.ds(n * CH, CH)],
                                     start=True, stop=True).then_inc(b_made, 1)
                    if k:
                        second(n, k - 1)
                second(n, NK - 1)
                wait(pe, y_kept, n + 1)
                wait(pe, added, n)
                for j in range(J):
                    mm = nc.tensor.transpose(p_o[:, j, :], yT[:, j * P:(j + 1) * P], ident[:])
                mm.then_inc(turned, 1)

        @block.scalar
        def _(act):
            act.wait_ge(loaded, 16 * len(loads))
            with act.Fori(0, NCH) as n:
                for k in range(NK):
                    u = k % 2
                    wait(act, a_made, n * NK + k + 1)
                    wait(act, gated_done if gelu else up_done, n * NK + max(k - 1, 0))
                    if gelu:
                        nc.scalar.activation(act_h[:, u, :], p_a[u][:], ACT.Gelu,
                                             bias=b1[:, k:k + 1]).then_inc(act_done, 1)
                    else:
                        nc.scalar.activation(act_h[:, u, :], p_a[u][:], ACT.Silu).then_inc(act_done, 1)
                wait(act, y_done, NK * (n + 1))
                wait(act, turned, n)
                nc.scalar.copy(yT[:], p_y[:]).then_inc(y_kept, 1)

        @block.vector
        def _(dve):
            for n in range(NW):
                dve.wait_ge(loaded if n == 0 else loaded3, 16 * len(loads) if n == 0 else 32)
                split(nc.vector, w_split, 6 * n, w_in[n][0][:], w_in[n][1][:], w_lo[:], w_raw[:], w_rest[:])
                dve.wait_ge(w_split, 6 * n + 4)
                nc.vector.tensor_copy(w_in[n][2][0:C], w_lo[0:C]).then_inc(w_split, 1)
                nc.vector.tensor_copy(w_in[n][2][C:P], w_in[n][0][C:P]).then_inc(w_split, 1)
                dve.wait_ge(w_split, 6 * n + 6)
            nc.vector.tensor_copy(spread[:], spread_raw[:]).then_inc(b_split, 1)
            if gelu:
                split(nc.vector, b_split, 1, b2_part[:, 0], b2_part[:, 1], b2_part[:, 2], b2_raw[:], b2_rest[:])
                dve.wait_ge(b_split, 5)
                nc.vector.tensor_copy(b2[0:96, 0, 0:C], b2_part[0:96, 0])
                nc.vector.tensor_copy(b2[96:P, 0, 0:C], b2_part[96:P, 1]).then_inc(b_split, 1)
                nc.vector.tensor_copy(b2[0:32, 1, 0:C], b2_part[0:32, 2]).then_inc(b_split, 1)
                nc.vector.tensor_copy(b2[32:64, 1, 0:C], b2_part[32:64, 1]).then_inc(b_split, 1)
            with dve.Fori(0, NCH) as n:
                for k in range(NK):
                    u = k % 2
                    wait(dve, act_done, n * NK + k + 1)
                    wait(dve, b_made, n * NK + k + 1)
                    wait(dve, y_done, n * NK + max(k - 1, 0))
                    if gelu:
                        nc.vector.tensor_tensor(gated[:, u, :], act_h[:, u, :], p_g[u][:],
                                                ALU.mult).then_inc(gated_done, 1)
                    else:
                        nc.vector.tensor_tensor(up[:, u, :], act_h[:, u, :], p_b[u][:],
                                                ALU.mult).then_inc(up_done, 1)
                        wait(dve, up_done, n * NK + k + 1)
                        nc.vector.tensor_tensor(gated[:, u, :], up[:, u, :], p_g[u][:],
                                                ALU.mult).then_inc(gated_done, 1)
                wait(dve, turned, n + 1)
                x = hid[:, bass.ds(n * J, J), :]
                nc.vector.tensor_tensor(x, x, p_o[:, :, 0:C], ALU.add).then_inc(added, 1)
            wait(dve, added, NCH)


def build(nc, ins, out, stages):
    with ExitStack() as ctx:
        g = Scope(nc, ctx, "g")
        hid = g.sb("hid", [P, NT, C])
        ident = g.sb("ident", [P, P])
        ident_bf = g.sb("ident_bf", [P, P], BF16)
        loaded, made, stored = g.sem("loaded"), g.sem("made"), g.sem("stored")
        summed = g.sem("summed")
        fetched = [g.sem(f"fetched{r}") for r in range(4)]
        with nc.Block() as block:
            @block.gpsimd
            def _(pool):
                nc.gpsimd.memset(ident[:], 0.0).then_inc(made, 1)
                pool.wait_ge(made, 1)
                nc.gpsimd.affine_select(out=ident[:], in_=ident[:], compare_op=ALU.not_equal, fill=1.0,
                                        base=0, pattern=[[-1, P]], channel_multiplier=1).then_inc(made, 1)
                pool.wait_ge(made, 2)
                nc.gpsimd.tensor_copy(ident_bf[:], ident[:]).then_inc(made, 1)
                pool.wait_ge(made, 3)

            @block.sync
            def _(sp):
                if "h" in ins:
                    sp.dma_start(hid[:], ins["h"].rearrange("(t p) c -> p t c", p=P)).then_inc(loaded, 16)
                    sp.wait_ge(loaded, 16)

        def attn_layer(tag, H, scale, w, bias_row):
            with ExitStack() as sub:
                m = Scope(nc, sub, tag)
                A_all = m.sb("A_all", [C, H, C])
                W_aug = m.sb("W_aug", [P, H, 2, C + 1])
                V_all = m.sb("V_all", [P, NT, C])
                Q_all = m.sb("Q_all", [C, B * S])
                K_all = m.sb("K_all", [P, 3, B * S], BF16)
                attention_weights(nc, tag, H, scale, w, ident, A_all, W_aug)
                normalise(nc, tag + "v", hid, V_all, bias_row=bias_row, one=True)
                channel_major(nc, tag, ident, V_all, Q_all, K_all)
                attention(nc, tag, H, hid, ident_bf, A_all, W_aug, V_all, Q_all, K_all)

        if "tok" in stages:
            with ExitStack() as sub:
                m = Scope(nc, sub, "tk")
                Q_all = m.sb("Q_all", [P, NT, C])
                I_all = m.sb("I_all", [P, NT, 8], I32)
                F_all = m.sb("F_all", [P, NT, 8, 4])
                sampling_points(nc, "tk", ins, ident_bf, Q_all, I_all, F_all)
                deformable_attention(nc, "tk", ins, ident, Q_all, I_all, F_all, hid, fetched)
        if "attn0" in stages:
            attn_layer("l0", 8, 8 ** -0.5, {"q": ins["WQT"], "k": ins["WKT"], "v": ins["WVT"], "o": ins["Wout"],
                                            "bq": None}, ins["bout"])
        def moe_layer(tag, kinds, hid, router, norm_row, w):
            with ExitStack() as sub:
                m = Scope(nc, sub, tag)
                X_all = m.sb("X_all", [P, 2, B * S], BF16)
                G_all = m.sb("G_all", [P, B * S], BF16)
                with ExitStack() as inner:
                    xn = Scope(nc, inner, tag + "i").sb("xn", [P, NT, C])
                    normalise(nc, tag + "v", hid, xn, rms=kinds[0] == "rms", weight_row=norm_row)
                    gates(nc, tag, kinds[0], hid, xn, ident_bf, router, X_all, G_all)
                experts(nc, tag, kinds[1], hid, ident, w, X_all, G_all)

        if "moe0" in stages:
            moe_layer("m0", ("layer", "gelu"), hid, ins["router0"], None,
                      {"w1": ins["w1_0"], "w2": ins["w2_0"], "b1": ins["b1_0"], "b2": ins["b2_0"],
                       "spread": ins["spread0"]})
        if "attn1" in stages:
            attn_layer("l1", 1, C ** -0.5, {"q": ins["Wq1"], "k": ins["Wk1"], "v": ins["Wv1"], "o": ins["Wo1T"],
                                            "bq": ins["bq1"], "bk": ins["bk1"], "bv": ins["bv1"]}, ins["bo1"])

        xs = g.sb("xs", [P, NT, C])
        last = "moe1" in stages or "gqa" in stages
        if last:
            normalise(nc, "n1", hid, xs)
        if "gqa" in stages:
            with ExitStack() as sub:
                m = Scope(nc, sub, "q1")
                A_all = m.sb("A_all", [C, 4, C])
                W_aug = m.sb("W_aug", [P, 4, 2, C + 1])
                V_all = m.sb("V_all", [P, NT, C])
                Q_all = m.sb("Q_all", [C, B * S])
                K_all = m.sb("K_all", [P, 3, B * S], BF16)
                masks = m.sb("masks", [P, 2, P], BF16)
                masks_32 = m.sb("masks_32", [P, 2, P])
                w_loaded, w_ready = m.sem("w_loaded"), m.sem("w_ready")
                with nc.Block() as block:
                    @block.gpsimd
                    def _(pool):
                        nc.gpsimd.memset(W_aug[:], 0.0).then_inc(w_ready, 1)
                        nc.gpsimd.memset(masks_32[:], 0.0).then_inc(w_ready, 1)
                        pool.wait_ge(w_ready, 2)
                        for k, sign in enumerate((1, -1)):
                            nc.gpsimd.affine_select(out=masks_32[:, k], in_=masks_32[:, k], compare_op=ALU.is_ge,
                                                    fill=-1e30, base=0, pattern=[[-sign, P]],
                                                    channel_multiplier=sign).then_inc(w_ready, 1)
                        pool.wait_ge(w_ready, 4)
                        nc.gpsimd.tensor_copy(masks[:], masks_32[:]).then_inc(w_ready, 1)
                        pool.wait_ge(w_ready, 5)
                        nc.gpsimd.memset(W_aug[0:1, :, 0, C:C + 1], 1.0).then_inc(w_ready, 1)
                        pool.wait_ge(w_ready, 6)
                        nc.gpsimd.memset(W_aug[C:C + 1, :, 1, C:C + 1], 1.0).then_inc(w_ready, 1)
                        pool.wait_ge(w_ready, 7)

                    @block.sync
                    def _(sp):
                        sp.dma_start(A_all[:], ins["pick"]).then_inc(w_loaded, 16)
                        sp.wait_ge(w_ready, 7)
                        for h in range(4):
                            for e in range(2):
                                o = e * C + 1 + 16 * (h // 2)
                                sp.dma_start(W_aug[o:o + 16, h, e, 0:C], ins["woT"][h * 16:(h + 1) * 16]).then_inc(w_loaded, 16)
                        sp.wait_ge(w_loaded, 16 * 9)
                rotary_heads(nc, "q1", xs, ident, ident_bf, ins["ln1"], ins["wqkv"], ins["rope"], V_all, Q_all, K_all)
                attention(nc, "q1", 4, xs, ident_bf, A_all, W_aug, V_all, Q_all, K_all, (masks[:, 0], masks[:, 1]))
        if "moe1" in stages:
            moe_layer("m1", ("rms", "silu"), xs, ins["router1"], ins["ln2"],
                      {"w1": ins["w1_1"], "w3": ins["w3_1"], "w2": ins["w2_1"], "spread": ins["spread1"]})

        with nc.Block() as block:
            @block.sync
            def _(sp):
                if last:
                    sp.wait_ge(summed, 1)
                sp.dma_start(out.rearrange("(t p) c -> p t c", p=P), hid[:] if not last or "attn0" in stages else xs[:]).then_inc(stored, 16)
                sp.wait_ge(stored, 16)

            @block.vector
            def _(dve):
                if last:
                    nc.vector.tensor_tensor(hid[:], hid[:], xs[:], ALU.add).then_inc(summed, 1)


def host_layout(v, np):
    ins = {}
    if "x" in v:
        image = v["x"].transpose(0, 2, 3, 1)
        ins["pixels"] = np.stack([image[:, :-1], image[:, 1:]], 3).reshape(B * (WD - 1) * WD, 2 * C)
        line = np.linspace(-1.0, 1.0, GRID, dtype=np.float32)
        at = (line + np.float32(1)) * np.float32(0.5) * np.float32(WD - 1)
        lo = np.clip(np.floor(at), 0, WD - 2)
        fr = np.clip(at - lo, 0, 1).astype(np.float32)
        lo = lo.astype(np.int64)
        corner = [image[:, lo + dy][:, :, lo + dx] for dx in (0, 1) for dy in (0, 1)]
        ins["patches"] = np.stack(corner, 3).reshape(B * S, 4 * C)
        tokens = lambda a: a.reshape(T, P, a.shape[-1]).transpose(1, 0, 2)
        fx, fy = np.meshgrid(fr, fr)
        ins["f_ref"] = tokens(np.stack([(1 - fx) * (1 - fy), (1 - fx) * fy, fx * (1 - fy), fx * fy], -1))
        ins["ref"] = tokens(np.stack(np.meshgrid(line, line), -1))
        ins["w_qo"] = np.concatenate([v["L0_tok_W_q"].T, v["L0_tok_W_o1"]], 1)
        ins["w_kv"] = np.concatenate([v["L0_tok_W_k"].T, v["L0_tok_W_v"].T], 1)
        ins["w_o2"] = v["L0_tok_W_o2"]
        for n in ("b_o1", "ln_g", "ln_b", "b_o2"):
            ins[n] = v[f"L0_tok_{n}"].reshape(1, 16)
        ins["o_rows"] = (np.array([0, 0, 0, 1, 1, 2, 3, 3]).repeat(16)[:, None] == np.arange(3)).astype(np.float32)
    heads = lambda w: w.T.reshape(8, C, C).transpose(1, 0, 2)
    for n in "QKV":
        ins[f"W{n}T"] = heads(v[f"L0_attn_W{n}"])
    ins["Wout"] = v["L0_attn_Wout"].reshape(8, C, C).transpose(1, 0, 2)
    ins["bout"] = v["L0_attn_bout"].reshape(1, C)
    for n in "qkv":
        ins[f"W{n}1"] = v[f"L1_attn_W{n}"].reshape(C, 1, C)
        ins[f"b{n}1"] = v[f"L1_attn_b{n}"].reshape(C, 1)
    ins["Wo1T"] = v["L1_attn_Wo"].T.reshape(C, 1, C)
    ins["bo1"] = v["L1_attn_bo"].reshape(1, C)
    of_expert = lambda n: (np.arange(E)[:, None] == np.arange(E * n)[None, :] // n).astype(np.float32)
    ins["router0"] = v["L0_ffn_router_w"].T
    ins["w1_0"] = v["L0_ffn_w1"].transpose(1, 0, 2).reshape(C, E * C)
    ins["w2_0"] = v["L0_ffn_w2"].reshape(E * C, C)
    ins["b1_0"] = v["L0_ffn_b1"].reshape(E * C // P, P).T
    ins["b2_0"] = v["L0_ffn_b2"]
    ins["spread0"] = of_expert(C)
    pick = np.zeros((C, 4, C), np.float32)
    for h in range(4):
        for d in range(16):
            pick[16 * h + d, h, 1 + 32 * (h // 2) + d] = 0.25
    ins["pick"] = pick
    freq = 1.0 / 10000.0 ** (np.arange(0, 16, 2, dtype=np.float32) / 16)
    angle = np.outer(np.arange(S, dtype=np.float32), freq)
    rope = np.stack([np.cos(np.concatenate([angle, angle], -1)),
                     np.sin(np.concatenate([angle, angle], -1)) * np.repeat(np.float32([-1, 1]), 8)])
    ins["rope"] = rope.astype(np.float32).reshape(2, T, P, 16).transpose(2, 0, 1, 3)
    ins["wqkv"] = np.concatenate([v["L1_ffn_wq"], v["L1_ffn_wk"], v["L1_ffn_wv"]]).T
    ins["woT"] = v["L1_ffn_wo"].T
    ins["ln1"] = v["L1_ffn_ln1_w"].reshape(1, C)
    ins["router1"] = v["L1_ffn_router_w"].T
    ins["ln2"] = v["L1_ffn_ln2_w"].reshape(1, C)
    for n in ("w1", "w3"):
        ins[n + "_1"] = v["L1_ffn_" + n].transpose(2, 0, 1).reshape(C, E * HID1)
    ins["w2_1"] = v["L1_ffn_w2"].transpose(0, 2, 1).reshape(E * HID1, C)
    ins["spread1"] = of_expert(HID1)
    return ins


def kernel(**inputs):
    import numpy as np
    import concourse.bacc as bacc
    from concourse.bass_utils import run_bass_kernel_spmd

    v = {k: np.asarray(a) for k, a in inputs.items()}
    ins = host_layout(v, np)
    if "h" in v:
        ins["h"] = v["h"].reshape(B * S, C)
    nc = bacc.Bacc("TRN2", target_bir_lowering=False, num_devices=1)
    arrays, aps = {}, {}
    for name, a in ins.items():
        arrays[name] = np.ascontiguousarray(a)
        aps[name] = nc.dram_tensor(name, arrays[name].shape, mybir.dt.from_np(arrays[name].dtype),
                                   kind="ExternalInput").ap()
    out = nc.dram_tensor("out_tokens", (B * S, C), F32, kind="ExternalOutput").ap()
    build(nc, aps, out, STAGES)
    res = run_bass_kernel_spmd(nc, [arrays], core_ids=[0])
    return res.results[0]["out_tokens"].reshape(B, S, C)


STAGES = ("tok", "attn0", "moe0", "attn1", "gqa", "moe1")
```

```python
from contextlib import ExitStack

import concourse.bass as bass
from concourse import mybir

F32 = mybir.dt.float32
BF16 = mybir.dt.bfloat16
I32 = mybir.dt.int32
U32 = mybir.dt.uint32
ACT = mybir.ActivationFunctionType
ALU = mybir.AluOpType
AX = mybir.AxisListType

P = 128
B = 8
S = 1024
C = 64
T = S // P
NT = B * T
EPS = 1e-5
EPS_RMS = 1e-6
E = 8
HID1 = int(8 / 3 * C)
WD = 128
GRID = 32
OFFSET_SCALE = 4.0


class Scope:

    def __init__(self, nc, ctx, tag):
        self.nc, self.ctx, self.tag = nc, ctx, tag
        self.sems, self.counting, self.held = [], [], ExitStack()
        ctx.push(self.clear)

    def sb(self, name, shape, dt=F32):
        return self.ctx.enter_context(self.nc.sbuf_tensor(f"{self.tag}_{name}", shape, dt))

    def ps(self, name, shape, dt=F32):
        return self.ctx.enter_context(self.nc.psum_tensor(f"{self.tag}_{name}", shape, dt))

    def sem(self, name):
        self.sems.append(self.held.enter_context(self.nc.semaphore(f"{self.tag}_{name}")))
        return self.sems[-1]

    def clear(self, failed=None, *_):
        if self.sems and failed is None:
            with self.nc.Block() as block:
                @block.sync
                def _(sp):
                    for s in self.sems:
                        sp.sem_clear(s)
        self.held.close()

    def counts(self, names):
        counting = [self.sem(n) for n in names.split()]
        self.counting += counting
        return counting

    def block(self):
        if self.counting:
            with self.nc.Block() as block:
                @block.sync
                def _(sp):
                    for s in self.counting:
                        sp.sem_inc(s, 1)
        return self.ctx.enter_context(self.nc.Block())


def wait(eng, sem, n):
    eng.wait_ge(sem, n + 1)


def split(eng, sem, count, hi, mid, lo, x, rest):
    eng.tensor_copy(hi, x).then_inc(sem, 1)
    eng.wait_ge(sem, count + 1)
    eng.tensor_tensor(rest, x, hi, ALU.subtract).then_inc(sem, 1)
    eng.wait_ge(sem, count + 2)
    eng.tensor_copy(mid, rest).then_inc(sem, 1)
    eng.wait_ge(sem, count + 3)
    eng.tensor_tensor(lo, rest, mid, ALU.subtract).then_inc(sem, 1)


def attention_weights(nc, block, m, p_a, p_w, H, scale, w, A_all, W_aug):
    raw = m.sb("raw", [C, 4, H, C])
    fold = m.sb("fold", [C, 3, H, C])
    v_two = m.sb("v_two", [C, H, 2, C])
    loaded, folded, zeroed, made_a, made_w, kept = (
        m.sem(n) for n in ("loaded", "folded", "zeroed", "made_a", "made_w", "kept"))
    bias = m.sb("bias", [C, 3]) if w["bq"] is not None else None
    n_loads = 4 + (3 if bias is not None else 0)

    @block.sync
    def _(sp):
        for n, key in enumerate(("q", "k", "v", "o")):
            sp.dma_start(raw[:, n], w[key]).then_inc(loaded, 16)
        if bias is not None:
            for n, key in enumerate(("bq", "bk", "bv")):
                sp.dma_start(bias[:, n:n + 1], w[key]).then_inc(loaded, 16)

    @block.gpsimd
    def _(pool):
        nc.gpsimd.memset(W_aug[:], 0.0).then_inc(zeroed, 1)
        pool.wait_ge(zeroed, 1)
        nc.gpsimd.memset(W_aug[0:1, :, 0, C:C + 1], 1.0).then_inc(zeroed, 1)
        nc.gpsimd.memset(W_aug[C:C + 1, :, 1, C:C + 1], 1.0).then_inc(zeroed, 1)
        pool.wait_ge(zeroed, 3)

    @block.vector
    def _(dve):
        dve.wait_ge(loaded, 16 * n_loads)
        nc.vector.tensor_tensor(fold[:, 0:3], raw[:, 0:3], raw[:, 0:3, :, 0:1].broadcast_to([C, 3, H, C]),
                                ALU.subtract).then_inc(folded, 1)
        dve.wait_ge(folded, 1)
        n = 1
        if bias is not None:
            nc.vector.tensor_copy(fold[:, 0:3, 0, 0], bias[:, :]).then_inc(folded, 1)
            n = 2
            dve.wait_ge(folded, 2)
        nc.vector.tensor_copy(v_two[:], fold[:, 2].unsqueeze(2).broadcast_to([C, H, 2, C])).then_inc(folded, 3 - n)
        dve.wait_ge(made_a, 1)
        nc.vector.tensor_scalar(A_all[:], p_a[:, 0:H], scale, None, ALU.mult).then_inc(kept, 1)
        dve.wait_ge(made_w, 1)
        dve.wait_ge(zeroed, 3)
        nc.vector.tensor_copy(W_aug[0:C, :, 0, 0:C], p_w[0:C, 0:H]).then_inc(kept, 1)
        nc.vector.tensor_copy(W_aug[C:P, :, 1, 0:C], p_w[C:P, 0:H]).then_inc(kept, 1)
        dve.wait_ge(kept, 3)

    @block.tensor
    def _(pe):
        pe.wait_ge(folded, 3)
        for h in range(H):
            mm = nc.tensor.matmul(p_a[:, h, :], fold[:, 0, h, :], fold[:, 1, h, :], start=True, stop=True)
        mm.then_inc(made_a, 1)
        for h in range(H):
            mm = nc.tensor.matmul(p_w[:, h, :], v_two[:, h].rearrange("p e c -> p (e c)"), raw[:, 3, h, :], start=True, stop=True)
        mm.then_inc(made_w, 1)


def normalise(nc, tag, x, out, rms=False, weight_row=None, bias_row=None, one=False):
    HT = NT // 2
    with ExitStack() as ctx:
        m = Scope(nc, ctx, tag)
        sq = m.sb("sq", [P, NT, C])
        mean, ssq, std = (m.sb(n, [P, NT]) for n in ("mean", "ssq", "std"))
        eps = m.sb("eps", [P, 1])
        row = m.sb("row", [P, C]) if weight_row is not None or bias_row is not None else None
        ready, loaded = m.sem("ready"), m.sem("loaded")
        step = m.sem("step")
        squared = m.sem("squared")
        rooted = m.sem("rooted")
        block = m.block()
        names = [] if rms else ["sum0", "sum1", "mean0", "mean1", "cen0", "cen1"]
        names += ["ssq0", "ssq1", "rstd0", "rstd1", "out0", "out1"]
        at = {n: k + 1 for k, n in enumerate(names)}
        of = lambda v, h: v[:, h * HT:(h + 1) * HT]
        along = lambda v: v.unsqueeze(2).broadcast_to([P, HT, C])
        on = lambda n: row[:].unsqueeze(1).broadcast_to([P, n, C])

        @block.sync
        def _(sp):
            if row is not None:
                src = weight_row if weight_row is not None else bias_row
                sp.dma_start(row[:], src.broadcast_to([P, C])).then_inc(loaded, 16)

        @block.vector
        def _(dve):
            if not rms:
                for h in range(2):
                    nc.vector.tensor_reduce(of(mean, h), of(x, h), AX.X, ALU.add).then_inc(step, 1)
                for h in range(2):
                    dve.wait_ge(step, at[f"sum{h}"])
                    nc.vector.tensor_scalar(of(mean, h), of(mean, h), 1.0 / C, None, ALU.mult).then_inc(step, 1)
                for h in range(2):
                    dve.wait_ge(step, at[f"mean{h}"])
                    nc.vector.tensor_tensor(of(out, h), of(x, h), along(of(mean, h)), ALU.subtract).then_inc(step, 1)
            if bias_row is not None:
                dve.wait_ge(loaded, 16)
                dve.wait_ge(step, at["cen1"])
                nc.vector.tensor_tensor(x[:], x[:], on(NT), ALU.add)
            for h in range(2):
                dve.wait_ge(squared, h + 1)
                nc.vector.tensor_reduce(of(ssq, h), of(sq, h), AX.X, ALU.add).then_inc(step, 1)
            for h in range(2):
                dve.wait_ge(rooted, h + 1)
                nc.vector.reciprocal(of(std, h), of(std, h)).then_inc(step, 1)
            for h in range(2):
                dve.wait_ge(step, at[f"rstd{h}"])
                a = x if rms else out
                b = sq if weight_row is not None else out
                nc.vector.tensor_tensor(of(b, h), of(a, h), along(of(std, h)), ALU.mult).then_inc(step, 1)
            dve.wait_ge(step, at["out1"])
            if weight_row is not None:
                dve.wait_ge(loaded, 16)
                nc.vector.tensor_tensor(out[:], sq[:], on(NT), ALU.mult)

        @block.scalar
        def _(act):
            act.wait_ge(ready, 1)
            for h in range(2):
                if not rms:
                    act.wait_ge(step, at[f"cen{h}"])
                nc.scalar.activation(of(sq, h), of(x if rms else out, h), ACT.Square).then_inc(squared, 1)
            for h in range(2):
                act.wait_ge(step, at[f"ssq{h}"])
                nc.scalar.activation(of(std, h), of(ssq, h), ACT.Sqrt, bias=eps[:], scale=1.0 / C).then_inc(rooted, 1)

        @block.gpsimd
        def _(pool):
            nc.gpsimd.memset(eps[:], EPS_RMS if rms else EPS).then_inc(ready, 1)
            if one:
                pool.wait_ge(step, at["out1"])
                nc.gpsimd.memset(out[:, :, 0:1], 1.0).then_inc(ready, 1)
                pool.wait_ge(ready, 2)


def key_parts(dve, sem, count, b, K_all, keys, rest):
    into = lambda k, a, z: K_all[a:z, k, bass.ds(b * S, S)]
    dve.tensor_tensor(rest, keys, into(0, 0, P), ALU.subtract).then_inc(sem, 1)
    dve.tensor_copy(into(2, C, P), into(0, C, P)).then_inc(sem, 1)
    wait(dve, sem, count + 2)
    dve.tensor_copy(into(1, 0, P), rest).then_inc(sem, 1)
    wait(dve, sem, count + 3)
    dve.tensor_tensor(into(2, 0, C), rest[0:C], into(1, 0, C), ALU.subtract).then_inc(sem, 1)


def channel_major(nc, tag, ident, V_all, Q_all, K_all):
    with ExitStack() as ctx:
        m = Scope(nc, ctx, tag + "n")
        xt = [m.sb(f"xt{u}", [P, T, 2, C]) for u in range(2)]
        k_rest = [m.sb(f"k_rest{u}", [P, S]) for u in range(2)]
        p_t = [m.ps(f"p_t{u}", [P, S]) for u in range(2)]
        doubled = m.counts("doubled0 doubled1")
        turned = m.counts("turned0 turned1")
        q_kept = m.counts("q_kept0 q_kept1")
        k_high = m.counts("k_high0 k_high1")
        k_parts = m.counts("k_parts0 k_parts1")
        block = m.block()

        @block.scalar
        def _(act):
            def double(g, u):
                wait(act, turned[u], g)
                src = V_all[:, bass.ds((2 * g + u) * T, T), :].unsqueeze(2).broadcast_to([P, T, 2, C])
                nc.scalar.copy(xt[u][:], src).then_inc(doubled[u], 1)

            def keep(g, u):
                b = 2 * g + u
                wait(act, turned[u], g + 1)
                nc.scalar.copy(K_all[:, 0, bass.ds(b * S, S)], p_t[u][:]).then_inc(k_high[u], 1)
                nc.scalar.copy(Q_all[:, bass.ds(b * S, S)], p_t[u][0:C]).then_inc(q_kept[u], 1)

            double(0, 0)
            with act.Fori(0, B // 2 - 1) as g:
                double(g, 1)
                keep(g, 0)
                double(g + 1, 0)
                keep(g, 1)
            g = B // 2 - 1
            double(g, 1)
            keep(g, 0)
            keep(g, 1)
            for u in range(2):
                wait(act, q_kept[u], B // 2)

        @block.tensor
        def _(pe):
            with pe.Fori(0, B // 2) as g:
                for u in range(2):
                    wait(pe, doubled[u], g + 1)
                    wait(pe, q_kept[u], g)
                    wait(pe, k_parts[u], 4 * g)
                    for t in range(T):
                        mm = nc.tensor.transpose(p_t[u][:, t * P:(t + 1) * P],
                                                 xt[u][:, t].rearrange("p e c -> p (e c)"), ident[:])
                    mm.then_inc(turned[u], 1)

        @block.vector
        def _(dve):
            with dve.Fori(0, B // 2) as g:
                for u in range(2):
                    wait(dve, k_high[u], g + 1)
                    wait(dve, q_kept[u], g + 1)
                    key_parts(nc.vector, k_parts[u], 4 * g, 2 * g + u, K_all, p_t[u][:], k_rest[u][:])
            for u in range(2):
                wait(dve, k_parts[u], 4 * (B // 2))


def attention(nc, tag, H, hid, ident_bf, A_all, W_aug, V_all, Q_all, K_all, causal=None):
    N = B * H
    HS = S // 2
    chunks = [(t, e) for t in range(T) for e in range(2) if not causal or e >= t // (T // 2)]
    NC = len(chunks)
    of_tile = [[c for c, (t, e) in enumerate(chunks) if t == k] for k in range(T)]
    row_chunks = [(t, e) for t in range(T) for e in range(2) if not causal or e <= t // (T // 2)]
    NR = len(row_chunks)
    half_rows = len([r for r in row_chunks if r[0] < T // 2])
    PR = (NC + 2 + 2) // 3 * 3
    RE = 4
    less_after = (of_tile[3][-1], of_tile[6][0]) if causal else (of_tile[5][0], of_tile[7][-1])
    first_part = 6 if causal else 10
    with ExitStack() as ctx:
        m = Scope(nc, ctx, tag + "a")
        A_st = [m.sb(f"A_st{u}", [C, 2, C]) for u in range(2)]
        V_st = [m.sb(f"V_st{u}", [P, T, C]) for u in range(2)]
        q_bf = [m.sb(f"q_bf{u}", [P, S], BF16) for u in range(2)]
        q_hm = [m.sb(f"q_hm{u}", [P, S], BF16) for u in range(2)]
        q_hl = [m.sb(f"q_hl{u}", [P, S], BF16) for u in range(2)]
        q_rest = m.sb("q_rest", [P, S])
        peak = [m.sb(f"peak{u}", [P, T, 2]) for u in range(2)]
        down = m.sb("down", [P, T])
        neg = [m.sb(f"neg{u}", [P, 2, T, P], BF16) for u in range(2)]
        ex = m.sb("ex", [P, RE, HS])
        z = m.sb("z", [P, HS])
        rden = m.sb("rden", [P, 2, 2, 2])
        y = m.sb("y", [P, 2, 2, 2, C])
        p_q = m.ps("p_q", [P, S])
        p_m = [m.ps(f"p_m{r}", [P, HS]) for r in range(2)]
        p_s = [m.ps(f"p_s{r}", [P, HS]) for r in range(3)]
        p_z = m.ps("p_z", [P, HS])

        zeroed = m.sem("zeroed")
        (A_placed,
         V_placed,
         q_made,
         q_cast,
         m_made,
         m_taken,
         n_step,
         q_less,
         q_high,
         q_top,
         q_step,
         s_made,
         exp_done,
         pv_done,
         z_kept,
         y_made,
         y_read,
         r_done,
         h_done,
         ) = m.counts("A_placed V_placed q_made q_cast m_made m_taken n_step q_less q_high q_top q_step s_made "
                      "exp_done pv_done z_kept y_made y_read r_done h_done")
        block = m.block()

        def slot(c):
            return (c + 1) % 3 if c < 3 else c % 3

        def first_query(c):
            t, e = chunks[c]
            return (t % (T // 2)) * P if causal and e == t // (T // 2) else 0

        def keys_seen(t, e):
            return min(max((t + 1) * P - e * HS, 0), HS) if causal else HS

        @block.gpsimd
        def _(pool):
            for u in range(2):
                nc.gpsimd.memset(q_bf[u][:], 0.0).then_inc(zeroed, 1)
                nc.gpsimd.memset(neg[u][:], 0.0).then_inc(zeroed, 1)
                nc.gpsimd.memset(peak[u][:], -3e38).then_inc(zeroed, 1)

            def place_A(i, u):
                nc.gpsimd.tensor_copy(A_st[u][:], A_all[:, bass.ds(i % H, 1), :].broadcast_to([C, 2, C])).then_inc(A_placed, 1)

            def place_V(i, u):
                nc.gpsimd.tensor_copy(V_st[u][:], V_all[:, bass.ds((i // H) * T, T), :]).then_inc(V_placed, 1)

            def top(i, u, e):
                wait(pool, q_high, 2 * i + e + 1)
                nc.gpsimd.nop(nofuse=True)
                nc.gpsimd.tensor_copy(q_hl[u][0:C, e * HS:(e + 1) * HS],
                                      q_hm[u][0:C, e * HS:(e + 1) * HS]).then_inc(q_top, 1)

            def body(i, u, more):
                if more == 2:
                    wait(pool, q_made, i + 1)
                    nc.gpsimd.nop(nofuse=True)
                    place_A(i + 2, u)
                if more >= 1:
                    top(i + 1, 1 - u, 0)
                    top(i + 1, 1 - u, 1)
                if more == 2:
                    wait(pool, pv_done, NC * (i + 1))
                    nc.gpsimd.nop(nofuse=True)
                    place_V(i + 2, u)

            for u in range(2):
                place_A(u, u)
                place_V(u, u)
            top(0, 0, 0)
            top(0, 0, 1)
            with pool.Fori(0, N // 2 - 1) as g:
                body(g * 2, 0, 2)
                body(g * 2 + 1, 1, 2)
            body(N - 2, 0, 1)
            wait(pool, A_placed, N)
            wait(pool, V_placed, N)

        @block.tensor
        def _(pe):
            pe.wait_ge(zeroed, 6)

            def project(i, u):
                wait(pe, A_placed, i + 1)
                wait(pe, q_step, 6 * i)
                for e in range(2):
                    mm = nc.tensor.matmul(p_q[:, e * HS:(e + 1) * HS], A_st[u][:].rearrange("p a c -> p (a c)"),
                                          Q_all[:, bass.ds((i // H) * S + e * HS, HS)], start=True, stop=True)
                mm.then_inc(q_made, 1)

            def rows(i, u, k):
                t, e = row_chunks[k]
                n = keys_seen(t, e)
                diagonal = causal and e == t // (T // 2)
                if k == 0:
                    wait(pe, q_cast, i + 1)
                wait(pe, m_taken, NR * i + max(k - 1, 0))
                mm = nc.tensor.matmul(p_m[k % 2][:, 0:n], q_bf[u][:, t * P:(t + 1) * P],
                                      K_all[:, 0, bass.ds((i // H) * S + e * HS, n)], start=True, stop=not diagonal)
                if diagonal:
                    mm = nc.tensor.matmul(p_m[k % 2][:, n - P:n], ident_bf[:], causal[0], start=False, stop=True)
                mm.then_inc(m_made, 1)

            def subtract(i, u, e):
                wait(pe, n_step, 6 * i + 3 * e + 3)
                for t in range(T // 2 * e, T // 2 * (e + 1)):
                    for k in range(2):
                        mm = nc.tensor.matmul(p_q[:, t * P:(t + 1) * P], neg[u][:, k, t, :], ident_bf[:],
                                              start=False, stop=True, skip_group_check=True)
                mm.then_inc(q_less, 1)

            def score(i, u, c, fresh=False):
                t, e = chunks[c]
                s0 = first_query(c)
                diagonal = causal and e == t // (T // 2)
                if c < 3:
                    if not fresh:
                        wait(pe, exp_done, NC * i + (min(PR - 4 + c, NC) - NC))
                elif c == 3:
                    wait(pe, exp_done, NC * i + 3)
                elif c in (4, 5):
                    wait(pe, y_read, 2 * i)
                else:
                    wait(pe, exp_done, NC * i + c - 2)
                if c < 2:
                    wait(pe, q_top, 2 * i + c + 1)
                    wait(pe, q_step, 6 * i + 3 * c + 3)
                for k, q in enumerate((q_hm[u], q_hm[u], q_hl[u])):
                    mm = nc.tensor.matmul(p_s[slot(c)][:, s0:HS], K_all[:, k, bass.ds((i // H) * S + t * P, P)],
                                          q[:, e * HS + s0:(e + 1) * HS], start=(k == 0), stop=(k == 2 and not diagonal))
                if diagonal:
                    mm = nc.tensor.matmul(p_s[slot(c)][:, s0:s0 + P], ident_bf[:], causal[1],
                                          start=False, stop=True)
                mm.then_inc(s_made, 1)

            def total(i, u, t):
                wait(pe, exp_done, NC * i + of_tile[t][-1] + 1)
                if t == 0:
                    wait(pe, V_placed, i + 1)
                    wait(pe, z_kept, i)
                for c in of_tile[t]:
                    e, s0 = chunks[c][1], first_query(c)
                    last = c == max(k for k in range(NC) if chunks[k][1] == e)
                    nc.tensor.matmul(p_z[e * C:(e + 1) * C, s0:HS], V_st[u][:, t, :], ex[:, c % RE, s0:HS],
                                     start=(t == 0), stop=last).then_inc(pv_done, 1)

            def output(i, more):
                wait(pe, z_kept, i + 1)
                wait(pe, exp_done, NC * i + NC + (2 if more else 0))
                for k in range(2):
                    for j in range(2):
                        mm = nc.tensor.matmul(p_s[k + 1][:, j * 2 * (C + 1):(j + 1) * 2 * (C + 1)],
                                              z[:, (2 * k + j) * P:(2 * k + j + 1) * P],
                                              W_aug[:, bass.ds(i % H, 1), :, :].rearrange("p a e c -> p (a e c)"),
                                              start=True, stop=True)
                    mm.then_inc(y_made, 1)

            per_tile = 4 if causal else 3

            def body(i, u, more):
                n = 1 - u
                left = list(range(NR)) if more else []

                def rows_now(k):
                    for _ in range(min(k, len(left))):
                        rows(i + 1, n, left.pop(0))

                total(i, u, 0)
                rows_now(1)
                score(i, u, 3)
                for t in range(1, T):
                    quota = per_tile if t <= 5 else 0
                    for c in of_tile[t + 1] if t < T - 1 else []:
                        score(i, u, c)
                        if more and c in less_after:
                            subtract(i + 1, n, less_after.index(c))
                        rows_now(min(quota, 1))
                        quota -= min(quota, 1)
                    total(i, u, t)
                    rows_now(quota)
                assert not left
                if more:
                    for c in range(3):
                        score(i + 1, n, c)
                if more == 2:
                    project(i + 2, u)
                output(i, more)

            project(0, 0)
            for k in range(NR):
                rows(0, 0, k)
            subtract(0, 0, 0)
            subtract(0, 0, 1)
            for c in range(3):
                score(0, 0, c, fresh=True)
            project(1, 1)
            with pe.Fori(0, N // 2 - 1) as g:
                body(g * 2, 0, 2)
                body(g * 2 + 1, 1, 2)
            body(N - 2, 0, 1)
            body(N - 1, 1, 0)

        @block.scalar
        def _(act):
            act.wait_ge(zeroed, 6)

            def cast(i, u):
                wait(act, q_made, i + 1)
                nc.scalar.copy(q_bf[u][0:C, :], p_q[0:C, :]).then_inc(q_cast, 1)

            def high(i, u, e):
                wait(act, q_less, 2 * i + e + 1)
                nc.scalar.copy(q_hm[u][:, e * HS:(e + 1) * HS], p_q[:, e * HS:(e + 1) * HS]).then_inc(q_high, 1)

            def body(i, u, more):
                for c in range(NC):
                    wait(act, s_made, NC * i + c + 1)
                    wait(act, pv_done, NC * i + max(c - RE + 1, 0))
                    s0 = first_query(c)
                    nc.scalar.activation(ex[:, c % RE, s0:HS], p_s[slot(c)][:, s0:HS], ACT.Exp).then_inc(exp_done, 1)
                    if more and c == 2:
                        cast(i + 1, 1 - u)
                    if more and c in less_after:
                        high(i + 1, 1 - u, less_after.index(c))

            cast(0, 0)
            high(0, 0, 0)
            high(0, 0, 1)
            with act.Fori(0, N // 2 - 1) as g:
                body(g * 2, 0, 2)
                body(g * 2 + 1, 1, 2)
            body(N - 2, 0, 1)
            body(N - 1, 1, 0)

        @block.vector
        def _(dve):
            dve.wait_ge(zeroed, 6)

            def maxima(i, u, k):
                t, e = row_chunks[k]
                wait(dve, m_made, NR * i + k + 1)
                nc.vector.tensor_reduce(peak[u][:, t, e:e + 1], p_m[k % 2][:, 0:keys_seen(t, e)], AX.X,
                                        ALU.max).then_inc(m_taken, 1)

            def negate(i, u, e):
                a, b = T // 2 * e, T // 2 * (e + 1)
                two = lambda v: v[:, a:b].unsqueeze(2).broadcast_to([P, T // 2, 2])
                at = lambda k: neg[u][:, k, a:b, :].rearrange("p t (e c) -> p t e c", e=2)[:, :, :, 0]
                wait(dve, m_taken, NR * i + (half_rows if e == 0 else NR))
                wait(dve, n_step, 6 * i + 3 * e)
                nc.vector.tensor_reduce(down[:, a:b], peak[u][:, a:b, :], AX.X, ALU.max, negate=True).then_inc(n_step, 1)
                wait(dve, n_step, 6 * i + 3 * e + 1)
                nc.vector.tensor_copy(at(0), two(down)).then_inc(n_step, 1)
                wait(dve, n_step, 6 * i + 3 * e + 2)
                nc.vector.tensor_tensor(at(1), two(down), at(0), ALU.subtract).then_inc(n_step, 1)

            def part(i, u, e, n):
                h = slice(e * HS, (e + 1) * HS)
                k = 6 * i + 3 * e
                if n == 0:
                    wait(dve, q_high, 2 * i + e + 1)
                    wait(dve, q_top, 2 * i)
                wait(dve, q_step, k + n)
                if n == 0:
                    op = nc.vector.tensor_tensor(q_rest[C:P, h], p_q[C:P, h], q_hm[u][C:P, h], ALU.subtract)
                elif n == 1:
                    op = nc.vector.tensor_copy(q_hm[u][C:P, h], q_rest[C:P, h])
                else:
                    op = nc.vector.tensor_tensor(q_hl[u][C:P, h], q_rest[C:P, h], q_hm[u][C:P, h], ALU.subtract)
                op.then_inc(q_step, 1)

            def finish(i):
                wait(dve, pv_done, NC * (i + 1))
                wait(dve, y_made, 2 * i)
                nc.vector.tensor_copy(z[:], p_z[:]).then_inc(z_kept, 1)
                x = hid[:, bass.ds((i // H) * T, T), :].rearrange("p (e t) c -> p e t c", e=2)
                for k in range(2):
                    wait(dve, y_made, 2 * i + k + 1)
                    p = p_s[k + 1][:, 0:4 * (C + 1)].rearrange("p (j e c) -> p e j c", j=2, e=2)
                    nc.vector.reciprocal(rden[:, k], p[:, :, :, C]).then_inc(r_done, 1)
                    wait(dve, r_done, 2 * i + k + 1)
                    nc.vector.tensor_tensor(y[:, k], p[:, :, :, 0:C],
                                            rden[:, k].unsqueeze(3).broadcast_to([P, 2, 2, C]),
                                            ALU.mult).then_inc(y_read, 1)
                wait(dve, y_read, 2 * i + 2)
                wait(dve, h_done, 2 * i)
                for k in range(2):
                    out = x[:, :, 2 * k:2 * k + 2, :]
                    nc.vector.tensor_tensor(out, out, y[:, k], ALU.add).then_inc(h_done, 1)

            def queries(i, u):
                for k in range(NR):
                    maxima(i, u, k)
                    if k == half_rows:
                        negate(i, u, 0)
                    if first_part <= k < first_part + 3:
                        part(i, u, 0, k - first_part)
                negate(i, u, 1)
                for n in range(3):
                    part(i, u, 1, n)

            for k in range(NR):
                maxima(0, 0, k)
            for e in range(2):
                negate(0, 0, e)
            for e in range(2):
                for n in range(3):
                    part(0, 0, e, n)
            with dve.Fori(0, N // 2 - 1) as g:
                for u in range(2):
                    queries(g * 2 + (u + 1), 1 - u)
                    finish(g * 2 + u)
            queries(N - 1, 1)
            finish(N - 2)
            finish(N - 1)
            wait(dve, h_done, 2 * N)


def rotary_heads(nc, tag, xn, ident, ident_bf, wqkv, rope, V_all, Q_all, K_all):
    with ExitStack() as ctx:
        m = Scope(nc, ctx, tag + "r")
        rest = m.sb("rest", [P, T, C])
        x_p = [m.sb(f"x_p{k}", [P, T, P], BF16) for k in range(2)]
        x_T = [m.sb(f"x_T{k}", [P, S], BF16) for k in range(2)]
        w_raw, w_rest = m.sb("w_raw", [P, P]), m.sb("w_rest", [P, P])
        w_s = m.sb("w_s", [P, 3, P], BF16)
        w_lo = m.sb("w_lo", [P, P], BF16)
        tab = m.sb("tab", [P, 2, T, 16])
        qkv = m.sb("qkv", [P, T, P])
        t_cos, t_sin = m.sb("t_cos", [P, T, 96]), m.sb("t_sin", [P, T, 96])
        q_n, k_n = m.sb("q_n", [P, T, P]), m.sb("k_n", [P, T, P])
        k_rest = m.sb("k_rest", [P, S])
        p_x = [m.ps(f"p_x{k}", [P, S], BF16) for k in range(2)]
        p_p = m.ps("p_p", [P, T, P])
        p_q = m.ps("p_q", [P, S])
        p_k = m.ps("p_k", [P, S])
        ready, loaded, w_split = m.sem("ready"), m.sem("loaded"), m.sem("w_split")
        (x_split,
         x_turned,
         x_kept,
         projected,
         p_kept,
         v_kept,
         rope_step,
         qk_turned,
         q_kept,
         k_high,
         k_kept,
         ) = m.counts("x_split x_turned x_kept projected p_kept v_kept rope_step qk_turned q_kept k_high k_kept")
        block = m.block()

        @block.sync
        def _(sp):
            for h in range(2):
                sp.dma_start(w_raw[h * C:(h + 1) * C], wqkv).then_inc(loaded, 16)
            sp.dma_start(tab[:], rope).then_inc(loaded, 16)

        @block.gpsimd
        def _(pool):
            nc.gpsimd.memset(q_n[:], 0.0).then_inc(ready, 1)
            nc.gpsimd.memset(k_n[:], 0.0).then_inc(ready, 1)
            nc.gpsimd.memset(V_all[:], 0.0).then_inc(ready, 1)
            pool.wait_ge(ready, 3)
            for e in range(2):
                nc.gpsimd.memset(k_n[:, :, e * C:e * C + 1], 1.0).then_inc(ready, 1)
            nc.gpsimd.memset(V_all[:, :, 0:1], 1.0).then_inc(ready, 1)

        @block.vector
        def _(dve):
            dve.wait_ge(loaded, 48)
            split(nc.vector, w_split, 0, w_s[:, 0], w_s[:, 1], w_lo[:], w_raw[:], w_rest[:])
            dve.wait_ge(w_split, 4)
            nc.vector.tensor_copy(w_s[0:C, 2], w_lo[0:C]).then_inc(w_split, 1)
            nc.vector.tensor_copy(w_s[C:P, 2], w_s[C:P, 0]).then_inc(w_split, 1)

            def split_x(b):
                wait(dve, x_turned, b)
                split(nc.vector, x_split, 5 * b + 1, x_p[0][:, :, 0:C], x_p[0][:, :, C:P], x_p[1][:, :, C:P],
                      xn[:, bass.ds(b * T, T), :], rest[:])
                nc.vector.tensor_copy(x_p[1][:, :, 0:C], x_p[0][:, :, 0:C]).then_inc(x_split, 1)

            def by_position(b):
                wait(dve, p_kept, b + 1)
                wait(dve, rope_step, 6 * b)
                of = qkv[:, :, 0:96].rearrange("p t (h d) -> p t h d", d=16)
                cs = lambda k, lo, hi: tab[:, k, :, lo:hi].unsqueeze(2).broadcast_to([P, T, 6, hi - lo])
                tc, ts = (v[:].rearrange("p t (h d) -> p t h d", d=16) for v in (t_cos, t_sin))
                nc.vector.tensor_tensor(tc, of, cs(0, 0, 16), ALU.mult).then_inc(rope_step, 1)
                nc.vector.tensor_tensor(ts[:, :, :, 0:8], of[:, :, :, 8:16], cs(1, 0, 8), ALU.mult).then_inc(rope_step, 1)
                nc.vector.tensor_tensor(ts[:, :, :, 8:16], of[:, :, :, 0:8], cs(1, 8, 16), ALU.mult).then_inc(rope_step, 1)
                wait(dve, rope_step, 6 * b + 3)
                wait(dve, qk_turned, b)
                nc.vector.tensor_tensor(q_n[:, :, 0:C], t_cos[:, :, 0:C], t_sin[:, :, 0:C], ALU.add).then_inc(rope_step, 1)
                two = lambda v: v[:, :, C:96].rearrange("p t (g d) -> p t g d", g=2)
                for e in range(2):
                    nc.vector.tensor_tensor(
                        k_n[:, :, e * C:(e + 1) * C].rearrange("p t (g d) -> p t g d", g=2)[:, :, :, 1:17],
                        two(t_cos), two(t_sin), ALU.add).then_inc(rope_step, 1)

            def parts(b):
                wait(dve, k_high, b + 1)
                wait(dve, k_kept, 4 * b)
                key_parts(nc.vector, k_kept, 4 * b, b, K_all, p_k[:], k_rest[:])

            split_x(0)
            dve.wait_ge(ready, 6)
            with dve.Fori(0, B - 1) as b:
                by_position(b)
                split_x(b + 1)
                parts(b)
            by_position(B - 1)
            parts(B - 1)
            wait(dve, k_kept, 4 * B)

        @block.scalar
        def _(act):
            def keep_x(b):
                wait(act, x_turned, b + 1)
                wait(act, projected, b)
                for k in range(2):
                    nc.scalar.copy(x_T[k][:], p_x[k][:]).then_inc(x_kept, 1)

            def keep_projections(b):
                wait(act, projected, b + 1)
                wait(act, rope_step, 6 * b)
                wait(act, v_kept, b)
                nc.scalar.copy(qkv[:], p_p[:]).then_inc(p_kept, 1)
                wait(act, p_kept, b + 1)
                nc.scalar.copy(V_all[:, bass.ds(b * T, T), 1:33], qkv[:, :, 96:P]).then_inc(v_kept, 1)

            def keep_k(b):
                wait(act, qk_turned, b + 1)
                nc.scalar.copy(K_all[:, 0, bass.ds(b * S, S)], p_k[:]).then_inc(k_high, 1)

            def keep_q(b):
                nc.scalar.copy(Q_all[:, bass.ds(b * S, S)], p_q[0:C]).then_inc(q_kept, 1)

            act.wait_ge(ready, 6)
            keep_x(0)
            keep_projections(0)
            with act.Fori(0, B - 1) as b:
                keep_k(b)
                keep_x(b + 1)
                keep_q(b)
                keep_projections(b + 1)
            keep_k(B - 1)
            keep_q(B - 1)
            wait(act, q_kept, B)
            wait(act, v_kept, B)

        @block.tensor
        def _(pe):
            def turn_x(b):
                wait(pe, x_split, 5 * b + 5)
                wait(pe, x_kept, 2 * b)
                for k in range(2):
                    for t in range(T):
                        mm = nc.tensor.transpose(p_x[k][:, t * P:(t + 1) * P], x_p[k][:, t, :], ident_bf[:])
                mm.then_inc(x_turned, 1)

            def project(b):
                wait(pe, x_kept, 2 * b + 2)
                wait(pe, p_kept, b)
                for t in range(T):
                    for q in range(3):
                        mm = nc.tensor.matmul(p_p[:, t, :], x_T[q // 2][:, t * P:(t + 1) * P], w_s[:, q],
                                              start=(q == 0), stop=(q == 2))
                mm.then_inc(projected, 1)

            def turn_qk(b):
                wait(pe, rope_step, 6 * b + 6)
                wait(pe, q_kept, b)
                wait(pe, k_high, b)
                wait(pe, k_kept, 4 * b)
                for t in range(T):
                    nc.tensor.transpose(p_k[:, t * P:(t + 1) * P], k_n[:, t, :], ident[:])
                    mm = nc.tensor.transpose(p_q[:, t * P:(t + 1) * P], q_n[:, t, :], ident[:])
                mm.then_inc(qk_turned, 1)

            pe.wait_ge(w_split, 6)
            turn_x(0)
            project(0)
            with pe.Fori(0, B - 1) as b:
                turn_qk(b)
                turn_x(b + 1)
                project(b + 1)
            turn_qk(B - 1)


def sampling_points(nc, tag, d, ident_bf, Q_all, I_all, F_all):
    G = 16
    N = C + G
    with ExitStack() as ctx:
        m = Scope(nc, ctx, tag + "s")
        patch = [m.sb(f"patch{u}", [P, T, 4, C]) for u in range(2)]
        f_ref = m.sb("f_ref", [P, T, 4])
        ref = m.sb("ref", [P, T, 2])
        half = m.sb("half", [P, T, 2, C])
        feat, rest = m.sb("feat", [P, T, C]), m.sb("rest", [P, T, C])
        x_p = [m.sb(f"x_p{k}", [P, T, P], BF16) for k in range(2)]
        x_T = [m.sb(f"x_T{k}", [P, S], BF16) for k in range(2)]
        w_raw, w_rest = m.sb("w_raw", [P, N]), m.sb("w_rest", [P, N])
        w_s, w_lo = m.sb("w_s", [P, 3, N], BF16), m.sb("w_lo", [P, N], BF16)
        o_raw, o_rest, o_sum = m.sb("o_raw", [P, G]), m.sb("o_rest", [P, G]), m.sb("o_sum", [P, 3, G])
        o_p = m.sb("o_p", [P, 3, G], BF16)
        o_s = m.sb("o_s", [P, G], BF16)
        o_rows = m.sb("o_rows", [P, 3])
        rows = m.sb("rows", [P, 4, G])
        o, cen, sq, lin = (m.sb(n, [P, NT, G]) for n in ("o", "cen", "sq", "lin"))
        mean, ssq, std, rstd = (m.sb(n, [P, NT]) for n in ("mean", "ssq", "std", "rstd"))
        h, h_rest = m.sb("h", [P, NT, G]), m.sb("h_rest", [P, NT, G])
        h_p = m.sb("h_p", [P, NT, P], BF16)
        h_T = [m.sb(f"h_T{u}", [P, S], BF16) for u in range(2)]
        eps = m.sb("eps", [P, 1])
        xy, lo, up, fr, om = (m.sb(n, [P, NT, 8, 2]) for n in ("xy", "lo", "up", "fr", "om"))
        whole = m.sb("whole", [P, NT, 8, 2], I32)
        row, base = m.sb("row", [P, NT, 8]), m.sb("base", [P, NT, 8])
        p_x = [m.ps(f"p_x{k}", [P, S], BF16) for k in range(2)]
        p_p = m.ps("p_p", [P, T, P])
        p_h = [m.ps(f"p_h{u}", [P, S], BF16) for u in range(2)]
        p_o = [m.ps(f"p_o{u}", [P, T, G]) for u in range(2)]
        ready, loaded, split_w, split_o = (m.sem(n) for n in ("ready", "loaded", "split_w", "split_o"))
        patch_in = [m.sem(f"patch_in{u}") for u in range(2)]
        step = m.sem("step")
        rooted, bent = m.sem("rooted"), m.sem("bent")
        (parts,
         x_turned, x_kept, projected, p_kept, o_kept,
         ) = m.counts("parts x_turned x_kept projected p_kept o_kept")
        patch_read = m.counts("patch_read0 patch_read1")
        h_turned = m.counts("h_turned0 h_turned1")
        h_kept = m.counts("h_kept0 h_kept1")
        offset = m.counts("offset0 offset1")
        biased = m.counts("biased0 biased1")
        block = m.block()
        NF = 7
        names = ["o", "sum", "mean", "cen", "sq", "ssq", "rstd", "unit", "scaled", "lin",
                 "h_hi", "h_rest", "h_mid", "h_lo", "h_hi2", "h_mid2", "h_hi3",
                 "moved", "placed", "unit2", "grown", "clipped", "whole", "back", "over",
                 "floor", "cap", "fr", "om", "row", "row_b", "idx0", "idx", "f00", "f01", "f10", "f11"]
        at = {n: k + 1 for k, n in enumerate(names)}

        @block.sync
        def _(sp):
            loads = [(w_raw[k * C:(k + 1) * C], d["w_qo"]) for k in range(2)]
            loads += [(o_raw[k * G:(k + 1) * G], d["w_o2"]) for k in range(6)]
            loads += [(rows[:, k], d[n].broadcast_to([P, G])) for k, n in enumerate(("b_o1", "ln_g", "ln_b", "b_o2"))]
            loads += [(f_ref[:], d["f_ref"]), (ref[:], d["ref"]), (o_rows[:], d["o_rows"])]
            assert len(loads) == 15
            sp.wait_ge(ready, 1)
            for dst, src in loads:
                sp.dma_start(dst, src).then_inc(loaded, 16)
            with sp.Fori(0, B // 2) as g:
                for u in range(2):
                    wait(sp, patch_read[u], g)
                    src = d["patches"][bass.ds((2 * g + u) * S, S), :].rearrange("(t p) c -> p t c", p=P)
                    sp.dma_start(patch[u][:].rearrange("p t k c -> p t (k c)"), src).then_inc(patch_in[u], 16)

        @block.gpsimd
        def _(pool):
            nc.gpsimd.memset(o_raw[:], 0.0).then_inc(ready, 1)
            nc.gpsimd.memset(eps[:], EPS).then_inc(ready, 1)
            nc.gpsimd.memset(h_p[:], 0.0).then_inc(ready, 1)
            nc.gpsimd.iota(base[:], pattern=[[(WD - 1) * WD, B], [0, T], [0, 8]], base=0, channel_multiplier=0,
                           allow_small_or_imprecise_dtypes=True).then_inc(ready, 1)

        @block.vector
        def _(dve):
            dve.wait_ge(ready, 1)
            dve.wait_ge(loaded, 16 * 15)
            split(nc.vector, split_w, 0, w_s[:, 0], w_s[:, 1], w_lo[:], w_raw[:], w_rest[:])
            dve.wait_ge(split_w, 4)
            nc.vector.tensor_copy(w_s[0:C, 2], w_lo[0:C]).then_inc(split_w, 1)
            nc.vector.tensor_copy(w_s[C:P, 2], w_s[C:P, 0]).then_inc(split_w, 1)
            split(nc.vector, split_o, 0, o_p[:, 0], o_p[:, 1], o_p[:, 2], o_raw[:], o_rest[:])
            dve.wait_ge(split_o, 4)
            nc.vector.tensor_tensor(o_sum[:], o_p[:], o_rows[:].unsqueeze(2).broadcast_to([P, 3, G]),
                                    ALU.mult).then_inc(split_o, 1)
            dve.wait_ge(split_o, 5)
            nc.vector.tensor_tensor(o_sum[:, 0], o_sum[:, 0], o_sum[:, 1], ALU.add).then_inc(split_o, 1)
            dve.wait_ge(split_o, 6)
            nc.vector.tensor_tensor(o_s[:], o_sum[:, 0], o_sum[:, 2], ALU.add).then_inc(split_o, 1)

            tt, ts = nc.vector.tensor_tensor, nc.vector.tensor_scalar
            with dve.Fori(0, B // 2) as g:
                for u in range(2):
                    b = 2 * g + u
                    dve.wait_ge(patch_in[u], (g + 1) * 16)
                    tt(patch[u][:], patch[u][:], f_ref[:].unsqueeze(3).broadcast_to([P, T, 4, C]),
                       ALU.mult).then_inc(parts, 1)
                    wait(dve, parts, NF * b + 1)
                    tt(half[:], patch[u][:, :, 0:2], patch[u][:, :, 2:4], ALU.add).then_inc(patch_read[u], 1)
                    wait(dve, patch_read[u], g + 1)
                    tt(feat[:], half[:, :, 0], half[:, :, 1], ALU.add).then_inc(parts, 1)
                    wait(dve, parts, NF * b + 2)
                    wait(dve, x_turned, b)
                    split(nc.vector, parts, NF * b + 2 + 1, x_p[0][:, :, 0:C], x_p[0][:, :, C:P],
                          x_p[1][:, :, C:P], feat[:], rest[:])
                    nc.vector.tensor_copy(x_p[1][:, :, 0:C], x_p[0][:, :, 0:C]).then_inc(parts, 1)

            def do(name, ins, settle=True):
                ins.then_inc(step, 1)
                assert at[name] == do.n + 1, name
                do.n += 1
                if settle:
                    dve.wait_ge(step, do.n)

            do.n = 0
            on = lambda k: rows[:, k].unsqueeze(1).broadcast_to([P, NT, G])
            along = lambda v, n: v[:].unsqueeze(2).broadcast_to([P, NT, n])
            wait(dve, p_kept, B)
            do("o", tt(o[:], lin[:], on(0), ALU.add))
            do("sum", nc.vector.tensor_reduce(mean[:], o[:], AX.X, ALU.add))
            do("mean", ts(mean[:], mean[:], 1.0 / G, None, ALU.mult))
            do("cen", tt(cen[:], o[:], along(mean, G), ALU.subtract))
            do("sq", tt(sq[:], cen[:], cen[:], ALU.mult))
            do("ssq", nc.vector.tensor_reduce(ssq[:], sq[:], AX.X, ALU.add))
            dve.wait_ge(rooted, 1)
            do("rstd", nc.vector.reciprocal(rstd[:], std[:]))
            do("unit", tt(o[:], cen[:], along(rstd, G), ALU.mult))
            do("scaled", tt(sq[:], o[:], on(1), ALU.mult))
            do("lin", tt(cen[:], sq[:], on(2), ALU.add))
            dve.wait_ge(bent, 1)
            dve.wait_ge(ready, 4)
            part = lambda k: h_p[:, :, k * G:(k + 1) * G]
            split(nc.vector, step, at["lin"], part(0), part(1), part(2), h[:], h_rest[:])
            for k, src in ((3, 0), (4, 1), (5, 0)):
                nc.vector.tensor_copy(part(k), part(src)).then_inc(step, 1)
            do.n += 7
            flat = lambda v: v.rearrange("p t n k -> p t (n k)")
            with dve.Fori(0, B // 2) as g:
                for u in range(2):
                    wait(dve, offset[u], g + 1)
                    tt(flat(xy[:, bass.ds((2 * g + u) * T, T)]), p_o[u][:], rows[:, 3].unsqueeze(1).broadcast_to([P, T, G]),
                       ALU.add).then_inc(biased[u], 1)
            for u in range(2):
                wait(dve, biased[u], B // 2)
            do("moved", ts(xy[:], xy[:], OFFSET_SCALE, 2.0 / (WD - 1), ALU.mult, ALU.mult))
            for t in range(T):
                here = xy[:].rearrange("p (b t) n k -> p b t n k", b=B)[:, :, t]
                ins = tt(here, here, ref[:, t].unsqueeze(1).unsqueeze(1).broadcast_to([P, B, 8, 2]), ALU.add)
            do("placed", ins)
            do("unit2", ts(xy[:], xy[:], 1.0, 0.5, ALU.add, ALU.mult))
            do("grown", ts(xy[:], xy[:], float(WD - 1), 0.0, ALU.mult, ALU.max))
            do("clipped", ts(xy[:], xy[:], float(WD - 1), None, ALU.min))
            do("whole", nc.vector.tensor_copy(whole[:], xy[:]))
            do("back", nc.vector.tensor_copy(lo[:], whole[:]))
            do("over", tt(up[:], lo[:], xy[:], ALU.is_gt))
            do("floor", tt(lo[:], lo[:], up[:], ALU.subtract))
            do("cap", ts(lo[:], lo[:], float(WD - 2), None, ALU.min))
            do("fr", tt(fr[:], xy[:], lo[:], ALU.subtract))
            do("om", ts(om[:], fr[:], -1.0, 1.0, ALU.mult, ALU.add))
            do("row", ts(row[:], lo[:, :, :, 1], float(WD), None, ALU.mult))
            do("row_b", tt(row[:], row[:], base[:], ALU.add))
            do("idx0", tt(row[:], row[:], lo[:, :, :, 0], ALU.add))
            do("idx", nc.vector.tensor_copy(I_all[:], row[:]), False)
            for n, (fx, fy) in enumerate(((om, om), (om, fr), (fr, om), (fr, fr))):
                do(f"f{n // 2}{n % 2}", tt(F_all[:, :, :, n], fx[:, :, :, 0], fy[:, :, :, 1], ALU.mult), n == 3)

        @block.scalar
        def _(act):
            with act.Fori(0, B) as b:
                wait(act, x_turned, b + 1)
                wait(act, projected, b)
                for k in range(2):
                    nc.scalar.copy(x_T[k][:], p_x[k][:]).then_inc(x_kept, 1)
                wait(act, projected, b + 1)
                nc.scalar.copy(lin[:, bass.ds(b * T, T), :], p_p[:, :, C:N]).then_inc(p_kept, 1)
                nc.scalar.copy(Q_all[:, bass.ds(b * T, T), :], p_p[:, :, 0:C]).then_inc(o_kept, 1)
            act.wait_ge(ready, 2)
            act.wait_ge(step, at["ssq"])
            nc.scalar.activation(std[:], ssq[:], ACT.Sqrt, bias=eps[:], scale=1.0 / G).then_inc(rooted, 1)
            act.wait_ge(step, at["lin"])
            nc.scalar.activation(h[:], cen[:], ACT.Gelu_apprx_tanh).then_inc(bent, 1)
            with act.Fori(0, B // 2) as g:
                for u in range(2):
                    wait(act, h_turned[u], g + 1)
                    wait(act, offset[u], g)
                    nc.scalar.copy(h_T[u][:], p_h[u][:]).then_inc(h_kept[u], 1)
            wait(act, o_kept, B)

        @block.tensor
        def _(pe):
            pe.wait_ge(split_w, 6)
            with pe.Fori(0, B) as b:
                wait(pe, parts, NF * b + NF)
                wait(pe, x_kept, 2 * b)
                for k in range(2):
                    for t in range(T):
                        mm = nc.tensor.transpose(p_x[k][:, t * P:(t + 1) * P], x_p[k][:, t, :], ident_bf[:])
                mm.then_inc(x_turned, 1)
                wait(pe, x_kept, 2 * b + 2)
                wait(pe, o_kept, b)
                for t in range(T):
                    for q in range(3):
                        mm = nc.tensor.matmul(p_p[:, t, 0:N], x_T[q // 2][:, t * P:(t + 1) * P], w_s[:, q],
                                              start=(q == 0), stop=(q == 2))
                mm.then_inc(projected, 1)
            pe.wait_ge(split_o, 7)
            pe.wait_ge(step, at["h_hi3"])

            def turn(g, u):
                wait(pe, h_kept[u], g)
                for t in range(T):
                    mm = nc.tensor.transpose(p_h[u][:, t * P:(t + 1) * P],
                                             h_p[:, bass.ds((2 * g + u) * T + t, 1), :].rearrange("p a c -> p (a c)"),
                                             ident_bf[:])
                mm.then_inc(h_turned[u], 1)

            def offsets(g, u):
                wait(pe, h_kept[u], g + 1)
                wait(pe, biased[u], g)
                for t in range(T):
                    mm = nc.tensor.matmul(p_o[u][:, t, :], h_T[u][:, t * P:(t + 1) * P], o_s[:], start=True, stop=True)
                mm.then_inc(offset[u], 1)

            turn(0, 0)
            with pe.Fori(0, B // 2 - 1) as g:
                turn(g, 1)
                offsets(g, 0)
                turn(g + 1, 0)
                offsets(g, 1)
            g = B // 2 - 1
            turn(g, 1)
            offsets(g, 0)
            offsets(g, 1)


def deformable_attention(nc, tag, d, ident, Q_all, I_all, F_all, hid, fetched, beside):
    U = 4
    R = len(fetched)
    NP = 8
    with ExitStack() as ctx:
        m = Scope(nc, ctx, tag + "d")
        put_beside = beside(ctx)
        patch = [m.sb(f"patch{r}", [P, NP, 4 * C]) for r in range(R)]
        rows = [m.sb(f"rows{r}", [P, NP], I32) for r in range(R)]
        half = m.sb("half", [P, NP, 2 * C])
        point = [m.sb(f"point{r}", [P, NP, C]) for r in range(2)]
        p_sb = [m.sb(f"p_sb{r}", [P, NP // 2, P]) for r in range(2)]
        w_kv = m.sb("w_kv", [P, 2, 2 * C])
        prod = m.sb("prod", [P, NP, C])
        score = m.sb("score", [P, U, NP, NP])
        top, tot = m.sb("top", [P, U, NP]), m.sb("tot", [P, U, NP])
        shifted, ex, attn = (m.sb(n, [P, U, NP, NP]) for n in ("shifted", "ex", "attn"))
        val = [m.sb(f"val{k}", [P, NP, C]) for k in range(U)]
        p_t = [m.ps(f"p_t{r}", [P, NP // 2, P]) for r in range(2)]
        p_kv = [m.ps(f"p_kv{r}", [P, NP, 2 * C]) for r in range(2)]
        ready, loaded = m.sem("ready"), m.sem("loaded")
        (step,
         ended,
         rows_set, turned, t_kept, projected, v_kept, raised,
         ) = m.counts("step ended rows_set turned t_kept projected v_kept raised")
        freed = m.counts(" ".join(f"freed{r}" for r in range(R)))
        block = m.block()
        put_beside(block)
        names = []
        for k in range(U):
            names += [f"prod{k}", f"point{k}"]
            if k:
                names += [f"qk{k - 1}", f"score{k - 1}"]
        end_names = [f"qk{U - 1}", f"score{U - 1}", "top", "shifted", "tot", "rtot", "attn"]
        for k in range(U):
            end_names += [f"av{k}", f"out{k}"]
        at = {n: k + 1 for k, n in enumerate(names)}
        end_at = {n: k + 1 for k, n in enumerate(end_names)}
        NV, NE = len(names), len(end_names)
        PASSES = NT // U

        @block.sync
        def _(sp):
            sp.wait_ge(ready, 1)
            for e in range(2):
                sp.dma_start(w_kv[e * C:(e + 1) * C, e], d["w_kv"]).then_inc(loaded, 16)

        @block.gpsimd
        def _(pool):
            nc.gpsimd.memset(w_kv[:], 0.0).then_inc(ready, 1)
            with pool.Fori(0, PASSES) as g:
                for k in range(U):
                    wait(pool, freed[k], g)
                    nc.gpsimd.tensor_copy(rows[k][:], I_all[:, bass.ds(g * U + k, 1), :].rearrange("p a n -> p (a n)")).then_inc(rows_set, 1)
                    wait(pool, rows_set, g * U + k + 1)
                    nc.gpsimd.nop(nofuse=True)
                    for n in range(NP):
                        nc.gpsimd.indirect_dma_start(
                            out=patch[k][:, n, :], out_offset=None, in_=d["pixels"],
                            in_offset=bass.IndirectOffsetOnAxis(ap=rows[k][:, n:n + 1], axis=0),
                        ).then_inc(fetched[k], 16)

        @block.vector
        def _(dve):
            tt = nc.vector.tensor_tensor

            def sample(g, k):
                dve.wait_ge(fetched[k], (g + 1) * (16 * NP))
                f = F_all[:, bass.ds(g * U + k, 1), :, :].rearrange("p a n k -> p (a n k)")
                x = patch[k][:].rearrange("p n (k c) -> p (n k) c", c=C)
                tt(x, x, f.unsqueeze(2).broadcast_to([P, 4 * NP, C]), ALU.mult).then_inc(step, 1)
                wait(dve, step, g * NV + at[f"prod{k}"])
                tt(half[:], patch[k][:, :, 0:2 * C], patch[k][:, :, 2 * C:4 * C], ALU.add).then_inc(freed[k], 1)
                wait(dve, freed[k], g + 1)
                wait(dve, turned, g * U + max(k - 1, 0))
                tt(point[k % 2][:], half[:, :, 0:C], half[:, :, C:2 * C], ALU.add).then_inc(step, 1)

            def scores(g, k, sem, done):
                wait(dve, v_kept, g * U + k + 1)
                q = Q_all[:, bass.ds(g * U + k, 1), :].broadcast_to([P, NP, C])
                tt(prod[:], p_kv[k % 2][:, :, 0:C], q, ALU.mult).then_inc(sem, 1)
                wait(dve, sem, done + 1)
                nc.vector.tensor_reduce(score[:, k].rearrange("p n h -> p (n h)"),
                                        prod[:].rearrange("p n (h d) -> p (n h) d", h=NP), AX.X, ALU.add).then_inc(sem, 1)

            def go_on(g):
                for k in range(1, U):
                    sample(g, k)
                    if k == 1:
                        wait(dve, ended, g * NE)
                    else:
                        wait(dve, step, g * NV + at[f"score{k - 2}"])
                    scores(g, k - 1, step, g * NV + at[f"qk{k - 1}"] - 1)

            def end(g):
                def after(name):
                    wait(dve, ended, g * NE + end_at[name])

                def do(name, ins):
                    ins.then_inc(ended, 1)
                    assert end_at[name] == do.n + 1, name
                    do.n += 1

                wait(dve, step, g * NV + NV)
                scores(g, U - 1, ended, g * NE)
                do.n = 2
                after(f"score{U - 1}")
                do("top", nc.vector.tensor_reduce(top[:], score[:].rearrange("p t n h -> p t h n"), AX.X, ALU.max))
                after("top")
                do("shifted", tt(shifted[:], score[:], top[:].unsqueeze(2).broadcast_to([P, U, NP, NP]), ALU.subtract))
                wait(dve, raised, g + 1)
                do("tot", nc.vector.tensor_reduce(tot[:], ex[:].rearrange("p t n h -> p t h n"), AX.X, ALU.add))
                after("tot")
                do("rtot", nc.vector.reciprocal(tot[:], tot[:]))
                after("rtot")
                do("attn", tt(attn[:], ex[:], tot[:].unsqueeze(2).broadcast_to([P, U, NP, NP]), ALU.mult))
                after("attn")
                for k in range(U):
                    v = val[k][:].rearrange("p n (h d) -> p (n h) d", h=NP)
                    do(f"av{k}", tt(v, v, attn[:, k].rearrange("p n h -> p (n h)").unsqueeze(2).broadcast_to([P, NP * NP, C // NP]),
                                    ALU.mult))
                    after(f"av{k}")
                    do(f"out{k}", nc.vector.tensor_reduce(
                        hid[:, bass.ds(g * U + k, 1), :].rearrange("p a c -> p (a c)"),
                        val[k][:].rearrange("p n c -> p c n"), AX.X, ALU.add))

            sample(0, 0)
            go_on(0)
            with dve.Fori(0, PASSES - 1) as g:
                sample(g + 1, 0)
                end(g)
                go_on(g + 1)
            end(PASSES - 1)
            wait(dve, ended, NE * PASSES)

        @block.scalar
        def _(act):
            def points(g, k):
                wait(act, turned, g * U + k + 1)
                wait(act, projected, g * U + max(k - 1, 0))
                nc.scalar.copy(p_sb[k % 2][:], p_t[k % 2][:]).then_inc(t_kept, 1)

            def values(g, k):
                wait(act, projected, g * U + k + 1)
                if k == 0:
                    wait(act, ended, g * NE)
                nc.scalar.copy(val[k][:], p_kv[k % 2][:, :, C:2 * C]).then_inc(v_kept, 1)

            def raise_scores(g):
                wait(act, ended, g * NE + end_at["shifted"])
                nc.scalar.activation(ex[:], shifted[:], ACT.Exp, scale=float((C // NP) ** -0.5)).then_inc(raised, 1)

            def go_on(g):
                values(g, 0)
                for k in range(1, U):
                    points(g, k)
                    values(g, k)

            points(0, 0)
            go_on(0)
            with act.Fori(0, PASSES - 1) as g:
                points(g + 1, 0)
                raise_scores(g)
                go_on(g + 1)
            raise_scores(PASSES - 1)

        @block.tensor
        def _(pe):
            pe.wait_ge(loaded, 32)
            with pe.Fori(0, PASSES) as g:
                for k in range(U):
                    i = g * U + k
                    r = k % 2
                    wait(pe, step, g * NV + at[f"point{k}"])
                    wait(pe, t_kept, g * U + max(k - 1, 0))
                    for j in range(NP // 2):
                        mm = nc.tensor.transpose(p_t[r][:, j, :], point[r][:, 2 * j:2 * j + 2, :].rearrange("p n c -> p (n c)"),
                                                 ident[:])
                    mm.then_inc(turned, 1)
                    wait(pe, t_kept, i + 1)
                    if k == 1:
                        wait(pe, ended, g * NE)
                    if k >= 2:
                        wait(pe, step, g * NV + at[f"qk{k - 2}"])
                    for j in range(NP // 2):
                        mm = nc.tensor.matmul(p_kv[r][:, 2 * j:2 * j + 2, :], p_sb[r][:, j, :],
                                              w_kv[:].rearrange("p e n -> p (e n)"), start=True, stop=True)
                    mm.then_inc(projected, 1)


def gates(nc, tag, kind, hid, xn, ident_bf, router, X_all, G_all):
    layer = kind == "layer"
    with ExitStack() as ctx:
        m = Scope(nc, ctx, tag + "g")
        rest = m.sb("rest", [P, T, C])
        x_hm = [m.sb(f"x_hm{u}", [P, T, P], BF16) for u in range(2)]
        x_hl = [m.sb(f"x_hl{u}", [P, T, P], BF16) for u in range(2)]
        w_raw = m.sb("w_raw", [P, E])
        w_rest = m.sb("w_rest", [P, E])
        w_s = m.sb("w_s", [P, 3, E], BF16)
        w_lo = m.sb("w_lo", [P, E], BF16)
        logits, ex, prob, others, eq, named, gate, g_rest = (m.sb(n, [P, NT, E]) for n in (
            "logits", "ex", "prob", "others", "eq", "named", "gate", "g_rest"))
        top, tot, rtot, norm, rnorm = (m.sb(n, [P, NT]) for n in ("top", "tot", "rtot", "norm", "rnorm"))
        best = m.sb("best", [P, 2, NT])
        lead = m.sb("lead", [P, 2, NT])
        rank = m.sb("rank", [P, NT, E])
        hit = m.sb("hit", [P, 2, NT, E])
        g_s = m.sb("g_s", [P, NT, P], BF16)
        p_t = [m.ps(f"p_t{u}", [P, 2, S], BF16) for u in range(2)]
        p_l = [m.ps(f"p_l{u}", [P, T, E]) for u in range(2)]
        p_g = [m.ps(f"p_g{u}", [P, S], BF16) for u in range(2)]
        (x_split,
         ) = m.counts("x_split")
        turned = m.counts("turned0 turned1")
        kept = m.counts("kept0 kept1")
        scored = m.counts("scored0 scored1")
        logits_kept = m.counts("logits_kept0 logits_kept1")
        gates_turned = m.counts("gates_turned0 gates_turned1")
        gates_kept = m.counts("gates_kept0 gates_kept1")
        ready, loaded, w_split = m.sem("ready"), m.sem("loaded"), m.sem("w_split")
        step = m.sem("step")
        raised = m.sem("raised")
        joined = m.sem("joined")
        block = m.block()

        @block.sync
        def _(sp):
            for h in range(2):
                sp.dma_start(w_raw[h * C:(h + 1) * C], router).then_inc(loaded, 16)

        @block.gpsimd
        def _(pool):
            nc.gpsimd.memset(g_s[:], 0.0).then_inc(ready, 1)
            nc.gpsimd.iota(rank[:], pattern=[[0, NT], [-1, E]], base=E, channel_multiplier=0,
                           allow_small_or_imprecise_dtypes=True).then_inc(ready, 1)
            pool.wait_ge(ready, 2)
            if layer:
                nc.gpsimd.tensor_tensor(hid[:], hid[:], xn[:], ALU.add).then_inc(joined, 1)
                pool.wait_ge(joined, 1)

        names = ["top", "shifted", "tot", "rtot", "prob", "best0", "eq0", "named0", "lead0", "hit0", "less",
                 "others", "best1", "eq1", "named1", "lead1", "hit1", "norm", "floor", "rnorm",
                 "val0", "val1", "both", "gate", "g_hi", "g_rest", "g_mid", "g_lo", "g_hi2"]
        at = {n: k + 1 for k, n in enumerate(names)}

        @block.vector
        def _(dve):
            dve.wait_ge(loaded, 32)
            split(nc.vector, w_split, 0, w_s[:, 0], w_s[:, 1], w_lo[:], w_raw[:], w_rest[:])
            dve.wait_ge(w_split, 4)
            nc.vector.tensor_copy(w_s[0:C, 2], w_lo[0:C]).then_inc(w_split, 1)
            nc.vector.tensor_copy(w_s[C:P, 2], w_s[C:P, 0]).then_inc(w_split, 1)
            with dve.Fori(0, B // 2) as g:
                for u in range(2):
                    b = 2 * g + u
                    wait(dve, turned[u], g)
                    split(nc.vector, x_split, 5 * b + 1, x_hm[u][:, :, 0:C], x_hm[u][:, :, C:P], x_hl[u][:, :, C:P],
                          xn[:, bass.ds(b * T, T), :], rest[:])
                    nc.vector.tensor_copy(x_hl[u][:, :, 0:C], x_hm[u][:, :, 0:C]).then_inc(x_split, 1)

            def do(name, ins):
                ins.then_inc(step, 1)
                assert at[name] == do.n + 1, name
                do.n += 1
                dve.wait_ge(step, do.n)

            do.n = 0
            tt, ts = nc.vector.tensor_tensor, nc.vector.tensor_scalar
            reduce = nc.vector.tensor_reduce
            along = lambda v: v.unsqueeze(2).broadcast_to([P, NT, E])
            for u in range(2):
                wait(dve, logits_kept[u], B // 2)
            do("top", reduce(top[:], logits[:], AX.X, ALU.max))
            do("shifted", tt(ex[:], logits[:], along(top[:]), ALU.subtract))
            dve.wait_ge(raised, 1)
            do("tot", reduce(tot[:], prob[:], AX.X, ALU.add))
            do("rtot", nc.vector.reciprocal(rtot[:], tot[:]))
            do("prob", tt(prob[:], prob[:], along(rtot[:]), ALU.mult))
            dve.wait_ge(ready, 2)
            for k, p in enumerate((prob, others)):
                do(f"best{k}", reduce(best[:, k], p[:], AX.X, ALU.max))
                do(f"eq{k}", tt(eq[:], p[:], along(best[:, k]), ALU.is_equal))
                do(f"named{k}", tt(named[:], eq[:], rank[:], ALU.mult))
                do(f"lead{k}", reduce(lead[:, k], named[:], AX.X, ALU.max))
                do(f"hit{k}", tt(hit[:, k], rank[:], along(lead[:, k]), ALU.is_equal))
                if k == 0:
                    do("less", ts(eq[:], hit[:, 0], -2.0, None, ALU.mult))
                    do("others", tt(others[:], prob[:], eq[:], ALU.add))
            do("norm", tt(norm[:], best[:, 0], best[:, 1], ALU.add))
            do("floor", ts(norm[:], norm[:], 1e-12 if layer else 1e-9, None, ALU.max if layer else ALU.add))
            do("rnorm", nc.vector.reciprocal(rnorm[:], norm[:]))
            for k in range(2):
                do(f"val{k}", tt(hit[:, k], hit[:, k], along(best[:, k]), ALU.mult))
            do("both", tt(eq[:], hit[:, 0], hit[:, 1], ALU.add))
            do("gate", tt(gate[:], eq[:], along(rnorm[:]), ALU.mult))
            split(nc.vector, step, at["gate"], g_s[:, :, 0:E], g_s[:, :, 32:32 + E],
                  g_s[:, :, 64:64 + E], gate[:], g_rest[:])
            nc.vector.tensor_copy(g_s[:, :, 96:96 + E], g_s[:, :, 0:E]).then_inc(step, 1)
            with dve.Fori(0, B // 2) as g:
                wait(dve, gates_turned[0], g + 1)
                nc.vector.tensor_copy(G_all[:, bass.ds(2 * g * S, S)], p_g[0][:]).then_inc(gates_kept[0], 1)
            wait(dve, gates_kept[0], B // 2)

        @block.scalar
        def _(act):
            def keep(g, u):
                wait(act, turned[u], g + 1)
                for k in range(2):
                    nc.scalar.copy(X_all[:, k, bass.ds((2 * g + u) * S, S)], p_t[u][:, k]).then_inc(kept[u], 1)

            def keep_logits(g, u):
                wait(act, scored[u], g + 1)
                nc.scalar.copy(logits[:, bass.ds((2 * g + u) * T, T), :], p_l[u][:]).then_inc(logits_kept[u], 1)

            keep(0, 0)
            with act.Fori(0, B // 2 - 1) as g:
                keep(g, 1)
                keep_logits(g, 0)
                keep(g + 1, 0)
                keep_logits(g, 1)
            g = B // 2 - 1
            keep(g, 1)
            keep_logits(g, 0)
            keep_logits(g, 1)
            act.wait_ge(step, at["shifted"])
            nc.scalar.activation(prob[:], ex[:], ACT.Exp).then_inc(raised, 1)
            with act.Fori(0, B // 2) as g:
                wait(act, gates_turned[1], g + 1)
                nc.scalar.copy(G_all[:, bass.ds((2 * g + 1) * S, S)], p_g[1][:]).then_inc(gates_kept[1], 1)
            wait(act, gates_kept[1], B // 2)

        @block.tensor
        def _(pe):
            def turn(g, u):
                wait(pe, x_split, 5 * (2 * g + u) + 5)
                wait(pe, kept[u], 2 * g)
                for k, x in enumerate((x_hm[u], x_hl[u])):
                    for t in range(T):
                        mm = nc.tensor.transpose(p_t[u][:, k, t * P:(t + 1) * P], x[:, t, :], ident_bf[:])
                mm.then_inc(turned[u], 1)

            def score(g, u):
                wait(pe, kept[u], 2 * g + 2)
                wait(pe, logits_kept[u], g)
                b = 2 * g + u
                for t in range(T):
                    for k in range(3):
                        mm = nc.tensor.matmul(p_l[u][:, t, :], X_all[:, k // 2, bass.ds(b * S + t * P, P)], w_s[:, k],
                                              start=(k == 0), stop=(k == 2))
                mm.then_inc(scored[u], 1)

            pe.wait_ge(w_split, 6)
            turn(0, 0)
            with pe.Fori(0, B // 2 - 1) as g:
                turn(g, 1)
                score(g, 0)
                turn(g + 1, 0)
                score(g, 1)
            g = B // 2 - 1
            turn(g, 1)
            score(g, 0)
            score(g, 1)
            pe.wait_ge(step, at["g_hi2"])
            with pe.Fori(0, B // 2) as g:
                for u in range(2):
                    wait(pe, gates_kept[u], g)
                    for t in range(T):
                        mm = nc.tensor.transpose(p_g[u][:, t * P:(t + 1) * P],
                                                 g_s[:, bass.ds((2 * g + u) * T + t, 1), :].rearrange("p a c -> p (a c)"),
                                                 ident_bf[:])
                    mm.then_inc(gates_turned[u], 1)


def experts(nc, tag, kind, hid, ident, w, X_all, G_all):
    gelu = kind == "gelu"
    hidden = w["w2"].shape[0]
    NK = (hidden + P - 1) // P
    full, over = hidden // P, hidden % P
    CH = 512
    NCH = B * S // CH
    J = CH // P
    RG = 4
    uses = [len(range(r, NK, RG)) for r in range(RG)]
    pairs = [list(range(k, min(k + 2, NK))) for k in range(0, NK, 2)]
    left = [p for p in pairs if p[0] + 3 >= NK]
    with ExitStack() as ctx:
        m = Scope(nc, ctx, tag + "e")
        NW = 1 if gelu else 2
        w_raw = m.sb("w_raw", [P, NK * P])
        w_rest = m.sb("w_rest", [P, NK * P])
        w_lo = m.sb("w_lo", [P, NK * P], BF16)
        w_in = [[m.sb(f"w_in{n}{k}", [P, NK * P], BF16) for k in range(3)] for n in range(NW)]
        w2 = m.sb("w2", [P, NK, C])
        two = m.sb("two", [P, C])
        b1 = m.sb("b1", [P, NK]) if gelu else None
        b2_raw = m.sb("b2_raw", [P, C])
        b2_rest = m.sb("b2_rest", [P, C])
        b2_part = m.sb("b2_part", [P, 3, C], BF16)
        b2 = m.sb("b2", [P, 2, P], BF16)
        spread_raw = m.sb("spread_raw", [P, NK * P])
        spread = m.sb("spread", [P, NK * P], BF16)
        act_h = m.sb("act_h", [P, 2, CH])
        up = m.sb("up", [P, 2, CH])
        gated = m.sb("gated", [P, RG, CH])
        yT = m.sb("yT", [P, CH])
        p_a = [m.ps(f"p_a{r}", [P, CH]) for r in range(2)]
        p_b = [m.ps(f"p_b{r}", [P, CH]) for r in range(2)]
        p_g = [m.ps(f"p_g{r}", [P, CH]) for r in range(2)]
        p_y = m.ps("p_y", [P, CH])
        p_o = m.ps("p_o", [P, J, C])
        (a_made,
         b_made,
         act_done,
         up_done,
         gated_done,
         y_kept,
         turned,
         added,
         ) = m.counts("a_made b_made act_done up_done gated_done y_kept turned added")
        used = m.counts(" ".join(f"used{r}" for r in range(RG)))
        loaded, loaded3, zeroed, w_split, b_split = (m.sem(n) for n in
                                                     ("loaded", "loaded3", "zeroed", "w_split", "b_split"))
        block = m.block()
        loads = [(spread_raw[k * 32:k * 32 + E, 0:hidden], w["spread"]) for k in range(3)]
        loads.append((w2[:, 0:full, :], w["w2"][0:full * P, :].rearrange("(k p) c -> p k c", p=P)))
        loads += [(w_raw[h * C:(h + 1) * C, 0:hidden], w["w1"]) for h in range(2)]
        if over:
            loads.append((w2[0:over, full, :], w["w2"][full * P:hidden, :]))
        if gelu:
            loads.append((b1[:], w["b1"]))
            loads += [(b2_raw[k * 32:k * 32 + E], w["b2"]) for k in range(4)]
        zeroing = [spread_raw, w_raw, w2, b2_raw, b2]

        @block.sync
        def _(sp):
            sp.wait_ge(zeroed, len(zeroing))
            for dst, src in loads:
                sp.dma_start(dst, src).then_inc(loaded, 16)
            if not gelu:
                sp.wait_ge(w_split, 6)
                for h in range(2):
                    sp.dma_start(w_raw[h * C:(h + 1) * C, 0:hidden], w["w3"]).then_inc(loaded3, 16)

        @block.gpsimd
        def _(pool):
            for x in zeroing:
                nc.gpsimd.memset(x[:], 0.0).then_inc(zeroed, 1)

        @block.tensor
        def _(pe):
            pe.wait_ge(w_split, 6 * NW)
            pe.wait_ge(b_split, 10 if gelu else 3)

            def first(out, w, n, k):
                for q in range(3):
                    mm = nc.tensor.matmul(out, w[q][:, k * P:(k + 1) * P], X_all[:, q // 2, bass.ds(n * CH, CH)],
                                          start=(q == 0), stop=(q == 2))
                return mm

            def tile(n, k):
                u = k % 2
                last = n * NK + max(k - 1, 0)
                wait(pe, act_done, last)
                first(p_a[u][:], w_in[0], n, k).then_inc(a_made, 1)
                wait(pe, gated_done, last)
                if not gelu:
                    first(p_b[u][:], w_in[1], n, k)
                nc.tensor.matmul(p_g[u][:], spread[:, k * P:(k + 1) * P], G_all[:, bass.ds(n * CH, CH)],
                                 start=True, stop=True).then_inc(b_made, 1)

            def sums(n, pair):
                if pair[0] == 0:
                    wait(pe, y_kept, n)
                    if gelu:
                        for q in range(2):
                            nc.tensor.matmul(p_y[:], b2[:, q], G_all[:, bass.ds(n * CH, CH)], start=(q == 0), stop=False)
                wait(pe, gated_done, n * NK + pair[-1] + 1)
                for k in pair:
                    e = k % 2
                    mm = nc.tensor.matmul(p_y[e * C:(e + 1) * C], w2[:, k, :], gated[:, k % RG, :],
                                          start=(k < 2 and not gelu), stop=(k >= NK - 2))
                    mm.then_inc(used[k % RG], 1)

            def turn(n):
                wait(pe, y_kept, n + 1)
                wait(pe, added, n)
                for j in range(J):
                    mm = nc.tensor.matmul(p_o[:, j, :], yT[:, j * P:(j + 1) * P], two[:], start=True, stop=True)
                mm.then_inc(turned, 1)

            def chunk(n, before=None):
                rest = list(left) if before is not None else []
                if rest and NK % 2:
                    sums(before, rest.pop(0))
                for k in range(NK):
                    tile(n, k)
                    if rest:
                        sums(before, rest.pop(0))
                    elif k == 2 and before is not None:
                        turn(before)
                    if k >= 3 and k % 2:
                        sums(n, pairs[(k - 3) // 2])

            chunk(0)
            with pe.Fori(0, NCH - 1) as n:
                chunk(n + 1, n)
            for pair in left:
                sums(NCH - 1, pair)
            turn(NCH - 1)

        @block.scalar
        def _(act):
            act.wait_ge(loaded, 16 * len(loads))

            def keep(n):
                for k in pairs[-1] if len(pairs[-1]) == 2 else pairs[-2][1:] + pairs[-1]:
                    wait(act, used[k % RG], n * uses[k % RG] + k // RG + 1)
                wait(act, turned, n)
                nc.scalar.copy(yT[:], p_y[:]).then_inc(y_kept, 1)

            def chunk(n, before=None):
                for k in range(NK):
                    u = k % 2
                    wait(act, a_made, n * NK + k + 1)
                    wait(act, gated_done if gelu else up_done, n * NK + max(k - 1, 0))
                    if gelu:
                        nc.scalar.activation(act_h[:, u, :], p_a[u][:], ACT.Gelu,
                                             bias=b1[:, k:k + 1]).then_inc(act_done, 1)
                    else:
                        nc.scalar.activation(act_h[:, u, :], p_a[u][:], ACT.Silu).then_inc(act_done, 1)
                    if k == 1 and before is not None:
                        keep(before)

            chunk(0)
            with act.Fori(0, NCH - 1) as n:
                chunk(n + 1, n)
            keep(NCH - 1)

        @block.vector
        def _(dve):
            for n in range(NW):
                dve.wait_ge(loaded if n == 0 else loaded3, 16 * len(loads) if n == 0 else 32)
                split(nc.vector, w_split, 6 * n, w_in[n][0][:], w_in[n][1][:], w_lo[:], w_raw[:], w_rest[:])
                dve.wait_ge(w_split, 6 * n + 4)
                nc.vector.tensor_copy(w_in[n][2][0:C], w_lo[0:C]).then_inc(w_split, 1)
                nc.vector.tensor_copy(w_in[n][2][C:P], w_in[n][0][C:P]).then_inc(w_split, 1)
                dve.wait_ge(w_split, 6 * n + 6)
            nc.vector.tensor_copy(two[0:C], ident[0:C, 0:C]).then_inc(b_split, 1)
            nc.vector.tensor_copy(two[C:P], ident[C:P, C:P]).then_inc(b_split, 1)
            nc.vector.tensor_copy(spread[:], spread_raw[:]).then_inc(b_split, 1)
            if gelu:
                split(nc.vector, b_split, 3, b2_part[:, 0], b2_part[:, 1], b2_part[:, 2], b2_raw[:], b2_rest[:])
                dve.wait_ge(b_split, 7)
                nc.vector.tensor_copy(b2[0:96, 0, 0:C], b2_part[0:96, 0])
                nc.vector.tensor_copy(b2[96:P, 0, 0:C], b2_part[96:P, 1]).then_inc(b_split, 1)
                nc.vector.tensor_copy(b2[0:32, 1, 0:C], b2_part[0:32, 2]).then_inc(b_split, 1)
                nc.vector.tensor_copy(b2[32:64, 1, 0:C], b2_part[32:64, 1]).then_inc(b_split, 1)

            def add(n):
                wait(dve, turned, n + 1)
                x = hid[:, bass.ds(n * J, J), :]
                nc.vector.tensor_tensor(x, x, p_o[:], ALU.add).then_inc(added, 1)

            def chunk(n, before=None):
                for k in range(NK):
                    u = k % 2
                    wait(dve, act_done, n * NK + k + 1)
                    wait(dve, b_made, n * NK + k + 1)
                    wait(dve, used[k % RG], n * uses[k % RG] + k // RG)
                    if gelu:
                        nc.vector.tensor_tensor(gated[:, k % RG, :], act_h[:, u, :], p_g[u][:],
                                                ALU.mult).then_inc(gated_done, 1)
                    else:
                        nc.vector.tensor_tensor(up[:, u, :], act_h[:, u, :], p_b[u][:],
                                                ALU.mult).then_inc(up_done, 1)
                        wait(dve, up_done, n * NK + k + 1)
                        nc.vector.tensor_tensor(gated[:, k % RG, :], up[:, u, :], p_g[u][:],
                                                ALU.mult).then_inc(gated_done, 1)
                    if k == 2 and before is not None:
                        add(before)

            chunk(0)
            with dve.Fori(0, NCH - 1) as n:
                chunk(n + 1, n)
            add(NCH - 1)
            wait(dve, added, NCH)


def build(nc, ins, out, stages):
    with ExitStack() as ctx:
        g = Scope(nc, ctx, "g")
        hid = g.sb("hid", [P, NT, C])
        ident = g.sb("ident", [P, P])
        ident_bf = g.sb("ident_bf", [P, P], BF16)
        loaded, made, stored = g.sem("loaded"), g.sem("made"), g.sem("stored")
        summed = g.sem("summed")
        fetched = [g.sem(f"fetched{r}") for r in range(4)]
        with nc.Block() as block:
            @block.gpsimd
            def _(pool):
                nc.gpsimd.memset(ident[:], 0.0).then_inc(made, 1)
                pool.wait_ge(made, 1)
                nc.gpsimd.affine_select(out=ident[:], in_=ident[:], compare_op=ALU.not_equal, fill=1.0,
                                        base=0, pattern=[[-1, P]], channel_multiplier=1).then_inc(made, 1)
                pool.wait_ge(made, 2)
                nc.gpsimd.tensor_copy(ident_bf[:], ident[:]).then_inc(made, 1)
                pool.wait_ge(made, 3)

            @block.sync
            def _(sp):
                if "h" in ins:
                    sp.dma_start(hid[:], ins["h"].rearrange("(t p) c -> p t c", p=P)).then_inc(loaded, 16)
                    sp.wait_ge(loaded, 16)

        def fold(which, sub):
            scopes = [Scope(nc, sub, layers[k][0] + "w") for k in which]
            p_a, p_w = scopes[0].ps("p_a", [C, 8, C]), scopes[0].ps("p_w", [P, 8, C])

            def beside(block):
                for k, m in zip(which, scopes):
                    _, H, scale, w, _ = layers[k]
                    attention_weights(nc, block, m, p_a, p_w, H, scale, w, *made[k])
            return beside

        def attn_layer(k):
            tag, H, _, _, bias_row = layers[k]
            A_all, W_aug = made[k]
            if not folded:
                with ExitStack() as sub:
                    beside = fold([k], sub)
                    beside(sub.enter_context(nc.Block()))
            with ExitStack() as sub:
                m = Scope(nc, sub, tag)
                V_all = m.sb("V_all", [P, NT, C])
                Q_all = m.sb("Q_all", [C, B * S])
                K_all = m.sb("K_all", [P, 3, B * S], BF16)
                normalise(nc, tag + "v", hid, V_all, bias_row=bias_row, one=True)
                channel_major(nc, tag, ident, V_all, Q_all, K_all)
                attention(nc, tag, H, hid, ident_bf, A_all, W_aug, V_all, Q_all, K_all)

        layers = [("l0", 8, 8 ** -0.5, {"q": ins["WQT"], "k": ins["WKT"], "v": ins["WVT"], "o": ins["Wout"],
                                        "bq": None}, ins["bout"]),
                  ("l1", 1, C ** -0.5, {"q": ins["Wq1"], "k": ins["Wk1"], "v": ins["Wv1"], "o": ins["Wo1T"],
                                        "bq": ins["bq1"], "bk": ins["bk1"], "bv": ins["bv1"]}, ins["bo1"])]
        made = [(g.sb(f"A_all{k}", [C, layer[1], C]), g.sb(f"W_aug{k}", [P, layer[1], 2, C + 1]))
                for k, layer in enumerate(layers)]
        folded = "tok" in stages
        if folded:
            with ExitStack() as sub:
                m = Scope(nc, sub, "tk")
                Q_all = m.sb("Q_all", [P, NT, C])
                I_all = m.sb("I_all", [P, NT, 8], I32)
                F_all = m.sb("F_all", [P, NT, 8, 4])
                sampling_points(nc, "tk", ins, ident_bf, Q_all, I_all, F_all)
                deformable_attention(nc, "tk", ins, ident, Q_all, I_all, F_all, hid, fetched,
                                     lambda ctx: fold([0, 1], ctx))
        if "attn0" in stages:
            attn_layer(0)

        def moe_layer(tag, kinds, hid, router, norm_row, w):
            with ExitStack() as sub:
                m = Scope(nc, sub, tag)
                X_all = m.sb("X_all", [P, 2, B * S], BF16)
                G_all = m.sb("G_all", [P, B * S], BF16)
                with ExitStack() as inner:
                    xn = Scope(nc, inner, tag + "i").sb("xn", [P, NT, C])
                    normalise(nc, tag + "v", hid, xn, rms=kinds[0] == "rms", weight_row=norm_row)
                    gates(nc, tag, kinds[0], hid, xn, ident_bf, router, X_all, G_all)
                experts(nc, tag, kinds[1], hid, ident, w, X_all, G_all)

        if "moe0" in stages:
            moe_layer("m0", ("layer", "gelu"), hid, ins["router0"], None,
                      {"w1": ins["w1_0"], "w2": ins["w2_0"], "b1": ins["b1_0"], "b2": ins["b2_0"],
                       "spread": ins["spread0"]})
        if "attn1" in stages:
            attn_layer(1)

        xs = g.sb("xs", [P, NT, C])
        last = "moe1" in stages or "gqa" in stages
        if last:
            normalise(nc, "n1", hid, xs)
        if "gqa" in stages:
            with ExitStack() as sub:
                m = Scope(nc, sub, "q1")
                A_all = m.sb("A_all", [C, 4, C])
                W_aug = m.sb("W_aug", [P, 4, 2, C + 1])
                V_all = m.sb("V_all", [P, NT, C])
                Q_all = m.sb("Q_all", [C, B * S])
                K_all = m.sb("K_all", [P, 3, B * S], BF16)
                masks = m.sb("masks", [P, 2, P], BF16)
                masks_32 = m.sb("masks_32", [P, 2, P])
                w_loaded, w_ready = m.sem("w_loaded"), m.sem("w_ready")
                with nc.Block() as block:
                    @block.gpsimd
                    def _(pool):
                        nc.gpsimd.memset(W_aug[:], 0.0).then_inc(w_ready, 1)
                        nc.gpsimd.memset(masks_32[:], 0.0).then_inc(w_ready, 1)
                        pool.wait_ge(w_ready, 2)
                        for k, sign in enumerate((1, -1)):
                            nc.gpsimd.affine_select(out=masks_32[:, k], in_=masks_32[:, k], compare_op=ALU.is_ge,
                                                    fill=-1e30, base=0, pattern=[[-sign, P]],
                                                    channel_multiplier=sign).then_inc(w_ready, 1)
                        pool.wait_ge(w_ready, 4)
                        nc.gpsimd.tensor_copy(masks[:], masks_32[:]).then_inc(w_ready, 1)
                        pool.wait_ge(w_ready, 5)
                        nc.gpsimd.memset(W_aug[0:1, :, 0, C:C + 1], 1.0).then_inc(w_ready, 1)
                        pool.wait_ge(w_ready, 6)
                        nc.gpsimd.memset(W_aug[C:C + 1, :, 1, C:C + 1], 1.0).then_inc(w_ready, 1)
                        pool.wait_ge(w_ready, 7)

                    @block.sync
                    def _(sp):
                        sp.dma_start(A_all[:], ins["pick"]).then_inc(w_loaded, 16)
                        sp.wait_ge(w_ready, 7)
                        for h in range(4):
                            for e in range(2):
                                o = e * C + 1 + 16 * (h // 2)
                                sp.dma_start(W_aug[o:o + 16, h, e, 0:C], ins["woT"][h * 16:(h + 1) * 16]).then_inc(w_loaded, 16)
                        sp.wait_ge(w_loaded, 16 * 9)
                with ExitStack() as inner:
                    xn = Scope(nc, inner, "q1i").sb("xn", [P, NT, C])
                    normalise(nc, "q1v", xs, xn, rms=True, weight_row=ins["ln1"])
                    rotary_heads(nc, "q1", xn, ident, ident_bf, ins["wqkv"], ins["rope"], V_all, Q_all, K_all)
                attention(nc, "q1", 4, xs, ident_bf, A_all, W_aug, V_all, Q_all, K_all, (masks[:, 0], masks[:, 1]))
        if "moe1" in stages:
            moe_layer("m1", ("rms", "silu"), xs, ins["router1"], ins["ln2"],
                      {"w1": ins["w1_1"], "w3": ins["w3_1"], "w2": ins["w2_1"], "spread": ins["spread1"]})

        with nc.Block() as block:
            @block.sync
            def _(sp):
                if last:
                    sp.wait_ge(summed, 1)
                sp.dma_start(out.rearrange("(t p) c -> p t c", p=P), hid[:] if not last or "attn0" in stages else xs[:]).then_inc(stored, 16)
                sp.wait_ge(stored, 16)

            @block.vector
            def _(dve):
                if last:
                    nc.vector.tensor_tensor(hid[:], hid[:], xs[:], ALU.add).then_inc(summed, 1)


def host_layout(v, np):
    ins = {}
    if "x" in v:
        image = v["x"].transpose(0, 2, 3, 1)
        ins["pixels"] = np.stack([image[:, :-1], image[:, 1:]], 3).reshape(B * (WD - 1) * WD, 2 * C)
        line = np.linspace(-1.0, 1.0, GRID, dtype=np.float32)
        at = (line + np.float32(1)) * np.float32(0.5) * np.float32(WD - 1)
        lo = np.clip(np.floor(at), 0, WD - 2)
        fr = np.clip(at - lo, 0, 1).astype(np.float32)
        lo = lo.astype(np.int64)
        corner = [image[:, lo + dy][:, :, lo + dx] for dx in (0, 1) for dy in (0, 1)]
        ins["patches"] = np.stack(corner, 3).reshape(B * S, 4 * C)
        tokens = lambda a: a.reshape(T, P, a.shape[-1]).transpose(1, 0, 2)
        fx, fy = np.meshgrid(fr, fr)
        ins["f_ref"] = tokens(np.stack([(1 - fx) * (1 - fy), (1 - fx) * fy, fx * (1 - fy), fx * fy], -1))
        ins["ref"] = tokens(np.stack(np.meshgrid(line, line), -1))
        ins["w_qo"] = np.concatenate([v["L0_tok_W_q"].T, v["L0_tok_W_o1"]], 1)
        ins["w_kv"] = np.concatenate([v["L0_tok_W_k"].T, v["L0_tok_W_v"].T], 1)
        ins["w_o2"] = v["L0_tok_W_o2"]
        for n in ("b_o1", "ln_g", "ln_b", "b_o2"):
            ins[n] = v[f"L0_tok_{n}"].reshape(1, 16)
        ins["o_rows"] = (np.array([0, 0, 0, 1, 1, 2, 3, 3]).repeat(16)[:, None] == np.arange(3)).astype(np.float32)
    heads = lambda w: w.T.reshape(8, C, C).transpose(1, 0, 2)
    for n in "QKV":
        ins[f"W{n}T"] = heads(v[f"L0_attn_W{n}"])
    ins["Wout"] = v["L0_attn_Wout"].reshape(8, C, C).transpose(1, 0, 2)
    ins["bout"] = v["L0_attn_bout"].reshape(1, C)
    for n in "qkv":
        ins[f"W{n}1"] = v[f"L1_attn_W{n}"].reshape(C, 1, C)
        ins[f"b{n}1"] = v[f"L1_attn_b{n}"].reshape(C, 1)
    ins["Wo1T"] = v["L1_attn_Wo"].T.reshape(C, 1, C)
    ins["bo1"] = v["L1_attn_bo"].reshape(1, C)
    of_expert = lambda n: (np.arange(E)[:, None] == np.arange(E * n)[None, :] // n).astype(np.float32)
    ins["router0"] = v["L0_ffn_router_w"].T
    ins["w1_0"] = v["L0_ffn_w1"].transpose(1, 0, 2).reshape(C, E * C)
    ins["w2_0"] = v["L0_ffn_w2"].reshape(E * C, C)
    ins["b1_0"] = v["L0_ffn_b1"].reshape(E * C // P, P).T
    ins["b2_0"] = v["L0_ffn_b2"]
    ins["spread0"] = of_expert(C)
    pick = np.zeros((C, 4, C), np.float32)
    for h in range(4):
        for d in range(16):
            pick[16 * h + d, h, 1 + 32 * (h // 2) + d] = 0.25
    ins["pick"] = pick
    freq = 1.0 / 10000.0 ** (np.arange(0, 16, 2, dtype=np.float32) / 16)
    angle = np.outer(np.arange(S, dtype=np.float32), freq)
    rope = np.stack([np.cos(np.concatenate([angle, angle], -1)),
                     np.sin(np.concatenate([angle, angle], -1)) * np.repeat(np.float32([-1, 1]), 8)])
    ins["rope"] = rope.astype(np.float32).reshape(2, T, P, 16).transpose(2, 0, 1, 3)
    ins["wqkv"] = np.concatenate([v["L1_ffn_wq"], v["L1_ffn_wk"], v["L1_ffn_wv"]]).T
    ins["woT"] = v["L1_ffn_wo"].T
    ins["ln1"] = v["L1_ffn_ln1_w"].reshape(1, C)
    ins["router1"] = v["L1_ffn_router_w"].T
    ins["ln2"] = v["L1_ffn_ln2_w"].reshape(1, C)
    for n in ("w1", "w3"):
        ins[n + "_1"] = v["L1_ffn_" + n].transpose(2, 0, 1).reshape(C, E * HID1)
    ins["w2_1"] = v["L1_ffn_w2"].transpose(0, 2, 1).reshape(E * HID1, C)
    ins["spread1"] = of_expert(HID1)
    return ins


def kernel(**inputs):
    import numpy as np
    import concourse.bacc as bacc
    from concourse.bass_utils import run_bass_kernel_spmd

    v = {k: np.asarray(a) for k, a in inputs.items()}
    ins = host_layout(v, np)
    if "h" in v:
        ins["h"] = v["h"].reshape(B * S, C)
    nc = bacc.Bacc("TRN2", target_bir_lowering=False, num_devices=1)
    arrays, aps = {}, {}
    for name, a in ins.items():
        arrays[name] = np.ascontiguousarray(a)
        aps[name] = nc.dram_tensor(name, arrays[name].shape, mybir.dt.from_np(arrays[name].dtype),
                                   kind="ExternalInput").ap()
    out = nc.dram_tensor("out_tokens", (B * S, C), F32, kind="ExternalOutput").ap()
    build(nc, aps, out, STAGES)
    res = run_bass_kernel_spmd(nc, [arrays], core_ids=[0])
    return res.results[0]["out_tokens"].reshape(B, S, C)


STAGES = ("tok", "attn0", "moe0", "attn1", "gqa", "moe1")
```
